# Optimizing a Trainium2 kernel written in Bass

```python
import numpy as np
import jax
import jax.numpy as jnp

def _softmax(x, axis=-1):
    return jax.nn.softmax(x, axis=axis)

def _gelu(x):
    return jax.nn.gelu(x, approximate=True)

def _silu(x):
    return jax.nn.silu(x)

def _sigmoid(x):
    return jax.nn.sigmoid(x)

def _layernorm(x, axis=-1, eps=1e-05):
    m = jnp.mean(x, axis=axis, keepdims=True)
    v = jnp.var(x, axis=axis, keepdims=True)
    return (x - m) / jnp.sqrt(v + eps)

def _scatter_add(tgt, idx, src, axis=0):
    return tgt.at[idx].add(src)

def _segment_sum(src, seg, n):
    return jax.ops.segment_sum(src, seg, n)
kernel_name = 'mk_gps_d1_gnn_r8_e6e063'

def setup_inputs(seed: int=0):
    np.random.seed(seed)
    _w = jnp.asarray

    def _rec_inputs():
        import jax
        import jax.numpy as jnp
        _gk = jax.random.key(seed)
        x = -0.0003713 + 1 * jax.random.normal(jax.random.fold_in(_gk, 1), (6250, 256), jnp.float32)
        src = jax.random.randint(jax.random.fold_in(_gk, 2), (100000,), 0, 6250, jnp.int32)
        dst = jax.random.randint(jax.random.fold_in(_gk, 3), (100000,), 0, 6250, jnp.int32)
        _o = jnp.argsort(dst, stable=True)
        src = src[_o]
        dst = dst[_o]
        return (x, src, dst)
    x, src, dst = _rec_inputs()

    def _L0_gnn_setup():
        import jax, jax.numpy as jnp
        import numpy as np
        N = 6250
        E = 100000
        HID = 256
        L = 3
        HEADS = 8
        BASES = 4
        AGGS = 4
        EPS = 1e-05
        SLOPE = 0.01

        def _egconv(x, row, col, symw, deg, Wb, Wc, bc, bias):
            bases = x @ Wb
            comb = x @ Wc + bc
            msg = bases[row]
            agg_sum = jax.ops.segment_sum(msg, col, N)
            agg_mean = agg_sum / deg[:, None]
            agg_max = jax.ops.segment_max(msg, col, N)
            agg_sym = jax.ops.segment_sum(msg * symw[:, None], col, N)
            agg = jnp.stack([agg_mean, agg_max, agg_sum, agg_sym], axis=1)
            agg = agg.reshape(N, AGGS * BASES, HID // HEADS)
            w = comb.reshape(N, HEADS, BASES * AGGS)
            out = jnp.einsum('nhk,nkd->nhd', w, agg).reshape(N, HID)
            return out + bias

        def _bn_lrelu(h, gamma, beta):
            mu = h.mean(0)
            var = h.var(0)
            y = gamma * (h - mu) * jax.lax.rsqrt(var + EPS) + beta
            return jnp.where(y >= 0, y, SLOPE * y)
        key = jax.random.key(seed)
        ks = jax.random.split(key, 8)
        x = jax.random.normal(ks[0], (N, HID), jnp.float32)
        edge_index = jax.random.randint(ks[1], (2, E), 0, N, jnp.int32)
        s = 1.0 / np.sqrt(HID)
        Wb = jax.random.normal(ks[2], (L, HID, HID // HEADS * BASES), jnp.float32) * s
        Wc = jax.random.normal(ks[3], (L, HID, HEADS * BASES * AGGS), jnp.float32) * s
        bc = jax.random.normal(ks[4], (L, HEADS * BASES * AGGS), jnp.float32) * 0.01
        conv_bias = jax.random.normal(ks[5], (L, HID), jnp.float32) * 0.01
        bn_gamma = jnp.ones((L, HID), jnp.float32)
        bn_beta = jnp.zeros((L, HID), jnp.float32)
        fc_W = jax.random.normal(ks[6], (HID * (L + 1), HID), jnp.float32) / np.sqrt(HID * (L + 1))
        fc_b = jnp.zeros((HID,), jnp.float32)
        return dict(x=x, edge_index=edge_index, Wb=Wb, Wc=Wc, bc=bc, conv_bias=conv_bias, bn_gamma=bn_gamma, bn_beta=bn_beta, fc_W=fc_W, fc_b=fc_b)
    _L0_gnn_all = _L0_gnn_setup()
    _L0_gnn_in = {k: v for k, v in _L0_gnn_all.items() if k in ('Wb', 'Wc', 'bc', 'conv_bias', 'bn_gamma', 'bn_beta', 'fc_W', 'fc_b')}
    del _L0_gnn_all

    def _L0_mix_setup():
        import jax, jax.numpy as jnp
        import numpy as np
        MIDC = 256
        HEADS = 8
        HEADC = MIDC // HEADS
        EPS = 1e-05

        def _ln(x, gamma, beta):
            mu = jnp.mean(x, axis=-1, keepdims=True)
            var = jnp.var(x, axis=-1, keepdims=True)
            return (x - mu) * jax.lax.rsqrt(var + EPS) * gamma + beta
        key = jax.random.key(seed)
        ks = jax.random.split(key, 8)
        B, HW, C = (8, 512, MIDC)
        s = 1.0 / np.sqrt(C)
        return {'x': jax.random.normal(ks[0], (B, HW, C), jnp.float32), 'w_qkv': jax.random.normal(ks[1], (C, 3 * C), jnp.float32) * s, 'b_qkv': jnp.zeros((3 * C,), jnp.float32), 'kln_g': jnp.ones((HEADC,), jnp.float32), 'kln_b': jnp.zeros((HEADC,), jnp.float32), 'vln_g': jnp.ones((HEADC,), jnp.float32), 'vln_b': jnp.zeros((HEADC,), jnp.float32), 'w1': jax.random.normal(ks[2], (C, C), jnp.float32) * s, 'b1': jnp.zeros((C,), jnp.float32), 'w2': jax.random.normal(ks[3], (C, C), jnp.float32) * s, 'b2': jnp.zeros((C,), jnp.float32)}
    _L0_mix_all = _L0_mix_setup()
    _L0_mix_in = {k: v for k, v in _L0_mix_all.items() if k in ('w_qkv', 'b_qkv', 'kln_g', 'kln_b', 'vln_g', 'vln_b', 'w1', 'b1', 'w2', 'b2')}
    del _L0_mix_all

    def _L0_ffn_setup():
        import jax, jax.numpy as jnp
        import numpy as np
        TOP_K = 2
        LN_EPS = 1e-05
        key = jax.random.key(seed)
        ks = jax.random.split(key, 8)
        B, S, D, E, H = (16, 1024, 256, 8, 1024)
        x = jax.random.normal(ks[0], (B, S, D), dtype=jnp.float32)
        Wr = jax.random.normal(ks[1], (D, E), dtype=jnp.float32) * 0.1
        br = jnp.zeros((E,), dtype=jnp.float32)
        ln_g = jnp.ones((E, D), dtype=jnp.float32)
        ln_b = jnp.zeros((E, D), dtype=jnp.float32)
        W1 = jax.random.normal(ks[2], (E, D, H), dtype=jnp.float32) * (1.0 / np.sqrt(D))
        b1 = jnp.zeros((E, H), dtype=jnp.float32)
        W2 = jax.random.normal(ks[3], (E, H, D), dtype=jnp.float32) * (1.0 / np.sqrt(H))
        b2 = jnp.zeros((E, D), dtype=jnp.float32)
        return {'x': x, 'Wr': Wr, 'br': br, 'ln_g': ln_g, 'ln_b': ln_b, 'W1': W1, 'b1': b1, 'W2': W2, 'b2': b2}
    _L0_ffn_all = _L0_ffn_setup()
    _L0_ffn_in = {k: v for k, v in _L0_ffn_all.items() if k in ('Wr', 'br', 'ln_g', 'ln_b', 'W1', 'b1', 'W2', 'b2')}
    del _L0_ffn_all
    return {'x': x, 'src': src, 'dst': dst, 'L0_gnn_Wb': _L0_gnn_in['Wb'], 'L0_gnn_Wc': _L0_gnn_in['Wc'], 'L0_gnn_bc': _L0_gnn_in['bc'], 'L0_gnn_conv_bias': _L0_gnn_in['conv_bias'], 'L0_gnn_bn_gamma': _L0_gnn_in['bn_gamma'], 'L0_gnn_bn_beta': _L0_gnn_in['bn_beta'], 'L0_gnn_fc_W': _L0_gnn_in['fc_W'], 'L0_gnn_fc_b': _L0_gnn_in['fc_b'], 'L0_mix_w_qkv': _L0_mix_in['w_qkv'], 'L0_mix_b_qkv': _L0_mix_in['b_qkv'], 'L0_mix_kln_g': _L0_mix_in['kln_g'], 'L0_mix_kln_b': _L0_mix_in['kln_b'], 'L0_mix_vln_g': _L0_mix_in['vln_g'], 'L0_mix_vln_b': _L0_mix_in['vln_b'], 'L0_mix_w1': _L0_mix_in['w1'], 'L0_mix_b1': _L0_mix_in['b1'], 'L0_mix_w2': _L0_mix_in['w2'], 'L0_mix_b2': _L0_mix_in['b2'], 'L0_ffn_Wr': _L0_ffn_in['Wr'], 'L0_ffn_br': _L0_ffn_in['br'], 'L0_ffn_ln_g': _L0_ffn_in['ln_g'], 'L0_ffn_ln_b': _L0_ffn_in['ln_b'], 'L0_ffn_W1': _L0_ffn_in['W1'], 'L0_ffn_b1': _L0_ffn_in['b1'], 'L0_ffn_W2': _L0_ffn_in['W2'], 'L0_ffn_b2': _L0_ffn_in['b2']}

def reference(x, src, dst, L0_gnn_Wb, L0_gnn_Wc, L0_gnn_bc, L0_gnn_conv_bias, L0_gnn_bn_gamma, L0_gnn_bn_beta, L0_gnn_fc_W, L0_gnn_fc_b, L0_mix_w_qkv, L0_mix_b_qkv, L0_mix_kln_g, L0_mix_kln_b, L0_mix_vln_g, L0_mix_vln_b, L0_mix_w1, L0_mix_b1, L0_mix_w2, L0_mix_b2, L0_ffn_Wr, L0_ffn_br, L0_ffn_ln_g, L0_ffn_ln_b, L0_ffn_W1, L0_ffn_b1, L0_ffn_W2, L0_ffn_b2):
    import jax
    import jax.numpy as jnp

    def _L0_gnn_ref(x, edge_index, Wb, Wc, bc, conv_bias, bn_gamma, bn_beta, fc_W, fc_b):
        import jax, jax.numpy as jnp
        import numpy as np
        N = 6250
        E = 100000
        HID = 256
        L = 3
        HEADS = 8
        BASES = 4
        AGGS = 4
        EPS = 1e-05
        SLOPE = 0.01

        def _egconv(x, row, col, symw, deg, Wb, Wc, bc, bias):
            bases = x @ Wb
            comb = x @ Wc + bc
            msg = bases[row]
            agg_sum = jax.ops.segment_sum(msg, col, N)
            agg_mean = agg_sum / deg[:, None]
            agg_max = jax.ops.segment_max(msg, col, N)
            agg_sym = jax.ops.segment_sum(msg * symw[:, None], col, N)
            agg = jnp.stack([agg_mean, agg_max, agg_sum, agg_sym], axis=1)
            agg = agg.reshape(N, AGGS * BASES, HID // HEADS)
            w = comb.reshape(N, HEADS, BASES * AGGS)
            out = jnp.einsum('nhk,nkd->nhd', w, agg).reshape(N, HID)
            return out + bias

        def _bn_lrelu(h, gamma, beta):
            mu = h.mean(0)
            var = h.var(0)
            y = gamma * (h - mu) * jax.lax.rsqrt(var + EPS) + beta
            return jnp.where(y >= 0, y, SLOPE * y)
        loop = jnp.arange(N, dtype=edge_index.dtype)
        row = jnp.concatenate([edge_index[0], loop])
        col = jnp.concatenate([edge_index[1], loop])
        deg = jax.ops.segment_sum(jnp.ones_like(col, jnp.float32), col, N)
        dinv = jax.lax.rsqrt(deg)
        symw = dinv[row] * dinv[col]
        feats = [x]
        for l in range(L):
            h = _egconv(x, row, col, symw, deg, Wb[l], Wc[l], bc[l], conv_bias[l])
            feats.append(_bn_lrelu(h, bn_gamma[l], bn_beta[l]))
        return jnp.concatenate(feats, axis=-1) @ fc_W + fc_b

    def _L0_mix_ref(x, w_qkv, b_qkv, kln_g, kln_b, vln_g, vln_b, w1, b1, w2, b2):
        import jax, jax.numpy as jnp
        import numpy as np
        MIDC = 256
        HEADS = 8
        HEADC = MIDC // HEADS
        EPS = 1e-05

        def _ln(x, gamma, beta):
            mu = jnp.mean(x, axis=-1, keepdims=True)
            var = jnp.var(x, axis=-1, keepdims=True)
            return (x - mu) * jax.lax.rsqrt(var + EPS) * gamma + beta
        B, HW, C = x.shape
        bias = x
        qkv = (x @ w_qkv + b_qkv).reshape(B, HW, HEADS, 3 * HEADC)
        qkv = qkv.transpose(0, 2, 1, 3)
        q, k, v = jnp.split(qkv, 3, axis=-1)
        k = _ln(k, kln_g, kln_b)
        v = _ln(v, vln_g, vln_b)
        kv = jnp.einsum('bhnd,bhne->bhde', k, v) / HW
        out = jnp.einsum('bhnd,bhde->bhne', q, kv)
        out = out.transpose(0, 2, 1, 3).reshape(B, HW, C)
        ret = out + bias
        h = jax.nn.gelu(ret @ w1 + b1, approximate=False)
        return h @ w2 + b2 + bias

    def _L0_ffn_ref(x, Wr, br, ln_g, ln_b, W1, b1, W2, b2):
        import jax, jax.numpy as jnp
        import numpy as np
        TOP_K = 2
        LN_EPS = 1e-05
        B, S, D = x.shape
        N = B * S
        xt = x.reshape(N, D)
        logits = xt @ Wr + br
        probs = jax.nn.softmax(logits, axis=-1)
        top_p, top_idx = jax.lax.top_k(probs, TOP_K)
        weights = top_p / top_p.sum(axis=-1, keepdims=True)
        mu = xt.mean(axis=-1, keepdims=True)
        var = ((xt - mu) ** 2).mean(axis=-1, keepdims=True)
        xn = (xt - mu) * jax.lax.rsqrt(var + LN_EPS)
        xe = xn[None, :, :] * ln_g[:, None, :] + ln_b[:, None, :]
        h = jax.nn.gelu(jnp.einsum('end,edh->enh', xe, W1) + b1[:, None, :], approximate=False)
        y = jnp.einsum('enh,ehd->end', h, W2) + b2[:, None, :]
        y_tok = jnp.transpose(y, (1, 0, 2))
        sel = jnp.take_along_axis(y_tok, top_idx[:, :, None], axis=1)
        out = (weights[:, :, None] * sel).sum(axis=1)
        return out.reshape(B, S, D)
    edge_index = jnp.stack([src, dst])
    xn = _layernorm(x, axis=-1)
    x = x + _L0_gnn_ref(xn, edge_index, L0_gnn_Wb, L0_gnn_Wc, L0_gnn_bc, L0_gnn_conv_bias, L0_gnn_bn_gamma, L0_gnn_bn_beta, L0_gnn_fc_W, L0_gnn_fc_b) + _L0_mix_ref(xn[None], L0_mix_w_qkv, L0_mix_b_qkv, L0_mix_kln_g, L0_mix_kln_b, L0_mix_vln_g, L0_mix_vln_b, L0_mix_w1, L0_mix_b1, L0_mix_w2, L0_mix_b2)[0]
    x = x + _L0_ffn_ref(_layernorm(x, axis=-1)[None], L0_ffn_Wr, L0_ffn_br, L0_ffn_ln_g, L0_ffn_ln_b, L0_ffn_W1, L0_ffn_b1, L0_ffn_W2, L0_ffn_b2)[0]
    return x

_drawn_inputs = setup_inputs


def setup_inputs(seed=0):
    import zlib

    import numpy as np

    out = dict(_drawn_inputs(seed))
    spreads = {'L0_gnn_bn_gamma': (1.0, 0.2),
     'L0_gnn_bn_beta': (0.0, 0.1),
     'L0_gnn_fc_b': (0.0, 0.1),
     'L0_mix_b_qkv': (0.0, 0.1),
     'L0_mix_kln_g': (1.0, 0.2),
     'L0_mix_kln_b': (0.0, 0.296),
     'L0_mix_vln_g': (1.0, 0.2),
     'L0_mix_vln_b': (0.0, 0.28),
     'L0_mix_b1': (0.0, 0.1),
     'L0_mix_b2': (0.0, 0.1),
     'L0_ffn_br': (0.0, 0.1),
     'L0_ffn_ln_g': (1.0, 0.2),
     'L0_ffn_ln_b': (0.0, 0.355),
     'L0_ffn_b1': (0.0, 0.343),
     'L0_ffn_b2': (0.0, 0.1)}
    factors = {'L0_gnn_bc': 7.321, 'L0_gnn_conv_bias': 8.0}
    for name, (base, spread) in spreads.items():
        noise = np.random.default_rng([zlib.crc32(name.encode()), seed]).standard_normal(out[name].shape)
        drawn = base * np.exp(spread * noise) if base else spread * noise
        out[name] = jnp.asarray(drawn.astype(out[name].dtype))
    for name, factor in factors.items():
        out[name] = (out[name] * factor).astype(out[name].dtype)
    return out
```

```python
import concourse.bass as bass
from concourse import mybir
from contextlib import ExitStack, contextmanager

FP32 = mybir.dt.float32
BF16 = mybir.dt.bfloat16
I32 = mybir.dt.int32
ALU = mybir.AluOpType
ACT = mybir.ActivationFunctionType
AX = mybir.AxisListType.X

N = 6250
E = 100000
C = 256
CH = C // 128
P = 125
NT = N // P
L = 3
HEADS = 8
BASES = 4
HC = C // HEADS
BW = BASES * HC
TW = L * BW
EPS = 1e-5
SLOPE = 0.01

NG = 64
GROUPS = 98
NPAD = NG * GROUPS
HIST_A = NPAD // 128
SLOTS = 48
CHUNKS = SLOTS // 2
UNROLL = 4
RUN_ROWS = 128 * 784
BIG = 3.0e38

EXPERTS = 8
HID = 1024
BLOCKS = -(-2 * N // 128) + EXPERTS
ROWS = BLOCKS * 128


class Chain:

    def __init__(self, eng, sem):
        self.eng, self.sem, self.base, self.n = eng, sem, 0, 0

    def link(self, ins):
        self.mark(ins)
        self.wait()

    def mark(self, ins):
        ins.then_inc(self.sem, 1)
        self.n += 1

    def wait(self):
        self.eng.wait_ge(self.sem, self.base + self.n)

    @contextmanager
    def loop(self, i, first, per):
        n0 = self.n
        self.base = (i - first) * per
        yield
        assert self.n - n0 == per, (self.n - n0, per)
        self.n = n0
        self.base = 0

    def looped(self, steps, per):
        self.n += steps * per


def loop2(eng, chain, pairs, per, body):
    n0 = chain.n if chain else 0
    body(0, True)
    if chain:
        assert chain.n - n0 == per, ("links of a step", chain.n - n0, per)
    with eng.Fori(1, pairs) as i:
        if chain:
            with chain.loop(i, 1, per):
                body(i, False)
        else:
            body(i, False)
    if chain:
        chain.looped(pairs - 1, per)


def halves_to_mean_var(nc, ch, st, mv, half):
    dve = nc.vector
    ch.link(dve.tensor_tensor(half[:, :], st[:, :, 1], st[:, :, 4], ALU.subtract))
    ch.link(dve.tensor_scalar(half[:, :], half[:, :], 0.5, None, ALU.mult))
    ch.link(dve.tensor_tensor(mv[:, :, 0], st[:, :, 4], half[:, :], ALU.add))
    ch.link(dve.tensor_tensor(half[:, :], half[:, :], half[:, :], ALU.mult))
    ch.link(dve.tensor_tensor(mv[:, :, 1], st[:, :, 2], st[:, :, 5], ALU.add))
    ch.link(dve.scalar_tensor_tensor(mv[:, :, 1], mv[:, :, 1], 1.0 / C, half[:, :], ALU.mult, ALU.add))


def build(nc, a, out):
    def dram(name, shape, dt=FP32):
        return nc.dram_tensor(name, shape, dt, kind="Internal").ap()

    d = dict(
        cnt=dram("cnt_d", [NPAD]), rp=dram("rp_d", [NPAD]), dinv=dram("dinv_d", [NPAD]),
        srcp=dram("srcp_d", [RUN_ROWS + 64], I32), runs=dram("runs_d", [RUN_ROWS, SLOTS], I32),
        tab=dram("tab_d", [NPAD, TW + 1]), xnt=dram("xnt_d", [NT, 128, CH * P]),
        agg=dram("agg_d", [NPAD + 2 * NG, 4, TW]), ht=dram("ht_d", [NT, 128, 2 * L * P]),
        xg=dram("xg_d", [ROWS + 128, C]), yg=dram("yg_d", [ROWS, C]), x2=dram("x2_d", [N, C]),
    )

    top = ExitStack()

    @contextmanager
    def phase(tag, clear=False):
        with ExitStack() as c:
            sems = []

            def sb(name, shape, dt=FP32):
                return c.enter_context(nc.sbuf_tensor(f"{tag}_{name}", shape, dt))

            def ps(name, shape=(128, 512), dt=FP32):
                return c.enter_context(nc.psum_tensor(f"{tag}_{name}", list(shape), dt))

            def sm(name, swdge=False):
                if swdge:
                    return top.enter_context(nc.semaphore(f"{tag}_{name}"))
                sems.append(c.enter_context(nc.semaphore(f"{tag}_{name}")))
                return sems[-1]

            with ExitStack() as work:
                yield work, sb, ps, sm
            if clear:
                with nc.Block() as block:
                    @block.sync
                    def _(sp):
                        for s in sems:
                            sp.sem_clear(s)

    with top:
        def keep(stack, name, shape, dt=FP32):
            return stack.enter_context(nc.sbuf_tensor(name, shape, dt))

        ident = keep(top, "ident", [128, 128])
        pos = keep(top, "pos", [P, 2, NT], I32)
        gate = keep(top, "gate", [P, 2, NT])
        blk = keep(top, "blk", [1, BLOCKS], I32)
        with ExitStack() as nodes:
            x_sb = keep(nodes, "x_sb", [P, NT, C])
            mv = keep(nodes, "mv", [P, NT, 2])
            rstd = keep(nodes, "rstd", [P, NT])
            kvbd = keep(nodes, "kvbd", [128, CH, 128])
            phase_histogram(nc, phase, a, d, ident)
            phase_nodes(nc, phase, a, d, ident, x_sb, mv, rstd, kvbd)
            phase_edges(nc, phase, a, d, ident)
            with ExitStack() as mid:
                stats = keep(mid, "bn_stats", [128, 2 * L, NT, 6])
                phase_conv(nc, phase, a, d, ident, stats)
                phase_mix(nc, phase, a, d, ident, x_sb, mv, rstd, kvbd, stats)
            phase_route(nc, phase, a, d, ident, x_sb, pos, gate, blk)
        phase_experts(nc, phase, a, d, ident, blk)
        phase_combine(nc, phase, d, out, pos, gate)


def phase_histogram(nc, phase, a, d, ident):
    COLS = E // P
    W = 16
    PAIRS = COLS // W // 2
    with phase("h", clear=True) as (c, sb, ps, sm):
        dst = sb("dst", [P, COLS], I32)
        hi_i = sb("hi_i", [P, COLS], I32)
        lo_i = sb("lo_i", [P, COLS], I32)
        hi = sb("hi", [P, COLS], BF16)
        lo = sb("lo", [P, COLS], BF16)
        iota_i = sb("iota_i", [P, 128], I32)
        iota = sb("iota", [P, 128], BF16)
        one_hi = sb("one_hi", [P, 2, W, HIST_A], BF16)
        one_lo = sb("one_lo", [P, 2, W, 128], BF16)
        zero_b = sb("zero_b", [P, 128], BF16)
        zero_i = sb("zero_i", [1, 512], I32)
        zero_f = sb("zero_f", [NPAD - N, TW + 1])
        big = sb("big", [128, 2, TW])
        ones = sb("ones", [HIST_A, 128])
        below = sb("below", [HIST_A, HIST_A])
        cnt = sb("cnt", [HIST_A, 128])
        incl = sb("incl", [HIST_A, 128])
        deg = sb("deg", [HIST_A, 128])
        first = sb("first", [HIST_A, 128])
        p_cnt = ps("p_cnt")
        p_off = ps("p_off")
        s_dst, s_fill, s_pad, s_run, s_gp, s_dve = (sm(n) for n in
            ("dst", "fill", "pad", "run", "gp", "dve"))
        s_init = sm("init", swdge=True)
        s_one, s_used, s_cnt, s_tot, s_off, s_res, s_store, s_sqrt = (sm(n) for n in
            ("one", "used", "cnt", "tot", "off", "res", "store", "sqrt"))
        block = c.enter_context(nc.Block())

        @block.sync
        def _(sp):
            sp.dma_start(dst[:, :], a["dst"].rearrange("(p k) -> p k", p=P)).then_inc(s_dst, 16)
            sp.dma_start(d["srcp"][1:E + 1].rearrange("(p k) -> p k", p=P),
                         a["src"].rearrange("(p k) -> p k", p=P)).then_inc(s_pad, 16)
            sp.wait_ge(s_fill, 1)
            sp.dma_start(d["srcp"][0:1].rearrange("(o k) -> o k", o=1), zero_i[0:1, 0:1]).then_inc(s_pad, 16)
            tail = RUN_ROWS + 64 - E - 1
            sp.dma_start(d["srcp"][E + 1:].rearrange("(o k) -> o k", o=1), zero_i[0:1, 0:tail]).then_inc(s_pad, 16)
            sp.wait_ge(s_pad, 48)
            runs_in = bass.AP(d["srcp"].tensor, 0, [[RUN_ROWS // 128, 128], [1, RUN_ROWS // 128], [1, SLOTS]])
            sp.dma_start(d["runs"].rearrange("(p r) s -> p r s", p=128), runs_in).then_inc(s_run, 16)
            sp.wait_ge(s_res, 3)
            for name, t in (("cnt", cnt), ("rp", first), ("dinv", deg)):
                sp.dma_start(d[name].rearrange("(a b) -> a b", b=128), t[:, :]).then_inc(s_store, 16)
            sp.wait_ge(s_store, 48)
            sp.wait_ge(s_run, 16)

        @block.gpsimd
        def _(pool):
            nc.gpsimd.memset(zero_i[:, :], 0).then_inc(s_fill, 1)
            nc.gpsimd.iota(iota_i[:, :], pattern=[[1, 128]], base=0, channel_multiplier=0).then_inc(s_gp, 1)
            nc.gpsimd.memset(ident[:, :], 0.0).then_inc(s_gp, 1)
            nc.gpsimd.memset(below[:, :], 1.0).then_inc(s_gp, 1)
            pool.wait_ge(s_gp, 3)
            nc.gpsimd.affine_select(out=ident[:, :], in_=ident[:, :], compare_op=ALU.not_equal, fill=1.0,
                                    base=0, pattern=[[-1, 128]], channel_multiplier=1).then_inc(s_gp, 1)
            nc.gpsimd.affine_select(out=below[:, :], in_=below[:, :], compare_op=ALU.is_gt, fill=0.0,
                                    base=0, pattern=[[1, HIST_A]], channel_multiplier=-1).then_inc(s_gp, 1)
            nc.gpsimd.memset(zero_f[:, :], 0.0).then_inc(s_gp, 1)
            nc.gpsimd.memset(big[:, 0, :], 0.0).then_inc(s_gp, 1)
            nc.gpsimd.memset(big[:, 1, :], -BIG).then_inc(s_gp, 1)
            pool.wait_ge(s_gp, 8)
            pool.dma_start(d["tab"][N:NPAD, :], zero_f[:, :]).then_inc(s_init, 16)
            for g in range((NPAD + 2 * NG) // 128):
                for half in range(2):
                    for k in range(2):
                        pool.dma_start(d["agg"][g * 128:(g + 1) * 128, 2 * half + k, :],
                                       big[:, half, :]).then_inc(s_init, 16)
            pool.wait_ge(s_init, 16 * (1 + 4 * ((NPAD + 2 * NG) // 128)))

        @block.vector
        def _(dve):
            ch = Chain(dve, s_dve)
            nc.vector.memset(ones[:, :], 1.0)
            nc.vector.memset(zero_b[:, :], 0.0)
            dve.wait_ge(s_gp, 1)
            nc.vector.tensor_copy(iota[:, :], iota_i[:, :])
            dve.wait_ge(s_dst, 16)
            nc.vector.tensor_single_scalar(hi_i[:, :], dst[:, :], 7, op=ALU.logical_shift_right)
            ch.link(nc.vector.tensor_single_scalar(lo_i[:, :], dst[:, :], 127, op=ALU.bitwise_and))
            nc.vector.tensor_copy(hi[:, :], hi_i[:, :])
            ch.link(nc.vector.tensor_copy(lo[:, :], lo_i[:, :]))

            def step(i, first_step):
                for b in range(2):
                    t = 2 * i + b
                    if not first_step:
                        dve.wait_ge(s_used, t - 1)
                    cols = bass.ds(t * W, W)
                    nc.vector.tensor_tensor(
                        one_hi[:, b], hi[:, cols].unsqueeze(2).to_broadcast([P, W, HIST_A]),
                        iota[:, 0:HIST_A].unsqueeze(1).to_broadcast([P, W, HIST_A]), ALU.is_equal)
                    nc.vector.tensor_tensor(
                        one_lo[:, b], lo[:, cols].unsqueeze(2).to_broadcast([P, W, 128]),
                        iota[:, :].unsqueeze(1).to_broadcast([P, W, 128]), ALU.is_equal).then_inc(s_one, 1)
            loop2(dve, None, PAIRS, 0, step)
            dve.wait_ge(s_cnt, 1)
            ch.link(nc.vector.tensor_copy(cnt[:, :], p_cnt[0:HIST_A, 0:128]))
            nc.vector.tensor_tensor_scan(incl[:, :], ones[:, :], cnt[:, :], 0.0, ALU.mult, ALU.add).then_inc(s_tot, 1)
            ch.link(nc.vector.tensor_scalar_add(deg[:, :], cnt[:, :], 1.0))
            nc.vector.reciprocal(deg[:, :], deg[:, :]).then_inc(s_sqrt, 1)
            dve.wait_ge(s_tot, 1)
            ch.link(nc.vector.tensor_tensor(first[:, :], incl[:, :], cnt[:, :], ALU.subtract))
            dve.wait_ge(s_off, 1)
            nc.vector.tensor_scalar(first[:, :], first[:, :], p_off[0:HIST_A, 0:1], None, ALU.add).then_inc(s_res, 1)

        @block.scalar
        def _(act):
            act.wait_ge(s_sqrt, 1)
            nc.scalar.activation(deg[:, :], deg[:, :], ACT.Sqrt).then_inc(s_res, 2)

        @block.tensor
        def _(pe):
            def step(i, first_step):
                for b in range(2):
                    t = 2 * i + b
                    pe.wait_ge(s_one, t + 1)
                    for w in range(W):
                        last = nc.tensor.matmul(p_cnt[0:HIST_A, 0:128], one_hi[:, b, w, :], one_lo[:, b, w, :],
                                                start=first_step and b == 0 and w == 0, stop=False)
                    last.then_inc(s_used, 1)
            loop2(pe, None, PAIRS, 0, step)
            nc.tensor.matmul(p_cnt[0:HIST_A, 0:128], zero_b[:, 0:HIST_A], zero_b[:, :], start=False,
                             stop=True).then_inc(s_cnt, 1)
            pe.wait_ge(s_tot, 1)
            pe.wait_ge(s_gp, 5)
            nc.tensor.matmul(p_off[0:HIST_A, 0:1], below[:, :], incl[:, 127:128], start=True,
                             stop=True).then_inc(s_off, 1)


def phase_nodes(nc, phase, a, d, ident, x_sb, mv, rstd, kvbd):
    KV = 2 * C
    G = 2 * HEADS
    with phase("n", clear=True) as (c, sb, ps, sm):
        wb = sb("wb", [128, CH, L, BW])
        wqkv = sb("wqkv", [128, CH, 3 * C])
        b_kv = sb("b_kv", [P, 3 * C])
        ln_g = sb("ln_g", [P, 2, HC])
        ln_b = sb("ln_b", [P, 2, HC])
        dinv = sb("dinv", [P, NT])
        st = sb("st", [P, NT, 6])
        std = sb("std", [P, NT])
        half = sb("half", [P, NT])
        xn = sb("xn", [P, 2, C])
        xt = sb("xt", [128, 2, CH * P])
        rows = sb("rows", [P, 2, TW + 1])
        kv = sb("kv", [P, 2, KV])
        sq = sb("sq", [P, 2, KV])
        gs = sb("gs", [P, 2, G])
        gv = sb("gv", [P, 2, G])
        gd = sb("gd", [P, 2, G])
        kvg = sb("kvg", [P, 2, KV])
        kn = sb("kn", [P, 2, 2, C])
        zero = sb("zero", [P, C])
        p_t = [ps(f"p_t{b}") for b in range(2)]
        p_b = [ps(f"p_b{b}") for b in range(2)]
        p_k = [ps(f"p_k{b}") for b in range(2)]
        p_kv = ps("p_kv")
        s_x, s_w, s_bias, s_dve, s_act, s_pool = (sm(n) for n in ("x", "w", "bias", "dve", "act", "pool"))
        s_var, s_std, s_xn, s_tp, s_xt, s_bp, s_kp, s_row = (sm(n) for n in
            ("var", "std", "xn", "tp", "xt", "bp", "kp", "row"))
        s_sq, s_cen, s_gd, s_gstd, s_nrm, s_kn, s_kva, s_zero, s_din, s_end, s_kvd = (sm(n) for n in
            ("sq", "cen", "gd", "gstd", "nrm", "kn", "kva", "zero", "din", "end", "kvd"))
        s_tabw = [sm(f"tabw{b}") for b in range(2)]
        s_xtw = [sm(f"xtw{b}") for b in range(2)]
        block = c.enter_context(nc.Block())
        tab = d["tab"][0:N, :].rearrange("(p t) w -> p t w", t=NT)

        @block.sync
        def _(sp):
            sp.dma_start(x_sb[:, :, :], a["x"].rearrange("(p t) c -> p t c", t=NT)).then_inc(s_x, 16)
            for k in range(CH):
                sp.dma_start(wb[:, k], a["L0_gnn_Wb"][:, k * 128:(k + 1) * 128, :].rearrange("l p w -> p l w")).then_inc(s_w, 16)
                sp.dma_start(wqkv[:, k], a["L0_mix_w_qkv"][k * 128:(k + 1) * 128, :]).then_inc(s_w, 16)
            sp.dma_start(b_kv[:, :], a["L0_mix_b_qkv"].rearrange("(o n) -> o n", o=1).to_broadcast([P, 3 * C])).then_inc(s_bias, 16)
            for j, n in enumerate("kv"):
                sp.dma_start(ln_g[:, j, :], a[f"L0_mix_{n}ln_g"].rearrange("(o n) -> o n", o=1).to_broadcast([P, HC])).then_inc(s_bias, 16)
                sp.dma_start(ln_b[:, j, :], a[f"L0_mix_{n}ln_b"].rearrange("(o n) -> o n", o=1).to_broadcast([P, HC])).then_inc(s_bias, 16)
            sp.dma_start(dinv[:, :], d["dinv"][0:N].rearrange("(p t) -> p t", t=NT)).then_inc(s_din, 16)

            def step(i, first_step):
                for b in range(2):
                    t = 2 * i + b
                    sp.wait_ge(s_xt, t + 1)
                    sp.dma_start(d["xnt"][bass.ds(t, 1)].rearrange("o p c -> (o p) c"), xt[:, b]).then_inc(s_xtw[b], 16)
                    sp.wait_ge(s_row, t + 1)
                    sp.dma_start(tab[:, bass.ds(t, 1), :].rearrange("p o w -> p (o w)"), rows[:, b]).then_inc(s_tabw[b], 16)
            loop2(sp, None, NT // 2, 0, step)
            for b in range(2):
                sp.wait_ge(s_xtw[b], 16 * (NT // 2))
                sp.wait_ge(s_tabw[b], 16 * (NT // 2))

        @block.vector
        def _(dve):
            ch = Chain(dve, s_dve)
            nc.vector.memset(zero[:, :], 0.0)
            nc.vector.memset(kn[:, :, :, :], 0.0).then_inc(s_zero, 1)
            dve.wait_ge(s_x, 16)
            with dve.Fori(0, NT) as t:
                nc.vector.bn_stats(st[:, bass.ds(t, 1), :].rearrange("p o s -> p (o s)"),
                                   x_sb[:, bass.ds(t, 1), :].rearrange("p o c -> p (o c)"))
            dve.drain()
            halves_to_mean_var(nc, ch, st, mv, half)
            nc.vector.tensor_scalar_add(std[:, :], mv[:, :, 1], EPS).then_inc(s_var, 1)
            dve.wait_ge(s_std, 1)
            ch.link(nc.vector.reciprocal(rstd[:, :], std[:, :]))
            dve.wait_ge(s_bias, 80)
            dve.wait_ge(s_din, 16)

            def grouped(t3):
                return t3.rearrange("p (g c) -> p g c", c=HC)

            def spread(t2):
                return t2.unsqueeze(2).to_broadcast([P, G, HC])

            def step(i, first_step):
                for b in range(2):
                    t = 2 * i + b
                    if not first_step:
                        dve.wait_ge(s_tp, t - 1)
                    nc.vector.tensor_scalar(xn[:, b, :], x_sb[:, bass.ds(t, 1), :].rearrange("p o c -> p (o c)"),
                                            mv[:, bass.ds(t, 1), 0], rstd[:, bass.ds(t, 1)], ALU.subtract,
                                            ALU.mult).then_inc(s_xn, 1)
                    dve.wait_ge(s_kp, t + 1)
                    if not first_step:
                        dve.wait_ge(s_kn, t)
                    bias = b_kv[:, :].rearrange("p (h s) -> p h s", s=3 * HC)[:, :, HC:]
                    ch.link(nc.vector.tensor_tensor(kv[:, b, :].rearrange("p (h s) -> p h s", s=2 * HC),
                                                    p_k[b][0:P, :].rearrange("p (h s) -> p h s", s=2 * HC), bias, ALU.add))
                    ch.link(nc.vector.reduce_sum(gs[:, b, :], grouped(kv[:, b, :]), axis=AX))
                    ch.link(nc.vector.tensor_scalar(gs[:, b, :], gs[:, b, :], 1.0 / HC, None, ALU.mult))
                    nc.vector.tensor_tensor(kv[:, b, :].rearrange("p (g c) -> p g c", c=HC), grouped(kv[:, b, :]),
                                            spread(gs[:, b, :]), ALU.subtract).then_inc(s_cen, 1)
                    dve.wait_ge(s_sq, t + 1)
                    ch.link(nc.vector.reduce_sum(gv[:, b, :], grouped(sq[:, b, :]), axis=AX))
                    nc.vector.tensor_scalar(gv[:, b, :], gv[:, b, :], 1.0 / HC, EPS, ALU.mult, ALU.add).then_inc(s_gd, 1)
                    dve.wait_ge(s_gstd, t + 1)
                    ch.link(nc.vector.reciprocal(gd[:, b, :], gv[:, b, :]))
                    nc.vector.tensor_tensor(grouped(kvg[:, b, :]), grouped(kv[:, b, :]), spread(gd[:, b, :]),
                                            ALU.mult).then_inc(s_nrm, 1)
            loop2(dve, ch, NT // 2, 2 * 5, step)
            nc.vector.memset(kvbd[:, :, :], 0.0).then_inc(s_kvd, 1)
            dve.wait_ge(s_kvd, 1)
            dve.wait_ge(s_end, 1)
            for h in range(CH):
                for q in range(4):
                    r = slice(32 * q, 32 * q + 32)
                    nc.vector.tensor_scalar(kvbd[r, h, r], p_kv[r, h * 128 + 32 * q:h * 128 + 32 * q + 32],
                                            1.0 / N, None, ALU.mult)

        @block.gpsimd
        def _(pool):
            pool.wait_ge(s_zero, 1)
            pool.wait_ge(s_bias, 80)
            pool.engine_nop().then_inc(s_kn, 1)

            def both(t2):
                return t2.unsqueeze(1).to_broadcast([P, HEADS, HC])

            def step(i, first_step):
                for b in range(2):
                    t = 2 * i + b
                    pool.wait_ge(s_nrm, t + 1)
                    pool.wait_ge(s_kva, t + 1)
                    src = kvg[:, b, :].rearrange("p (h s c) -> p h s c", s=2, c=HC)
                    for j in range(2):
                        last = nc.gpsimd.tensor_tensor(src[:, :, j, :], src[:, :, j, :], both(ln_g[:, j, :]), ALU.mult)
                    last.then_inc(s_pool, 1)
                    pool.wait_ge(s_pool, t + 1)
                    for j in range(2):
                        last = nc.gpsimd.tensor_tensor(kn[:, b, j, :].rearrange("p (h c) -> p h c", c=HC),
                                                       src[:, :, j, :], both(ln_b[:, j, :]), ALU.add)
                    last.then_inc(s_kn, 1)
            loop2(pool, None, NT // 2, 0, step)

        @block.scalar
        def _(act):
            act.wait_ge(s_var, 1)
            nc.scalar.activation(std[:, :], std[:, :], ACT.Sqrt).then_inc(s_std, 1)

            def step(i, first_step):
                for b in range(2):
                    t = 2 * i + b
                    act.wait_ge(s_tp, t + 1)
                    if not first_step:
                        act.wait_ge(s_xtw[b], 16 * i)
                        act.wait_ge(s_kp, t - 1)
                    nc.scalar.activation(xt[:, b, :], p_t[b][:, 0:CH * P], ACT.Copy).then_inc(s_xt, 1)
                    act.wait_ge(s_bp, t + 1)
                    if not first_step:
                        act.wait_ge(s_tabw[b], 16 * i)
                    nc.scalar.activation(rows[:, b, 0:TW], p_b[b][0:P, 0:TW], ACT.Copy)
                    nc.scalar.activation(rows[:, b, TW:TW + 1], dinv[:, bass.ds(t, 1)], ACT.Copy).then_inc(s_row, 1)
                    act.wait_ge(s_cen, t + 1)
                    nc.scalar.activation(sq[:, b, :], kv[:, b, :], ACT.Square).then_inc(s_sq, 1)
                    act.wait_ge(s_gd, t + 1)
                    nc.scalar.activation(gv[:, b, :], gv[:, b, :], ACT.Sqrt).then_inc(s_gstd, 1)
            act.wait_ge(s_din, 16)
            loop2(act, None, NT // 2, 0, step)

        @block.tensor
        def _(pe):
            pe.wait_ge(s_w, 64)
            pe.wait_ge(s_zero, 1)
            nc.tensor.matmul(p_kv[:, 0:C], zero[:, 0:128], zero[:, :], start=True, stop=False).then_inc(s_kva, 1)

            def kv_sum(b):
                for h in range(CH):
                    last = nc.tensor.matmul(p_kv[:, h * 128:(h + 1) * 128], kn[:, b, 0, h * 128:(h + 1) * 128],
                                            kn[:, b, 1, h * 128:(h + 1) * 128], start=False, stop=False)
                return last

            def step(i, first_step):
                for b in range(2):
                    t = 2 * i + b
                    pe.wait_ge(s_xn, t + 1)
                    if not first_step:
                        pe.wait_ge(s_xt, t - 1)
                    for k in range(CH):
                        last = nc.tensor.transpose(p_t[b][:, k * P:(k + 1) * P], xn[:, b, k * 128:(k + 1) * 128], ident[0:P, 0:P])
                    last.then_inc(s_tp, 1)
                    pe.wait_ge(s_xt, t + 1)
                    if not first_step:
                        pe.wait_ge(s_row, t - 1)
                        pe.wait_ge(s_cen, t - 1)
                    for k in range(CH):
                        last = nc.tensor.matmul(p_b[b][0:P, 0:TW], xt[:, b, k * P:(k + 1) * P],
                                                wb[:, k].rearrange("p l w -> p (l w)"), start=k == 0, stop=k == CH - 1)
                    last.then_inc(s_bp, 1)
                    for k in range(CH):
                        rhs = wqkv[:, k, :].rearrange("p (h s) -> p h s", s=3 * HC)[:, :, HC:]
                        last = nc.tensor.matmul(p_k[b][0:P, :].rearrange("p (h s) -> p h s", s=2 * HC),
                                                xt[:, b, k * P:(k + 1) * P], rhs, start=k == 0, stop=k == CH - 1)
                    last.then_inc(s_kp, 1)
                    pe.wait_ge(s_kn, t + 1)
                    kv_sum(1 - b).then_inc(s_kva, 1)
            loop2(pe, None, NT // 2, 0, step)
            pe.wait_ge(s_kn, NT + 1)
            kv_sum(1)
            nc.tensor.matmul(p_kv[:, 0:C], zero[:, 0:128], zero[:, :], start=False, stop=True).then_inc(s_end, 1)


def phase_edges(nc, phase, a, d, ident):
    PAIRS = GROUPS // 2
    COLS = GROUPS * CHUNKS
    with phase("e", clear=True) as (c, sb, ps, sm):
        raw98 = sb("raw98", [GROUPS, 2, 2, NG])
        cnt = sb("cnt", [128, GROUPS])
        cmax = sb("cmax", [GROUPS, 1])
        start = sb("start", [128, GROUPS])
        start_c = sb("start_c", [128, GROUPS])
        start_i = sb("start_i", [128, GROUPS], I32)
        own_i = sb("own_i", [128, GROUPS], I32)
        own = sb("own", [128, GROUPS])
        slot_i = sb("slot_i", [128, CHUNKS], I32)
        slot = sb("slot", [128, CHUNKS])
        not_own = sb("not_own", [128, CHUNKS])
        half = sb("half", [128, 1])
        runs = sb("runs", [128, GROUPS, SLOTS], I32)
        valid = sb("valid", [128, COLS])
        take = sb("take", [128, COLS])
        idx = sb("idx", [128, COLS], I32)
        row = sb("row", [1, GROUPS])
        row_c = sb("row_c", [1, GROUPS])
        one = sb("one", [1, GROUPS])
        iters_i = sb("iters_i", [1, GROUPS], I32)
        iters = sb("iters", [1, GROUPS])
        upto = sb("upto", [1, GROUPS])
        base_i = sb("base_i", [1, GROUPS], I32)
        carry = sb("carry", [1, 1])
        top = sb("top", [1, 4])
        pass_i = sb("pass_i", [1, 1], I32)
        e2 = sb("e2", [128, NG])
        zero_b = sb("zero_b", [128, TW], BF16)
        ibuf = sb("ibuf", [128, UNROLL], I32)
        g = sb("g", [128, UNROLL, TW + 1])
        dg = sb("dg", [128, UNROLL, 128])
        prev = sb("prev", [128, 2, TW])
        acc = sb("acc", [128, 2, TW])
        ev = sb("ev", [128, 2, TW])
        p_s = [ps(f"p_s{b}") for b in range(2)]
        p_tr = ps("p_tr")
        p_row = ps("p_row")
        (s_in, s_dve, s_gp, s_tr, s_cmax, s_row, s_start, s_table, s_npass, s_e2, s_act) = (sm(n) for n in
            ("in", "dve", "gp", "tr", "cmax", "row", "start", "table", "npass", "e2", "act"))
        s_ib, s_pe, s_max, s_dg, s_group, s_ev, s_acc, s_pass = (sm(n) for n in
            ("ib", "pe", "max", "dg", "group", "ev", "acc", "pass"))
        s_runs = sm("runs", swdge=True)
        s_g = [sm(f"g{j}", swdge=True) for j in range(UNROLL)]
        s_ld = [sm(f"ld{b}") for b in range(2)]
        s_st = [sm(f"st{b}") for b in range(2)]
        block = c.enter_context(nc.Block())

        def passes(eng):
            eng.wait_ge(s_npass, 1)
            return eng.value_load(pass_i[0:1, 0:1], min_val=1, max_val=E // SLOTS + 2)

        def group_iters(eng, t):
            n = eng.value_load(iters_i[0:1, bass.ds(t, 1)], min_val=1, max_val=CHUNKS // UNROLL)
            first = eng.value_load(base_i[0:1, bass.ds(t, 1)], min_val=0, max_val=1 << 19)
            return n, first

        @block.sync
        def _(sp):
            for k, name in enumerate(("cnt", "rp")):
                for h in range(2):
                    sp.dma_start(raw98[:, k, h, :], d[name].rearrange("(g l) -> g l", l=NG)).then_inc(s_in, 16)

            def part(t, r):
                return d["agg"][bass.ds(t * NG, NG), r:r + 1, :].rearrange("n o w -> n (o w)")

            def load(t, b):
                for h in range(2):
                    sp.dma_start(prev[h * NG:(h + 1) * NG, b, :], part(t, h)).then_inc(s_ld[b], 16)
                    sp.dma_start(acc[h * NG:(h + 1) * NG, b, :], part(t, 2 + h)).then_inc(s_ld[b], 16)

            def store(t, b, p):
                sp.wait_ge(s_ev, p * GROUPS + t + 1)
                sp.wait_ge(s_acc, p * GROUPS + t + 1)
                for h in range(2):
                    sp.dma_start(part(t, h), ev[h * NG:(h + 1) * NG, b, :]).then_inc(s_st[b], 16)
                    sp.dma_start(part(t, 2 + h), acc[h * NG:(h + 1) * NG, b, :]).then_inc(s_st[b], 16)

            def step(i, p, first, last):
                if not first:
                    sp.wait_ge(s_st[1], 64 * (p * PAIRS + i))
                load(2 * i + 1, 1)
                store(2 * i, 0, p)
                if not last:
                    sp.wait_ge(s_st[0], 64 * (p * PAIRS + i + 1))
                    load(2 * i + 2, 0)
                store(2 * i + 1, 1, p)

            n_pass = passes(sp)
            with sp.Fori(0, n_pass) as p:
                load(0, 0)
                step(0, p, True, False)
                with sp.Fori(1, PAIRS - 1) as i:
                    step(i, p, False, False)
                step(PAIRS - 1, p, False, True)
                for b in range(2):
                    sp.wait_ge(s_st[b], 64 * PAIRS * (p + 1))
                sp.nop(nofuse=True)
                sp.sem_inc(s_pass, 1)

        @block.gpsimd
        def _(pool):
            nc.gpsimd.memset(half[0:NG, :], 0.0).then_inc(s_gp, 1)
            nc.gpsimd.memset(half[NG:128, :], 1.0).then_inc(s_gp, 1)
            for h in range(2):
                lanes = slice(h * NG, (h + 1) * NG)
                nc.gpsimd.iota(own_i[lanes, :], pattern=[[NG, GROUPS]], base=0, channel_multiplier=1).then_inc(s_gp, 1)
                nc.gpsimd.iota(slot_i[lanes, :], pattern=[[2, CHUNKS]], base=h, channel_multiplier=0).then_inc(s_gp, 1)
            n_pass = passes(pool)
            with pool.Fori(0, n_pass) as p:
                pool.wait_ge(s_start, p + 1)
                pool.nop(nofuse=True)
                for t in range(GROUPS):
                    nc.gpsimd.indirect_dma_start(
                        out=runs[:, t, :], out_offset=None, in_=d["runs"][:, :],
                        in_offset=bass.IndirectOffsetOnAxis(ap=start_i[:, t:t + 1], axis=0)).then_inc(s_runs, 16)
                pool.wait_ge(s_table, p + 1)
                pool.nop(nofuse=True)
                with pool.Fori(0, GROUPS) as t:
                    n, first = group_iters(pool, t)
                    with pool.Fori(0, n) as i:
                        it = first + i
                        for q in range(0, UNROLL, 2):
                            pool.wait_ge(s_pe, it * UNROLL + (q + 2))
                            pool.wait_ge(s_max, it * UNROLL + (q + 2))
                            nc.gpsimd.tensor_copy(ibuf[:, q:q + 2], idx[:, bass.ds(t * CHUNKS + i * UNROLL + q, 2)]).then_inc(s_ib, 1)
                            pool.wait_ge(s_ib, it * (UNROLL // 2) + (q // 2 + 1))
                            pool.nop(nofuse=True)
                            for j in (q, q + 1):
                                nc.gpsimd.indirect_dma_start(
                                    out=g[:, j, :], out_offset=None, in_=d["tab"][:, :],
                                    in_offset=bass.IndirectOffsetOnAxis(ap=ibuf[:, j:j + 1], axis=0)).then_inc(s_g[j], 16)

        @block.vector
        def _(dve):
            ch = Chain(dve, s_dve)
            v = nc.vector
            dve.sem_inc(s_max, UNROLL)
            v.memset(one[:, :], 1.0)
            v.memset(zero_b[:, :], 0.0)
            v.memset(carry[:, :], 0.0)
            for h in range(2):
                lanes = slice(h * NG, (h + 1) * NG)
                last = v.tensor_copy(e2[lanes, :], ident[lanes, lanes])
            last.then_inc(s_e2, 1)
            dve.wait_ge(s_in, 64)
            v.reduce_max(cmax[:, :], raw98[:, 0, 0, :], axis=AX).then_inc(s_cmax, 1)
            dve.wait_ge(s_gp, 6)
            v.tensor_copy(own[:, :], own_i[:, :])
            ch.link(v.tensor_copy(slot[:, :], slot_i[:, :]))
            dve.wait_ge(s_tr, 1)
            v.tensor_copy(cnt[:, :], p_tr[:, 0:GROUPS])
            v.tensor_scalar(start[:, :], p_tr[:, 128:128 + GROUPS], half[:, 0:1], None, ALU.add)
            ch.link(v.tensor_copy(row[:, :], p_row[0:1, 0:GROUPS]))
            ch.link(v.reduce_max(top[:, 0:1], row[:, :], axis=AX))
            ch.link(v.tensor_scalar(top[:, 1:2], top[:, 0:1], SLOTS + 0.5, 1.0 / SLOTS, ALU.add, ALU.mult))
            ch.link(v.tensor_copy(pass_i[:, :], top[:, 1:2]))
            ch.link(v.tensor_copy(top[:, 2:3], pass_i[:, :]))
            ch.link(v.tensor_tensor(top[:, 3:4], top[:, 2:3], top[:, 1:2], ALU.is_gt))
            ch.link(v.tensor_tensor(top[:, 2:3], top[:, 2:3], top[:, 3:4], ALU.subtract))
            v.tensor_copy(pass_i[:, :], top[:, 2:3]).then_inc(s_npass, 1)
            n_pass = passes(dve)
            before = ch.n
            PER_PASS = 14

            def wide(t2):
                return t2.unsqueeze(2).to_broadcast([128, GROUPS, CHUNKS])

            def over(t2):
                return t2.unsqueeze(1).to_broadcast([128, GROUPS, CHUNKS])

            def cube(t2):
                return t2.rearrange("p (g k) -> p g k", k=CHUNKS)

            with dve.Fori(0, n_pass) as p:
                ch.base = p * PER_PASS
                ch.link(v.tensor_scalar(start_c[:, :], start[:, :], float(E), None, ALU.min))
                v.tensor_copy(start_i[:, :], start_c[:, :]).then_inc(s_start, 1)
                ch.link(v.tensor_scalar(row_c[:, :], row[:, :], 2.0 * UNROLL, 2.0 * UNROLL, ALU.add, ALU.max))
                ch.link(v.tensor_scalar(row_c[:, :], row_c[:, :], float(SLOTS), None, ALU.min))
                ch.link(v.tensor_copy(iters_i[:, :], row_c[:, :]))
                ch.link(v.tensor_single_scalar(iters_i[:, :], iters_i[:, :], 3, op=ALU.logical_shift_right))
                ch.link(v.tensor_copy(iters[:, :], iters_i[:, :]))
                ch.link(v.tensor_tensor_scan(upto[:, :], one[:, :], iters[:, :], carry[:, 0:1], ALU.mult, ALU.add))
                ch.link(v.tensor_tensor(iters[:, :], upto[:, :], iters[:, :], ALU.subtract))
                v.tensor_copy(base_i[:, :], iters[:, :])
                ch.link(v.tensor_copy(carry[:, :], upto[:, GROUPS - 1:GROUPS]))
                v.tensor_tensor(cube(valid[:, :]), over(slot[:, :]), wide(cnt[:, :]), ALU.is_le)
                ch.link(v.tensor_scalar(not_own[:, :], slot[:, :], 0.5, None, ALU.is_gt))
                ch.link(v.tensor_tensor(cube(take[:, :]), cube(valid[:, :]), over(not_own[:, :]), ALU.mult))
                dve.wait_ge(s_runs, 16 * GROUPS * (p + 1))
                edge = runs[:, :, :].rearrange("p g (k s) -> p g k s", s=2)[:, :, :, 0]
                ch.link(v.tensor_tensor(edge, edge, wide(own_i[:, :]), ALU.subtract))
                ch.link(v.tensor_tensor(cube(take[:, :]), cube(take[:, :]), edge, ALU.mult))
                v.tensor_tensor(cube(idx[:, :]), cube(take[:, :]), wide(own[:, :]), ALU.add).then_inc(s_table, 1)
                dve.wait_ge(s_table, p + 1)
                dve.nop(nofuse=True)

                def group(t, b, k):
                    n, first = group_iters(dve, t)
                    dve.wait_ge(s_ld[b], 64 * (k + 1))
                    dve.nop(nofuse=True)
                    with dve.Fori(0, n) as i:
                        it = first + i
                        for j in range(UNROLL):
                            dve.wait_ge(s_g[j], 16 * (it + 1))
                            dve.wait_ge(s_max, it * UNROLL + (UNROLL + j))
                            v.tensor_tensor(acc[:, b, :], acc[:, b, :], g[:, j, 0:TW], ALU.max).then_inc(s_max, 1)
                    dve.wait_ge(s_max, (first + n) * UNROLL + UNROLL)
                    v.memset(top[0:1, 0:1], 0.0).then_inc(s_acc, 1)

                with dve.Fori(0, PAIRS) as i:
                    for b in range(2):
                        group(2 * i + b, b, p * PAIRS + i)
                dve.wait_ge(s_pass, p + 1)
                v.tensor_scalar(start[:, :], start[:, :], float(SLOTS), None, ALU.add)
                v.tensor_scalar(row[:, :], row[:, :], -float(SLOTS), None, ALU.add)
                ch.link(v.tensor_scalar(slot[:, :], slot[:, :], float(SLOTS), None, ALU.add))
                assert ch.n - before == PER_PASS, ch.n - before

        @block.scalar
        def _(act):
            act.wait_ge(s_e2, 1)
            n_pass = passes(act)
            with act.Fori(0, n_pass) as p:
                act.wait_ge(s_table, p + 1)
                act.nop(nofuse=True)

                def group(t, b):
                    n, first = group_iters(act, t)
                    with act.Fori(0, n) as i:
                        it = first + i
                        for j in range(UNROLL):
                            act.wait_ge(s_pe, it * UNROLL + (j + 1))
                            nc.scalar.activation(dg[:, j, 0:NG], e2[:, :], ACT.Copy,
                                                 scale=valid[:, bass.ds(t * CHUNKS + i * UNROLL + j, 1)]).then_inc(s_act, 1)
                        for j in range(UNROLL):
                            act.wait_ge(s_g[j], 16 * (it + 1))
                            act.wait_ge(s_act, it * UNROLL + (j + 1))
                            nc.scalar.activation(dg[:, j, NG:2 * NG], dg[:, j, 0:NG], ACT.Copy,
                                                 scale=g[:, j, TW:TW + 1]).then_inc(s_dg, 1)
                    act.wait_ge(s_group, p * GROUPS + t + 1)
                    nc.scalar.activation(ev[:, b, :], p_s[b][:, 0:TW], ACT.Copy).then_inc(s_ev, 1)

                with act.Fori(0, PAIRS) as i:
                    for b in range(2):
                        group(2 * i + b, b)

        @block.tensor
        def _(pe):
            pe.sem_inc(s_pe, UNROLL)
            pe.wait_ge(s_in, 64)
            pe.wait_ge(s_e2, 1)
            for k in range(2):
                nc.tensor.transpose(p_tr[:, k * 128:k * 128 + GROUPS], raw98[:, k].rearrange("g h l -> g (h l)"),
                                    ident[0:GROUPS, 0:GROUPS])
            pe.wait_ge(s_cmax, 1)
            nc.tensor.transpose(p_row[0:1, 0:GROUPS], cmax[:, :], ident[0:GROUPS, 0:GROUPS]).then_inc(s_tr, 1)
            n_pass = passes(pe)
            with pe.Fori(0, n_pass) as p:
                pe.wait_ge(s_table, p + 1)
                pe.nop(nofuse=True)

                def group(t, b, k):
                    n, first = group_iters(pe, t)
                    pe.wait_ge(s_ld[b], 64 * (k + 1))
                    nc.tensor.matmul(p_s[b][:, 0:TW], ident[:, :], prev[:, b, :], start=True, stop=False)
                    with pe.Fori(0, n) as i:
                        it = first + i
                        for j in range(UNROLL):
                            pe.wait_ge(s_dg, it * UNROLL + (j + 1))
                            nc.tensor.matmul(p_s[b][:, 0:TW], dg[:, j, :], g[:, j, 0:TW], start=False,
                                             stop=False).then_inc(s_pe, 1)
                    nc.tensor.matmul(p_s[b][:, 0:TW], zero_b[:, 0:128], zero_b[:, :], start=False,
                                     stop=True).then_inc(s_group, 1)

                with pe.Fori(0, PAIRS) as i:
                    for b in range(2):
                        group(2 * i + b, b, p * PAIRS + i)


def phase_conv(nc, phase, a, d, ident, stats):
    K = 3 * BASES
    LH = L * HEADS
    H2 = 2 * L
    with phase("c") as (c, sb, ps, sm):
        wc = sb("wc", [128, CH, L, 128])
        bc = sb("bc", [P, L * 128])
        cb = sb("cb", [P, L * C])
        dinv = sb("dinv", [P, NT])
        invdeg = sb("invdeg", [P, NT])
        xt = sb("xt", [128, 2, CH * P])
        ag = sb("ag", [P, 2, 4, TW])
        w16 = sb("w16", [P, 2, LH * 16])
        w12 = sb("w12", [P, 2, LH, K])
        prod = sb("prod", [P, L, HEADS, K, HC])
        h = sb("h", [P, 2, L * C])
        ht = sb("ht", [128, 2, H2 * P])
        p_w = [ps(f"p_w{b}") for b in range(2)]
        p_h = [[ps(f"p_h{b}{q}") for q in range(2)] for b in range(2)]
        (s_const, s_dve, s_pool, s_cw, s_w12, s_mx, s_prod, s_red, s_h, s_tp, s_ht, s_st) = (sm(n) for n in
            ("const", "dve", "pool", "cw", "w12", "mx", "prod", "red", "h", "tp", "ht", "st"))
        s_ld = [sm(f"ld{b}") for b in range(2)]
        s_out = [sm(f"out{b}") for b in range(2)]
        block = c.enter_context(nc.Block())
        agg = d["agg"][0:N].rearrange("(p t) r w -> p t (r w)", t=NT)

        @block.sync
        def _(sp):
            for k in range(CH):
                sp.dma_start(wc[:, k], a["L0_gnn_Wc"][:, k * 128:(k + 1) * 128, :].rearrange("l p w -> p l w")).then_inc(s_const, 16)
            for t, name in ((bc, "L0_gnn_bc"), (cb, "L0_gnn_conv_bias")):
                sp.dma_start(t[:, :], a[name].rearrange("(o l) n -> o (l n)", o=1).to_broadcast([P, t.shape[1]])).then_inc(s_const, 16)
            sp.dma_start(dinv[:, :], d["dinv"][0:N].rearrange("(p t) -> p t", t=NT)).then_inc(s_const, 16)

            def step(i, first):
                for b in range(2):
                    t = 2 * i + b
                    if not first:
                        sp.wait_ge(s_red, t - 1)
                        sp.wait_ge(s_cw, t - 1)
                    sp.dma_start(ag[:, b].rearrange("p r w -> p (r w)"), agg[:, bass.ds(t, 1), :].rearrange("p o w -> p (o w)")).then_inc(s_ld[b], 16)
                    sp.dma_start(xt[:, b], d["xnt"][bass.ds(t, 1)].rearrange("o p c -> (o p) c")).then_inc(s_ld[b], 16)
            loop2(sp, None, NT // 2, 0, step)

        @block.scalar
        def _(act):
            def step(i, first):
                for b in range(2):
                    t = 2 * i + b
                    act.wait_ge(s_tp, t + 1)
                    if not first:
                        act.wait_ge(s_out[b], 16 * i)
                        act.wait_ge(s_st, t - 1)
                    nc.scalar.activation(ht[:, b, 0:4 * P], p_h[b][0][:, 0:4 * P], ACT.Copy)
                    nc.scalar.activation(ht[:, b, 4 * P:], p_h[b][1][:, 0:2 * P], ACT.Copy).then_inc(s_ht, 1)
                    act.wait_ge(s_ht, t + 1)
                    act.dma_start(d["ht"][bass.ds(t, 1)].rearrange("o p c -> (o p) c"), ht[:, b]).then_inc(s_out[b], 16)
            loop2(act, None, NT // 2, 0, step)
            for b in range(2):
                act.wait_ge(s_out[b], 16 * (NT // 2))

        @block.gpsimd
        def _(pool):
            def step(i, first):
                for b in range(2):
                    t = 2 * i + b
                    pool.wait_ge(s_ld[b], 32 * (i + 1))
                    pool.wait_ge(s_w12, t + 1)
                    if not first or b:
                        pool.wait_ge(s_red, t)
                    for l in range(L):
                        for r in range(2):
                            last = nc.gpsimd.tensor_tensor(
                                prod[:, l, :, r * BASES:(r + 1) * BASES, :],
                                w12[:, b, l * HEADS:(l + 1) * HEADS, r * BASES:(r + 1) * BASES].unsqueeze(3).to_broadcast([P, HEADS, BASES, HC]),
                                ag[:, b, r, l * BW:(l + 1) * BW].rearrange("p (k c) -> p k c", c=HC).unsqueeze(1).to_broadcast([P, HEADS, BASES, HC]),
                                ALU.mult)
                    last.then_inc(s_prod, 1)
            loop2(pool, None, NT // 2, 0, step)

        @block.vector
        def _(dve):
            ch = Chain(dve, s_dve)
            v = nc.vector
            dve.wait_ge(s_const, 80)
            ch.link(v.tensor_tensor(invdeg[:, :], dinv[:, :], dinv[:, :], ALU.mult))

            def step(i, first):
                for b in range(2):
                    t = 2 * i + b
                    dve.wait_ge(s_cw, t + 1)
                    ch.link(v.tensor_tensor(w16[:, b, :], p_w[b][0:P, 0:LH * 16], bc[:, :], ALU.add))
                    w = w16[:, b, :].rearrange("p (x r k) -> p x r k", r=4, k=BASES)
                    v.scalar_tensor_tensor(w12[:, b, :, 0:BASES], w[:, :, 0], invdeg[:, bass.ds(t, 1)], w[:, :, 2], ALU.mult, ALU.add)
                    v.tensor_scalar(w12[:, b, :, BASES:2 * BASES], w[:, :, 3], dinv[:, bass.ds(t, 1)], None, ALU.mult)
                    v.tensor_copy(w12[:, b, :, 2 * BASES:], w[:, :, 1]).then_inc(s_w12, 1)
                    dve.wait_ge(s_ld[b], 32 * (i + 1))
                    v.tensor_tensor(ag[:, b, 2, :], ag[:, b, 2, :], ag[:, b, 3, :], ALU.max).then_inc(s_mx, 1)
                    dve.wait_ge(s_mx, t + 1)
                    dve.wait_ge(s_w12, t + 1)
                    for l in range(L):
                        last = v.tensor_tensor(
                            prod[:, l, :, 2 * BASES:, :],
                            w12[:, b, l * HEADS:(l + 1) * HEADS, 2 * BASES:].unsqueeze(3).to_broadcast([P, HEADS, BASES, HC]),
                            ag[:, b, 2, l * BW:(l + 1) * BW].rearrange("p (k c) -> p k c", c=HC).unsqueeze(1).to_broadcast([P, HEADS, BASES, HC]),
                            ALU.mult)
                    ch.link(last)
                    dve.wait_ge(s_prod, t + 1)
                    if not first:
                        dve.wait_ge(s_tp, t - 1)
                    for l in range(L):
                        last = v.reduce_sum(h[:, b, l * C:(l + 1) * C].rearrange("p (h c) -> p h c", c=HC),
                                            prod[:, l].rearrange("p h k c -> p h c k"), axis=AX)
                    last.then_inc(s_red, 1)
                    dve.wait_ge(s_red, t + 1)
                    v.tensor_tensor(h[:, b, :], h[:, b, :], cb[:, :], ALU.add).then_inc(s_h, 1)
                    dve.wait_ge(s_ht, t + 1)
                    for k in range(H2):
                        last = v.bn_stats(stats[:, k, bass.ds(t, 1), :].rearrange("p o s -> p (o s)"),
                                          ht[:, b, k * P:(k + 1) * P])
                    last.then_inc(s_st, 1)
            loop2(dve, ch, NT // 2, 2 * 2, step)

        @block.tensor
        def _(pe):
            pe.wait_ge(s_const, 80)

            def step(i, first):
                for b in range(2):
                    t = 2 * i + b
                    pe.wait_ge(s_ld[b], 32 * (i + 1))
                    if not first:
                        pe.wait_ge(s_w12, t - 1)
                    for k in range(CH):
                        last = nc.tensor.matmul(p_w[b][0:P, 0:TW], xt[:, b, k * P:(k + 1) * P],
                                                wc[:, k].rearrange("p l w -> p (l w)"), start=k == 0, stop=k == CH - 1)
                    last.then_inc(s_cw, 1)
                    pe.wait_ge(s_h, t + 1)
                    if not first:
                        pe.wait_ge(s_ht, t - 1)
                    for k in range(H2):
                        last = nc.tensor.transpose(p_h[b][k // 4][:, (k % 4) * P:(k % 4 + 1) * P],
                                                   h[:, b, k * 128:(k + 1) * 128], ident[0:P, 0:P])
                    last.then_inc(s_tp, 1)
            loop2(pe, None, NT // 2, 0, step)


def phase_mix(nc, phase, a, d, ident, x_sb, mv, rstd, kvbd, stats):
    H2 = 2 * L
    KF = 2 + H2
    with phase("m") as (c, sb, ps, sm):
        fcw = sb("fcw", [128, KF, C])
        wq = sb("wq", [128, CH, C])
        w1 = sb("w1", [128, CH, C])
        w2 = sb("w2", [128, CH, C])
        b_q = sb("b_q", [128, CH])
        b1 = sb("b1", [128, CH])
        gam = sb("gam", [128, H2])
        bet = sb("bet", [128, H2])
        fcb = sb("fcb", [P, C])
        b2 = sb("b2", [P, C])
        bmv = sb("bmv", [128, H2, 2])
        bs = sb("bs", [128, H2])
        bb = sb("bb", [128, H2])
        wqt = sb("wqt", [128, CH, C])
        rt = sb("rt", [128, CH, C])
        m1 = sb("m1", [128, CH, C])
        u = sb("u", [128, CH])
        c1 = sb("c1", [128, CH])
        xt = sb("xt", [128, 2, CH * P])
        ht = sb("ht", [128, 2, H2 * P])
        z = sb("z", [128, 2, H2 * P])
        gt = sb("gt", [128, 2, CH * P])
        xn = sb("xn", [P, 2, C])
        p_a = ps("p_a")
        p_b = ps("p_b")
        p_g = [ps(f"p_g{b}") for b in range(2)]
        p_o = [ps(f"p_o{b}") for b in range(2)]
        (s_c, s_dve, s_wqt, s_wqtc, s_rt, s_rtc, s_m1, s_m1c, s_u, s_uc, s_c1, s_c1c, s_bn, s_bns, s_bn2) = (sm(n) for n in
            ("c", "dve", "wqt", "wqtc", "rt", "rtc", "m1", "m1c", "u", "uc", "c1", "c1c", "bn", "bns", "bn2"))
        s_z, s_y, s_gp, s_gt, s_o, s_res, s_x2 = (sm(n) for n in ("z", "y", "gp", "gt", "o", "res", "x2"))
        s_ld = [sm(f"ld{b}") for b in range(2)]
        block = c.enter_context(nc.Block())

        @block.sync
        def _(sp):
            def rows128(name):
                return a[name].rearrange("(k p) n -> p k n", p=128)
            for k in range(CH):
                sp.dma_start(wq[:, k, :].rearrange("p (h s) -> p h s", s=HC),
                             a["L0_mix_w_qkv"][k * 128:(k + 1) * 128, :].rearrange("p (h s) -> p h s", s=3 * HC)[:, :, 0:HC]).then_inc(s_c, 16)
            sp.dma_start(w1[:, :, :], rows128("L0_mix_w1")).then_inc(s_c, 16)
            sp.dma_start(w2[:, :, :], rows128("L0_mix_w2")).then_inc(s_c, 16)
            sp.dma_start(fcw[:, :, :], rows128("L0_gnn_fc_W")).then_inc(s_c, 16)
            for k in range(CH):
                for h in range(4):
                    at = (4 * k + h) * 3 * HC
                    sp.dma_start(b_q[32 * h:32 * h + 32, k:k + 1],
                                 a["L0_mix_b_qkv"][at:at + HC].rearrange("(p o) -> p o", o=1)).then_inc(s_c, 16)
                sp.dma_start(b1[:, k:k + 1], a["L0_mix_b1"][k * 128:(k + 1) * 128].rearrange("(p o) -> p o", o=1)).then_inc(s_c, 16)
            for l in range(L):
                for k in range(CH):
                    sl = slice(k * 128, (k + 1) * 128)
                    q = l * CH + k
                    sp.dma_start(gam[:, q:q + 1], a["L0_gnn_bn_gamma"][l, sl].rearrange("(p o) -> p o", o=1)).then_inc(s_c, 16)
                    sp.dma_start(bet[:, q:q + 1], a["L0_gnn_bn_beta"][l, sl].rearrange("(p o) -> p o", o=1)).then_inc(s_c, 16)
            sp.dma_start(fcb[:, :], a["L0_gnn_fc_b"].rearrange("(o n) -> o n", o=1).to_broadcast([P, C])).then_inc(s_c, 16)
            sp.dma_start(b2[:, :], a["L0_mix_b2"].rearrange("(o n) -> o n", o=1).to_broadcast([P, C])).then_inc(s_c, 16)

            def step(i, first):
                for b in range(2):
                    t = 2 * i + b
                    if not first:
                        sp.wait_ge(s_o, t - 1)
                    sp.dma_start(ht[:, b], d["ht"][bass.ds(t, 1)].rearrange("o p c -> (o p) c")).then_inc(s_ld[b], 16)
                    sp.dma_start(xt[:, b], d["xnt"][bass.ds(t, 1)].rearrange("o p c -> (o p) c")).then_inc(s_ld[b], 16)
            loop2(sp, None, NT // 2, 0, step)
        N_CONST = 16 * (5 + 2 * 5 + 2 * H2 + 2)

        @block.vector
        def _(dve):
            ch = Chain(dve, s_dve)
            v = nc.vector
            dve.wait_ge(s_c, N_CONST)
            for k in range(H2):
                v.bn_aggr(bmv[:, k, :], stats[:, k, :, :].rearrange("p t s -> p (t s)"))
            ch.link(v.tensor_tensor(fcb[:, :], fcb[:, :], b2[:, :], ALU.add))
            v.tensor_scalar_add(bs[:, :], bmv[:, :, 1], EPS).then_inc(s_bn, 1)
            dve.wait_ge(s_bns, 1)
            ch.link(v.reciprocal(bb[:, :], bs[:, :]))
            ch.link(v.tensor_tensor(bs[:, :], bb[:, :], gam[:, :], ALU.mult))
            ch.link(v.tensor_tensor(bb[:, :], bs[:, :], bmv[:, :, 0], ALU.mult))
            v.tensor_tensor(bb[:, :], bet[:, :], bb[:, :], ALU.subtract).then_inc(s_bn2, 1)
            dve.wait_ge(s_wqt, 1)
            v.tensor_copy(wqt[:, 0, :], p_a[:, 0:C])
            v.tensor_copy(wqt[:, 1, :], p_a[:, C:2 * C]).then_inc(s_wqtc, 1)
            dve.wait_ge(s_rt, 1)
            ch.link(v.tensor_copy(rt[:, :, :], p_b[:, :].rearrange("p (k c) -> p k c", k=CH)))
            v.tensor_tensor(rt[:, 0, 0:128], rt[:, 0, 0:128], ident[:, :], ALU.add)
            v.tensor_tensor(rt[:, 1, 128:C], rt[:, 1, 128:C], ident[:, :], ALU.add).then_inc(s_rtc, 1)
            dve.wait_ge(s_m1, 1)
            v.tensor_copy(m1[:, :, :], p_a[:, :].rearrange("p (k c) -> p k c", k=CH)).then_inc(s_m1c, 1)
            dve.wait_ge(s_u, 1)
            v.tensor_copy(u[:, :], p_b[:, 0:CH]).then_inc(s_uc, 1)
            dve.wait_ge(s_c1, 1)
            v.tensor_tensor(c1[:, :], p_b[:, 8:8 + CH], b1[:, :], ALU.add).then_inc(s_c1c, 1)

            def step(i, first):
                for b in range(2):
                    t = 2 * i + b
                    dve.wait_ge(s_z, t + 1)
                    v.scalar_tensor_tensor(z[:, b, :], z[:, b, :], SLOPE, z[:, b, :], ALU.mult, ALU.max).then_inc(s_y, 1)
                    xrow = x_sb[:, bass.ds(t, 1), :].rearrange("p o c -> p (o c)")
                    ch.link(v.tensor_scalar(xn[:, b, :], xrow, mv[:, bass.ds(t, 1), 0], rstd[:, bass.ds(t, 1)], ALU.subtract, ALU.mult))
                    ch.link(v.tensor_tensor(xn[:, b, :], xn[:, b, :], xrow, ALU.add))
                    ch.link(v.tensor_tensor(xn[:, b, :], xn[:, b, :], fcb[:, :], ALU.add))
                    dve.wait_ge(s_o, t + 1)
                    v.tensor_tensor(xrow, p_o[b][0:P, 0:C], xn[:, b, :], ALU.add).then_inc(s_res, 1)
            loop2(dve, ch, NT // 2, 2 * 3, step)

        @block.scalar
        def _(act):
            act.wait_ge(s_bn, 1)
            nc.scalar.activation(bs[:, :], bs[:, :], ACT.Sqrt).then_inc(s_bns, 1)
            act.wait_ge(s_bn2, 1)
            act.wait_ge(s_c1c, 1)

            def step(i, first):
                for b in range(2):
                    t = 2 * i + b
                    act.wait_ge(s_ld[b], 32 * (i + 1))
                    if not first:
                        act.wait_ge(s_o, t - 1)
                    for k in range(H2):
                        sl = slice(k * P, (k + 1) * P)
                        last = nc.scalar.activation(z[:, b, sl], ht[:, b, sl], ACT.Identity, bias=bb[:, k:k + 1], scale=bs[:, k:k + 1])
                    last.then_inc(s_z, 1)
                    act.wait_ge(s_gp, t + 1)
                    for k in range(CH):
                        sl = slice(k * P, (k + 1) * P)
                        last = nc.scalar.activation(gt[:, b, sl], p_g[b][:, sl], ACT.Gelu, bias=c1[:, k:k + 1])
                    last.then_inc(s_gt, 1)
            loop2(act, None, NT // 2, 0, step)

        @block.tensor
        def _(pe):
            pe.wait_ge(s_c, N_CONST)
            for half in range(CH):
                for k in range(CH):
                    src = wq[:, k, half * 128:(half + 1) * 128]
                    last = nc.tensor.transpose(p_a[:, half * C + k * 128:half * C + (k + 1) * 128], src, ident[:, :])
            last.then_inc(s_wqt, 1)
            pe.wait_ge(s_wqtc, 1)
            for half in range(CH):
                last = nc.tensor.matmul(p_b[:, half * C:(half + 1) * C], kvbd[:, half, :], wqt[:, half, :], start=True, stop=True)
            last.then_inc(s_rt, 1)
            pe.wait_ge(s_rtc, 1)
            for k in range(CH):
                for half in range(CH):
                    last = nc.tensor.matmul(p_a[:, k * C:(k + 1) * C], rt[:, half, k * 128:(k + 1) * 128], w1[:, half, :],
                                            start=half == 0, stop=half == CH - 1)
            last.then_inc(s_m1, 1)
            for half in range(CH):
                last = nc.tensor.matmul(p_b[:, half:half + 1], kvbd[:, half, :], b_q[:, half:half + 1], start=True, stop=True)
            last.then_inc(s_u, 1)
            pe.wait_ge(s_uc, 1)
            for k in range(CH):
                for half in range(CH):
                    last = nc.tensor.matmul(p_b[:, 8 + k:9 + k], w1[:, half, k * 128:(k + 1) * 128], u[:, half:half + 1],
                                            start=half == 0, stop=half == CH - 1)
            last.then_inc(s_c1, 1)
            pe.wait_ge(s_m1c, 1)

            def step(i, first):
                for b in range(2):
                    t = 2 * i + b
                    pe.wait_ge(s_ld[b], 32 * (i + 1))
                    if not first:
                        pe.wait_ge(s_gt, t - 1)
                    for f in range(CH):
                        for k in range(CH):
                            last = nc.tensor.matmul(p_g[b][:, f * P:(f + 1) * P], m1[:, k, f * 128:(f + 1) * 128],
                                                    xt[:, b, k * P:(k + 1) * P], start=k == 0, stop=k == CH - 1)
                    last.then_inc(s_gp, 1)
                    if not first:
                        pe.wait_ge(s_res, t - 1)
                    for k in range(CH):
                        nc.tensor.matmul(p_o[b][0:P, 0:C], xt[:, b, k * P:(k + 1) * P], fcw[:, k, :], start=k == 0, stop=False)
                    pe.wait_ge(s_y, t + 1)
                    for k in range(H2):
                        nc.tensor.matmul(p_o[b][0:P, 0:C], z[:, b, k * P:(k + 1) * P], fcw[:, CH + k, :], start=False, stop=False)
                    pe.wait_ge(s_gt, t + 1)
                    for k in range(CH):
                        last = nc.tensor.matmul(p_o[b][0:P, 0:C], gt[:, b, k * P:(k + 1) * P], w2[:, k, :], start=False, stop=k == CH - 1)
                    last.then_inc(s_o, 1)
            loop2(pe, None, NT // 2, 0, step)


def phase_route(nc, phase, a, d, ident, x_sb, pos, gate, blk):
    X = EXPERTS
    T8 = NT * X
    with phase("r") as (c, sb, ps, sm):
        wr = sb("wr", [128, CH, X])
        br = sb("br", [P, X])
        xo = sb("xo", [P, NT, C])
        st = sb("st", [P, NT, 6])
        half = sb("half", [P, NT])
        mv = sb("mv", [P, NT, 2])
        mv2 = sb("mv2", [P, NT, 2])
        r1 = sb("r1", [P, NT])
        r2 = sb("r2", [P, NT])
        xt = sb("xt", [128, 2, CH * P])
        lg = sb("lg", [P, NT, X])
        lane_i = sb("lane_i", [P, X], I32)
        e_id = sb("e_id", [P, X])
        red = sb("red", [P, NT])
        tsum = sb("tsum", [P, NT])
        top1 = sb("top1", [P, NT])
        top2 = sb("top2", [P, NT])
        m1 = sb("m1", [P, NT, X])
        pick = sb("pick", [P, 2, NT, X])
        both = sb("both", [P, X, NT])
        ones = sb("ones", [P, T8])
        run = sb("run", [P, X, NT])
        lane = sb("lane", [P, X])
        lower = sb("lower", [P, P])
        fill = sb("fill", [P, X])
        fill_i = sb("fill_i", [P, X], I32)
        end = sb("end", [P, X])
        off = sb("off", [P, X])
        blk_i = sb("blk_i", [1, BLOCKS], I32)
        blk_f = sb("blk_f", [1, BLOCKS])
        blk_g = sb("blk_g", [1, BLOCKS, X])
        ibuf = sb("ibuf", [P, 2, 2], I32)
        xe = sb("xe", [P, 2, C])
        zeros = sb("zeros", [128, 4 * C])
        p_t = [ps(f"p_t{b}") for b in range(2)]
        p_l = [ps(f"p_l{b}") for b in range(2)]
        p_c = ps("p_c")
        (s_c, s_gp, s_dve, s_var, s_std, s_xo, s_tp, s_xt, s_lp, s_lg, s_var2, s_std2, s_ex, s_exd, s_lane,
         s_cnt, s_pos, s_xe, s_ib, s_x2, s_zero, s_zst, s_all) = (sm(n) for n in
            ("c", "gp", "dve", "var", "std", "xo", "tp", "xt", "lp", "lg", "var2", "std2", "ex", "exd", "lane",
             "cnt", "pos", "xe", "ib", "x2", "zero", "zst", "all"))
        s_sc = [sm(f"sc{b}", swdge=True) for b in range(2)]
        block = c.enter_context(nc.Block())

        @block.sync
        def _(sp):
            sp.dma_start(wr[:, :, :], a["L0_ffn_Wr"].rearrange("(k p) n -> p k n", p=128)).then_inc(s_c, 16)
            sp.dma_start(br[:, :], a["L0_ffn_br"].rearrange("(o n) -> o n", o=1).to_broadcast([P, X])).then_inc(s_c, 16)
            sp.dma_start(d["x2"].rearrange("(p t) c -> p t c", t=NT), x_sb[:, :, :]).then_inc(s_x2, 16)
            sp.wait_ge(s_zero, 1)
            for g in range(BLOCKS + 1):
                if g % 4 == 0:
                    n = min(4, BLOCKS + 1 - g)
                    sp.dma_start(d["xg"][g * 128:(g + n) * 128, :].rearrange("(p r) c -> p (r c)", p=128),
                                 zeros[:, 0:n * C]).then_inc(s_zst, 16)
            sp.wait_ge(s_x2, 16)
            sp.wait_ge(s_zst, 16 * (-(-(BLOCKS + 1) // 4)))

        @block.gpsimd
        def _(pool):
            g = nc.gpsimd
            g.memset(zeros[:, :], 0.0).then_inc(s_zero, 1)
            g.iota(lane_i[:, :], pattern=[[1, X]], base=0, channel_multiplier=0).then_inc(s_gp, 1)
            g.iota(blk_i[:, :], pattern=[[128, BLOCKS]], base=0, channel_multiplier=0).then_inc(s_gp, 1)
            g.memset(lower[:, :], 1.0).then_inc(s_gp, 1)
            pool.wait_ge(s_gp, 3)
            g.affine_select(out=lower[:, :], in_=lower[:, :], compare_op=ALU.is_gt, fill=0.0, base=0,
                            pattern=[[1, P]], channel_multiplier=-1).then_inc(s_gp, 1)
            pool.wait_ge(s_pos, 1)
            pool.wait_ge(s_zst, 16 * (-(-(BLOCKS + 1) // 4)))

            def step(i, first):
                for b in range(2):
                    t = 2 * i + b
                    if not first:
                        pool.wait_ge(s_sc[b], 32 * i)
                    g.tensor_copy(ibuf[:, b, :], pos[:, :, bass.ds(t, 1)].rearrange("p k o -> p (k o)")).then_inc(s_ib, 1)
                    pool.wait_ge(s_ib, t + 1)
                    pool.nop(nofuse=True)
                    pool.wait_ge(s_xe, t + 1)
                    pool.nop(nofuse=True)
                    for k in range(2):
                        g.indirect_dma_start(out=d["xg"][:, :], out_offset=bass.IndirectOffsetOnAxis(ap=ibuf[:, b, k:k + 1], axis=0),
                                             in_=xe[:, b, :], in_offset=None).then_inc(s_sc[b], 16)
            loop2(pool, None, NT // 2, 0, step)
            for b in range(2):
                pool.wait_ge(s_sc[b], 32 * (NT // 2))

        @block.scalar
        def _(act):
            act.wait_ge(s_var, 1)
            nc.scalar.activation(r1[:, :], r1[:, :], ACT.Sqrt).then_inc(s_std, 1)

            def step(i, first):
                for b in range(2):
                    t = 2 * i + b
                    act.wait_ge(s_tp, t + 1)
                    if not first:
                        act.wait_ge(s_lp, t - 1)
                    nc.scalar.activation(xt[:, b, :], p_t[b][:, 0:CH * P], ACT.Copy).then_inc(s_xt, 1)
            loop2(act, None, NT // 2, 0, step)
            act.wait_ge(s_var2, 1)
            nc.scalar.activation(r2[:, :], r2[:, :], ACT.Sqrt).then_inc(s_std2, 1)
            act.wait_ge(s_ex, 1)
            nc.scalar.activation(lg[:, :, :], lg[:, :, :], ACT.Exp).then_inc(s_exd, 1)

        @block.tensor
        def _(pe):
            pe.wait_ge(s_c, 32)

            def logits(t, b):
                pe.wait_ge(s_xt, t + 1)
                for k in range(CH):
                    last = nc.tensor.matmul(p_l[b][0:P, 0:X], xt[:, b, k * P:(k + 1) * P], wr[:, k, :], start=k == 0, stop=k == CH - 1)
                last.then_inc(s_lp, 1)

            def step(i, first):
                for b in range(2):
                    t = 2 * i + b
                    pe.wait_ge(s_xo, t + 1)
                    if not first:
                        pe.wait_ge(s_xt, t - 1)
                    for k in range(CH):
                        last = nc.tensor.transpose(p_t[b][:, k * P:(k + 1) * P],
                                                   xe[:, b, k * 128:(k + 1) * 128], ident[0:P, 0:P])
                    last.then_inc(s_tp, 1)
                    if not first:
                        pe.wait_ge(s_lg, t - 1)
                    logits(t, b)
            loop2(pe, None, NT // 2, 0, step)
            pe.wait_ge(s_lane, 1)
            pe.wait_ge(s_gp, 4)
            nc.tensor.matmul(p_c[0:P, 0:X], lower[:, :], lane[:, :], start=True, stop=True)
            nc.tensor.matmul(p_c[0:P, 8:8 + X], ones[:, 0:P], lane[:, :], start=True, stop=True).then_inc(s_cnt, 1)

        @block.vector
        def _(dve):
            ch = Chain(dve, s_dve)
            v = nc.vector
            v.memset(ones[:, :], 1.0)
            with dve.Fori(0, NT) as t:
                v.bn_stats(st[:, bass.ds(t, 1), :].rearrange("p o s -> p (o s)"),
                           x_sb[:, bass.ds(t, 1), :].rearrange("p o c -> p (o c)"))
            dve.drain()
            halves_to_mean_var(nc, ch, st, mv, half)
            v.tensor_scalar_add(r1[:, :], mv[:, :, 1], EPS).then_inc(s_var, 1)
            dve.wait_ge(s_std, 1)
            ch.link(v.reciprocal(r1[:, :], r1[:, :]))
            dve.wait_ge(s_c, 32)

            def cols(t3, t):
                return t3[:, bass.ds(t, 1), :].rearrange("p o c -> p (o c)")

            def step(i, first):
                for b in range(2):
                    t = 2 * i + b
                    ch.link(v.tensor_scalar(cols(xo, t), cols(x_sb, t), mv[:, bass.ds(t, 1), 0], r1[:, bass.ds(t, 1)], ALU.subtract, ALU.mult))
                    if not first:
                        dve.wait_ge(s_tp, t - 1)
                    v.tensor_scalar(xe[:, b, :], cols(x_sb, t), mv[:, bass.ds(t, 1), 0], r1[:, bass.ds(t, 1)], ALU.subtract, ALU.mult).then_inc(s_xo, 1)
                    v.bn_stats(cols(st, t), cols(xo, t))
                    dve.wait_ge(s_lp, t + 1)
                    v.tensor_tensor(cols(lg, t), p_l[b][0:P, 0:X], br[:, :], ALU.add).then_inc(s_lg, 1)
            loop2(dve, ch, NT // 2, 2, step)
            dve.drain()
            halves_to_mean_var(nc, ch, st, mv2, half)
            v.tensor_scalar_add(r2[:, :], mv2[:, :, 1], EPS).then_inc(s_var2, 1)
            dve.wait_ge(s_std2, 1)
            v.reciprocal(r2[:, :], r2[:, :])

            def by_token(t2):
                return t2.unsqueeze(2).to_broadcast([P, NT, X])

            ch.link(v.reduce_max(red[:, :], lg[:, :, :], axis=AX))
            v.tensor_tensor(lg[:, :, :], lg[:, :, :], by_token(red[:, :]), ALU.subtract).then_inc(s_ex, 1)
            dve.wait_ge(s_gp, 4)
            v.tensor_copy(e_id[:, :], lane_i[:, :])
            ch.link(v.tensor_copy(blk_f[:, :], blk_i[:, :]))
            dve.wait_ge(s_exd, 1)
            ch.link(v.reduce_sum(tsum[:, :], lg[:, :, :], axis=AX))
            ch.link(v.reciprocal(tsum[:, :], tsum[:, :]))
            ch.link(v.tensor_tensor(lg[:, :, :], lg[:, :, :], by_token(tsum[:, :]), ALU.mult))
            ids = e_id[:, :].unsqueeze(1).to_broadcast([P, NT, X])
            for k, top in enumerate((top1, top2)):
                ch.link(v.reduce_max(top[:, :], lg[:, :, :], axis=AX))
                ch.link(v.tensor_tensor(m1[:, :, :], lg[:, :, :], by_token(top[:, :]), ALU.not_equal))
                ch.link(v.scalar_tensor_tensor(m1[:, :, :], m1[:, :, :], 2.0 * X, ids, ALU.mult, ALU.add))
                ch.link(v.tensor_reduce(red[:, :], m1[:, :, :], axis=AX, op=ALU.min))
                ch.link(v.tensor_tensor(pick[:, k], ids, by_token(red[:, :]), ALU.is_equal))
                if k == 0:
                    ch.link(v.scalar_tensor_tensor(lg[:, :, :], pick[:, k], -2.0, lg[:, :, :], ALU.mult, ALU.add))
            ch.link(v.tensor_tensor(tsum[:, :], top1[:, :], top2[:, :], ALU.add))
            ch.link(v.reciprocal(tsum[:, :], tsum[:, :]))
            v.tensor_tensor(gate[:, 0, :], top1[:, :], tsum[:, :], ALU.mult)
            v.tensor_tensor(gate[:, 1, :], top2[:, :], tsum[:, :], ALU.mult)
            ch.link(v.tensor_tensor(both[:, :, :].rearrange("p e t -> p t e"), pick[:, 0], pick[:, 1], ALU.add))
            ch.link(v.tensor_tensor_scan(run[:, :, :].rearrange("p e t -> p (e t)"), ones[:, :],
                                         both[:, :, :].rearrange("p e t -> p (e t)"), 0.0, ALU.mult, ALU.add))
            v.tensor_copy(off[:, 0:1], run[:, 0:1, NT - 1])
            ch.link(v.tensor_copy(lane[:, 0:1], run[:, 0:1, NT - 1]))
            v.tensor_tensor(lane[:, 1:X], run[:, 1:X, NT - 1], run[:, 0:X - 1, NT - 1], ALU.subtract).then_inc(s_lane, 1)
            dve.wait_ge(s_cnt, 1)
            ch.link(v.tensor_scalar(fill[:, :], p_c[0:P, 8:8 + X], 127.0, None, ALU.add))
            ch.link(v.tensor_copy(fill_i[:, :], fill[:, :]))
            ch.link(v.tensor_single_scalar(fill_i[:, :], fill_i[:, :], 7, op=ALU.logical_shift_right))
            ch.link(v.tensor_copy(fill[:, :], fill_i[:, :]))
            ch.link(v.tensor_scalar(fill[:, :], fill[:, :], 128.0, None, ALU.mult))
            ch.link(v.tensor_tensor_scan(end[:, :], ones[:, 0:X], fill[:, :], 0.0, ALU.mult, ALU.add))
            ch.link(v.tensor_tensor(off[:, :], end[:, :], fill[:, :], ALU.subtract))
            ch.link(v.tensor_tensor(off[:, :], off[:, :], p_c[0:P, 0:X], ALU.add))
            ch.link(v.tensor_tensor(off[:, 1:X], off[:, 1:X], run[:, 0:X - 1, NT - 1], ALU.subtract))
            ch.link(v.tensor_tensor(run[:, :, :], run[:, :, :], both[:, :, :], ALU.subtract))
            ch.link(v.tensor_tensor(run[:, :, :], run[:, :, :], off[:, :].unsqueeze(2).to_broadcast([P, X, NT]), ALU.add))
            for k in range(2):
                ch.link(v.tensor_tensor(m1[:, :, :], pick[:, k], run[:, :, :].rearrange("p e t -> p t e"), ALU.mult))
                ch.link(v.reduce_sum(red[:, :], m1[:, :, :], axis=AX))
                last = v.tensor_copy(pos[:, k, :], red[:, :])
                ch.link(last)
            v.memset(half[:, 0:1], 0.0).then_inc(s_pos, 1)
            ch.link(v.tensor_tensor(blk_g[:, :, :], blk_f[:, :].unsqueeze(2).to_broadcast([1, BLOCKS, X]),
                                    end[0:1, :].unsqueeze(1).to_broadcast([1, BLOCKS, X]), ALU.is_ge))
            ch.link(v.reduce_sum(blk_f[:, :], blk_g[:, :, :], axis=AX))
            ch.link(v.tensor_scalar(blk_f[:, :], blk_f[:, :], float(X - 1), None, ALU.min))
            ch.link(v.tensor_copy(blk[:, :], blk_f[:, :]))

            def norm(i, first):
                for b in range(2):
                    t = 2 * i + b
                    if not first:
                        dve.wait_ge(s_sc[b], 32 * i)
                    v.tensor_scalar(xe[:, b, :], cols(xo, t), mv2[:, bass.ds(t, 1), 0], r2[:, bass.ds(t, 1)],
                                    ALU.subtract, ALU.mult).then_inc(s_xe, 1)
            loop2(dve, None, NT // 2, 0, norm)


def phase_experts(nc, phase, a, d, ident, blk):
    X = EXPERTS
    KH = HID // 128
    with phase("f") as (c, sb, ps, sm):
        w1 = sb("w1", [128, CH, X * HID])
        w2 = sb("w2", [128, KH, X * C])
        b1 = sb("b1", [128, X * HID])
        b2 = sb("b2", [128, X * C])
        ln = sb("ln", [16, 2, 128])
        lnt = sb("lnt", [128, 2, 16])
        shift = sb("shift", [128, 2, 128])
        xin = sb("xin", [128, 2, C])
        xt = sb("xt", [128, 2, C])
        hs = sb("hs", [128, 2, HID])
        ht = sb("ht", [128, HID])
        ys = sb("ys", [128, 2, C])
        p_x = ps("p_x")
        p_y = ps("p_y")
        p_h = [[ps(f"p_h{b}{q}") for q in range(2)] for b in range(2)]
        p_t = [ps(f"p_t{q}") for q in range(2)]
        (s_ln, s_w1, s_w2, s_b, s_lt, s_ltc, s_sh, s_bp, s_b1, s_scl, s_scv, s_xtp, s_xt, s_h, s_hb, s_ge, s_tp,
         s_ta, s_tv, s_y, s_ys) = (sm(n) for n in
            ("ln", "w1", "w2", "b", "lt", "ltc", "sh", "bp", "b1", "scl", "scv", "xtp", "xt", "h", "hb", "ge", "tp",
             "ta", "tv", "y", "ys"))
        s_x = [sm(f"x{b}") for b in range(2)]
        s_st = [sm(f"st{b}", swdge=True) for b in range(2)]
        block = c.enter_context(nc.Block())
        xg = d["xg"].rearrange("(t p) c -> p t c", p=128)
        yg = d["yg"].rearrange("(t p) c -> p t c", p=128)

        def expert(eng, t):
            return eng.value_load(blk[0:1, bass.ds(t, 1)], min_val=0, max_val=X - 1)

        @block.sync
        def _(sp):
            for j, n in enumerate(("g", "b")):
                sp.dma_start(ln[:, j, :], a[f"L0_ffn_ln_{n}"].rearrange("e (k p) -> (e k) p", p=128)).then_inc(s_ln, 16)
            for k in range(CH):
                sp.dma_start(w1[:, k, :].rearrange("p (e h) -> p e h", e=X),
                             a["L0_ffn_W1"][:, k * 128:(k + 1) * 128, :].rearrange("e p h -> p e h")).then_inc(s_w1, 16)
            sp.dma_start(b1[:, :], a["L0_ffn_b1"].rearrange("(o e) h -> o (e h)", o=1).to_broadcast([128, X * HID])).then_inc(s_b, 16)
            sp.dma_start(b2[:, :], a["L0_ffn_b2"].rearrange("(o e) h -> o (e h)", o=1).to_broadcast([128, X * C])).then_inc(s_b, 16)
            for e in range(X):
                sp.dma_start(w2[:, :, e * C:(e + 1) * C], a["L0_ffn_W2"][e].rearrange("(k p) c -> p k c", p=128)).then_inc(s_w2, 16)

            def load(t, b):
                sp.dma_start(xin[:, b, :], xg[:, bass.ds(t, 1), :].rearrange("p o c -> p (o c)")).then_inc(s_x[b], 16)

            def step(i, first):
                for b in range(2):
                    t = 2 * i + b
                    if not first:
                        sp.wait_ge(s_xtp, t - 1)
                    load(t, b)
            loop2(sp, None, BLOCKS // 2, 0, step)
            sp.wait_ge(s_xtp, BLOCKS - 1)
            load(BLOCKS, 0)

        @block.gpsimd
        def _(pool):
            def step(i, first):
                for b in range(2):
                    t = 2 * i + b
                    pool.wait_ge(s_ys, t + 1)
                    pool.dma_start(yg[:, bass.ds(t, 1), :].rearrange("p o c -> p (o c)"), ys[:, b, :]).then_inc(s_st[b], 16)
            loop2(pool, None, BLOCKS // 2, 0, step)
            for b in range(2):
                pool.wait_ge(s_st[b], 16 * (BLOCKS // 2))

        @block.tensor
        def _(pe):
            pe.wait_ge(s_ln, 32)
            for j in range(2):
                last = nc.tensor.transpose(p_x[:, j * 16:(j + 1) * 16], ln[:, j, :], ident[0:16, 0:16])
            last.then_inc(s_lt, 1)
            pe.wait_ge(s_w1, 32)
            for e in range(X):
                for k in range(CH):
                    pe.wait_ge(s_sh, CH * e + k + 1)
                    for q in range(2):
                        last = nc.tensor.matmul(p_h[e % 2][q][:, :], shift[:, k, :],
                                                w1[:, k, e * HID + q * 512:e * HID + (q + 1) * 512], start=k == 0, stop=k == CH - 1)
                    last.then_inc(s_bp, 1)
            pe.wait_ge(s_scl, X)
            pe.wait_ge(s_scv, X)
            pe.wait_ge(s_b1, X)

            def x_transposed(i, b):
                pe.wait_ge(s_x[b], 16 * (i + 1))
                for k in range(CH):
                    last = nc.tensor.transpose(p_x[:, k * 128:(k + 1) * 128], xin[:, b, k * 128:(k + 1) * 128], ident[:, :])
                last.then_inc(s_xtp, 1)

            def hidden(t, b):
                e = expert(pe, t)
                pe.wait_ge(s_xt, t + 1)
                for q in range(2):
                    for k in range(CH):
                        last = nc.tensor.matmul(p_h[b][q][:, :], xt[:, b, k * 128:(k + 1) * 128],
                                                w1[:, k, bass.ds(e * HID + q * 512, 512)], start=k == 0, stop=k == CH - 1)
                    last.then_inc(s_h, 1)

            def down(t, b, first):
                e = expert(pe, t)
                pe.wait_ge(s_ge, t + 1)
                if not first:
                    pe.wait_ge(s_ta, t)
                    pe.wait_ge(s_tv, t)
                for k in range(KH):
                    last = nc.tensor.transpose(p_t[k // 4][:, (k % 4) * 128:(k % 4 + 1) * 128],
                                               hs[:, b, k * 128:(k + 1) * 128], ident[:, :])
                last.then_inc(s_tp, 1)
                pe.wait_ge(s_ta, t + 1)
                pe.wait_ge(s_tv, t + 1)
                if not first:
                    pe.wait_ge(s_ys, t)
                for k in range(KH):
                    last = nc.tensor.matmul(p_y[:, 0:C], ht[:, k * 128:(k + 1) * 128], w2[:, k, bass.ds(e * C, C)],
                                            start=k == 0, stop=k == KH - 1)
                last.then_inc(s_y, 1)

            x_transposed(0, 0)

            def step(i, first):
                for b in range(2):
                    t = 2 * i + b
                    if not first:
                        pe.wait_ge(s_hb, t - 1)
                    hidden(t, b)
                    x_transposed(i + b, 1 - b)
                    if not (first and b == 0):
                        down(t - 1, 1 - b, first)
            pe.wait_ge(s_w2, 16 * X)
            loop2(pe, None, BLOCKS // 2, 0, step)
            down(BLOCKS - 1, 1, False)

        @block.scalar
        def _(act):
            act.wait_ge(s_ltc, 1)
            for e in range(X):
                act.wait_ge(s_bp, CH * (e + 1))
                nc.scalar.activation(w1[:, 0, e * HID:(e + 1) * HID], w1[:, 0, e * HID:(e + 1) * HID], ACT.Copy,
                                     scale=lnt[:, 0, CH * e:CH * e + 1]).then_inc(s_scl, 1)

            def x_copy(t, b):
                act.wait_ge(s_xtp, t + 1)
                nc.scalar.activation(xt[:, b, :], p_x[:, 0:C], ACT.Copy).then_inc(s_xt, 1)

            def h_copy(t):
                act.wait_ge(s_tp, t + 1)
                nc.scalar.activation(ht[:, 0:512], p_t[0][:, :], ACT.Copy).then_inc(s_ta, 1)

            act.wait_ge(s_b1, X)
            x_copy(0, 0)

            def step(i, first):
                for b in range(2):
                    t = 2 * i + b
                    x_copy(t + 1, 1 - b)
                    if not (first and b == 0):
                        if not (first and b == 1):
                            act.wait_ge(s_y, t - 1)
                        h_copy(t - 1)
                    act.wait_ge(s_hb, t + 1)
                    nc.scalar.activation(hs[:, b, :], hs[:, b, :], ACT.Gelu).then_inc(s_ge, 1)
            loop2(act, None, BLOCKS // 2, 0, step)
            act.wait_ge(s_y, BLOCKS - 1)
            h_copy(BLOCKS - 1)

        @block.vector
        def _(dve):
            v = nc.vector
            dve.wait_ge(s_lt, 1)
            v.tensor_copy(lnt[:, :, :], p_x[:, 0:32].rearrange("p (j r) -> p j r", j=2)).then_inc(s_ltc, 1)
            dve.wait_ge(s_ltc, 1)
            dve.wait_ge(s_b, 32)
            dve.wait_ge(s_w1, 32)
            for e in range(X):
                for k in range(CH):
                    if e > 0:
                        dve.wait_ge(s_bp, CH * (e - 1) + k + 1)
                    v.tensor_copy(shift[:, k, :], lnt[:, 1, CH * e + k:CH * e + k + 1].to_broadcast([128, 128])).then_inc(s_sh, 1)
                dve.wait_ge(s_bp, CH * (e + 1))
                for q in range(2):
                    sl = slice(e * HID + q * 512, e * HID + (q + 1) * 512)
                    last = v.tensor_tensor(b1[:, sl], p_h[e % 2][q][:, :], b1[:, sl], ALU.add)
                last.then_inc(s_b1, 1)
                sl = slice(e * HID, (e + 1) * HID)
                v.tensor_scalar(w1[:, 1, sl], w1[:, 1, sl], lnt[:, 0, CH * e + 1:CH * e + 2], None, ALU.mult).then_inc(s_scv, 1)

            def out_of(t, b, i, first):
                dve.wait_ge(s_tp, t + 1)
                if not first:
                    dve.wait_ge(s_y, t)
                v.tensor_copy(ht[:, 512:], p_t[1][:, :]).then_inc(s_tv, 1)
                e = expert(dve, t)
                dve.wait_ge(s_y, t + 1)
                if not first:
                    dve.wait_ge(s_st[b], 16 * i)
                v.tensor_tensor(ys[:, b, :], p_y[:, 0:C], b2[:, bass.ds(e * C, C)], ALU.add).then_inc(s_ys, 1)

            def step(i, first):
                for b in range(2):
                    t = 2 * i + b
                    e = expert(dve, t)
                    if not first:
                        dve.wait_ge(s_tp, t - 1)
                    for q in range(2):
                        dve.wait_ge(s_h, 2 * t + (q + 1))
                        last = v.tensor_tensor(hs[:, b, q * 512:(q + 1) * 512], p_h[b][q][:, :],
                                               b1[:, bass.ds(e * HID + q * 512, 512)], ALU.add)
                    last.then_inc(s_hb, 1)
                    if not (first and b == 0):
                        out_of(t - 1, 1 - b, i + b - 1 if not first else 0, first)
            loop2(dve, None, BLOCKS // 2, 0, step)
            out_of(BLOCKS - 1, 1, BLOCKS // 2 - 1, False)


def phase_combine(nc, phase, d, out, pos, gate):
    with phase("o") as (c, sb, ps, sm):
        x2 = sb("x2", [P, NT, C])
        ibuf = sb("ibuf", [P, 2, 2], I32)
        y = sb("y", [P, 2, 2, C])
        s_x, s_ib, s_one, s_out, s_done = (sm(n) for n in ("x", "ib", "one", "out", "done"))
        s_y = [sm(f"y{b}", swdge=True) for b in range(2)]
        block = c.enter_context(nc.Block())

        @block.sync
        def _(sp):
            sp.dma_start(x2[:, :, :], d["x2"].rearrange("(p t) c -> p t c", t=NT)).then_inc(s_x, 16)
            sp.wait_ge(s_out, NT)
            sp.dma_start(out.rearrange("(p t) c -> p t c", t=NT), x2[:, :, :]).then_inc(s_done, 16)
            sp.wait_ge(s_done, 16)

        @block.gpsimd
        def _(pool):
            def step(i, first):
                for b in range(2):
                    t = 2 * i + b
                    if not first:
                        pool.wait_ge(s_out, t - 1)
                    nc.gpsimd.tensor_copy(ibuf[:, b, :], pos[:, :, bass.ds(t, 1)].rearrange("p k o -> p (k o)")).then_inc(s_ib, 1)
                    pool.wait_ge(s_ib, t + 1)
                    pool.nop(nofuse=True)
                    for k in range(2):
                        nc.gpsimd.indirect_dma_start(out=y[:, b, k, :], out_offset=None, in_=d["yg"][:, :],
                                                     in_offset=bass.IndirectOffsetOnAxis(ap=ibuf[:, b, k:k + 1], axis=0)).then_inc(s_y[b], 16)
            loop2(pool, None, NT // 2, 0, step)

        @block.vector
        def _(dve):
            dve.wait_ge(s_x, 16)

            def step(i, first):
                for b in range(2):
                    t = 2 * i + b
                    row = x2[:, bass.ds(t, 1), :].rearrange("p o c -> p (o c)")
                    dve.wait_ge(s_y[b], 32 * (i + 1))
                    nc.vector.scalar_tensor_tensor(row, y[:, b, 0, :], gate[:, 0, bass.ds(t, 1)], row, ALU.mult, ALU.add).then_inc(s_one, 1)
                    dve.wait_ge(s_one, t + 1)
                    nc.vector.scalar_tensor_tensor(row, y[:, b, 1, :], gate[:, 1, bass.ds(t, 1)], row, ALU.mult, ALU.add).then_inc(s_out, 1)
            loop2(dve, None, NT // 2, 0, step)


_INS = ['x', 'src', 'dst', 'L0_gnn_Wb', 'L0_gnn_Wc', 'L0_gnn_bc', 'L0_gnn_conv_bias', 'L0_gnn_bn_gamma',
        'L0_gnn_bn_beta', 'L0_gnn_fc_W', 'L0_gnn_fc_b', 'L0_mix_w_qkv', 'L0_mix_b_qkv', 'L0_mix_kln_g',
        'L0_mix_kln_b', 'L0_mix_vln_g', 'L0_mix_vln_b', 'L0_mix_w1', 'L0_mix_b1', 'L0_mix_w2', 'L0_mix_b2',
        'L0_ffn_Wr', 'L0_ffn_br', 'L0_ffn_ln_g', 'L0_ffn_ln_b', 'L0_ffn_W1', 'L0_ffn_b1', 'L0_ffn_W2',
        'L0_ffn_b2']


def kernel(**inputs):
    import numpy as _np
    import concourse.bacc as _bacc
    from concourse import mybir as _mybir
    from concourse.bass_utils import run_bass_kernel_spmd as _run

    nc = _bacc.Bacc("TRN2", target_bir_lowering=False, num_devices=1)
    arrays, args = {}, {}
    for name in _INS:
        array = _np.ascontiguousarray(inputs[name])
        arrays[f"in_{name}"] = array
        args[name] = nc.dram_tensor(f"in_{name}", array.shape, _mybir.dt.from_np(array.dtype), kind="ExternalInput").ap()
    out = nc.dram_tensor("out_0", (N, C), _mybir.dt.float32, kind="ExternalOutput").ap()
    build(nc, args, out)
    result = _run(nc, [arrays], core_ids=[0])
    return result.results[0]["out_0"]
```

```python
import concourse.bass as bass
from concourse import mybir
from contextlib import ExitStack, contextmanager

FP32 = mybir.dt.float32
BF16 = mybir.dt.bfloat16
I32 = mybir.dt.int32
ALU = mybir.AluOpType
ACT = mybir.ActivationFunctionType
AX = mybir.AxisListType.X

N = 6250
E = 100000
C = 256
CH = C // 128
P = 125
NT = N // P
L = 3
HEADS = 8
BASES = 4
HC = C // HEADS
BW = BASES * HC
TW = L * BW
EPS = 1e-5
SLOPE = 0.01

NG = 64
SET = 4
SETS = 25
GROUPS = SET * SETS
NPAD = NG * GROUPS
HIST_A = NPAD // 128
SLOTS = 48
CHUNKS = SLOTS // 2
STEP = 2
BINS = 16
RUN_ROWS = 128 * 784
BIG = 3.0e38

EXPERTS = 8
HID = 1024
BLOCKS = -(-2 * N // 128) + EXPERTS
ROWS = BLOCKS * 128
KH = HID // 128
W2_LO = NT * C // (EXPERTS * C)


class Chain:

    def __init__(self, eng, sem):
        self.eng, self.sem, self.base, self.n = eng, sem, 0, 0

    def link(self, ins):
        self.mark(ins)
        self.wait()

    def mark(self, ins):
        ins.then_inc(self.sem, 1)
        self.n += 1

    def wait(self):
        self.eng.wait_ge(self.sem, self.base + self.n)

    @contextmanager
    def loop(self, i, first, per):
        n0 = self.n
        self.base = (i - first) * per
        yield
        assert self.n - n0 == per, (self.n - n0, per)
        self.n = n0
        self.base = 0

    def looped(self, steps, per):
        self.n += steps * per


def loop2(eng, chain, pairs, per, body):
    n0 = chain.n if chain else 0
    body(0, True)
    if chain:
        assert chain.n - n0 == per, ("links of a step", chain.n - n0, per)
    with eng.Fori(1, pairs) as i:
        if chain:
            with chain.loop(i, 1, per):
                body(i, False)
        else:
            body(i, False)
    if chain:
        chain.looped(pairs - 1, per)


def pipelined(eng, chain, pairs, head, tail, per, body):
    def at(i):
        return lambda b, k: 0 <= 2 * i + b + k < 2 * pairs
    for i in range(head):
        body(i, at(i))
    with eng.Fori(head, pairs - tail) as i:
        if chain:
            with chain.loop(i, head, per):
                body(i, lambda b, k: True)
        else:
            body(i, lambda b, k: True)
    if chain:
        chain.looped(pairs - head - tail, per)
    for i in range(pairs - tail, pairs):
        body(i, at(i))


def halves_to_mean_var(nc, ch, st, mv, half):
    dve = nc.vector
    ch.link(dve.tensor_tensor(half[:, :], st[:, :, 1], st[:, :, 4], ALU.subtract))
    ch.link(dve.tensor_scalar(half[:, :], half[:, :], 0.5, None, ALU.mult))
    ch.link(dve.tensor_tensor(mv[:, :, 0], st[:, :, 4], half[:, :], ALU.add))
    ch.link(dve.tensor_tensor(half[:, :], half[:, :], half[:, :], ALU.mult))
    ch.link(dve.tensor_tensor(mv[:, :, 1], st[:, :, 2], st[:, :, 5], ALU.add))
    ch.link(dve.scalar_tensor_tensor(mv[:, :, 1], mv[:, :, 1], 1.0 / C, half[:, :], ALU.mult, ALU.add))


def build(nc, a, out):
    def dram(name, shape, dt=FP32):
        return nc.dram_tensor(name, shape, dt, kind="Internal").ap()

    d = dict(
        order=dram("order_d", [NPAD, 4]), rank=dram("rank_d", [NPAD], I32), dinv=dram("dinv_d", [NPAD]),
        srcp=dram("srcp_d", [RUN_ROWS + 64], I32), runs=dram("runs_d", [RUN_ROWS, SLOTS], I32),
        tab=dram("tab_d", [NPAD, TW + 1]), xnt=dram("xnt_d", [NT, 128, CH * P]),
        agg=dram("agg_d", [NPAD, 4, TW]), ht=dram("ht_d", [NT, 128, 2 * L * P]),
        xg=dram("xg_d", [ROWS + 128, C]), yg=dram("yg_d", [ROWS, C]), x2=dram("x2_d", [N, C]),
    )

    top = ExitStack()

    @contextmanager
    def phase(tag, clear=False):
        with ExitStack() as c:
            sems = []

            def sb(name, shape, dt=FP32):
                return c.enter_context(nc.sbuf_tensor(f"{tag}_{name}", shape, dt))

            def ps(name, shape=(128, 512), dt=FP32):
                return c.enter_context(nc.psum_tensor(f"{tag}_{name}", list(shape), dt))

            def sm(name, swdge=False):
                if swdge:
                    return top.enter_context(nc.semaphore(f"{tag}_{name}"))
                sems.append(c.enter_context(nc.semaphore(f"{tag}_{name}")))
                return sems[-1]

            with ExitStack() as work:
                yield work, sb, ps, sm
            if clear:
                with nc.Block() as block:
                    @block.sync
                    def _(sp):
                        for s in sems:
                            sp.sem_clear(s)

    with top:
        def keep(stack, name, shape, dt=FP32):
            return stack.enter_context(nc.sbuf_tensor(name, shape, dt))

        ident = keep(top, "ident", [128, 128])
        pos = keep(top, "pos", [P, 2, NT], I32)
        gate = keep(top, "gate", [P, 2, NT])
        blk = keep(top, "blk", [1, BLOCKS], I32)
        with ExitStack() as nodes:
            x_mem = keep(nodes, "x_mem", [128, NT * C])
            x_sb = x_mem[0:P, :].rearrange("p (t c) -> p t c", c=C)
            xst = keep(nodes, "x_stats", [P, NT, 6])
            with ExitStack() as early:
                mv = keep(early, "mv", [P, NT, 2])
                rstd = keep(early, "rstd", [P, NT])
                kvbd = keep(early, "kvbd", [128, CH, 128])
                phase_histogram(nc, phase, a, d, ident)
                phase_nodes(nc, phase, a, d, ident, x_sb, mv, rstd, kvbd)
                phase_edges(nc, phase, a, d, ident)
                stats = keep(early, "bn_stats", [128, 2 * L, NT, 6])
                phase_conv(nc, phase, a, d, ident, stats)
                phase_mix(nc, phase, a, d, ident, x_sb, mv, rstd, kvbd, stats, xst)
            w1 = keep(nodes, "w1", [128, CH, EXPERTS * HID])
            b1 = keep(nodes, "b1", [128, EXPERTS * HID])
            w2_lo = x_mem[:, 0:W2_LO * EXPERTS * C].rearrange("p (k n) -> p k n", k=W2_LO)
            phase_route(nc, phase, a, d, ident, x_sb, xst, pos, gate, blk, w1, b1, w2_lo)
            phase_experts(nc, phase, a, d, ident, blk, w1, b1, w2_lo)
        phase_combine(nc, phase, d, out, pos, gate)


def phase_histogram(nc, phase, a, d, ident):
    COLS = E // P
    W = 16
    PAIRS = COLS // W // 2
    with phase("h", clear=True) as (c, sb, ps, sm):
        dst = sb("dst", [P, COLS], I32)
        hi_i = sb("hi_i", [P, COLS], I32)
        lo_i = sb("lo_i", [P, COLS], I32)
        hi = sb("hi", [P, COLS], BF16)
        lo = sb("lo", [P, COLS], BF16)
        iota_i = sb("iota_i", [P, 128], I32)
        iota = sb("iota", [P, 128], BF16)
        iota_f = sb("iota_f", [HIST_A, BINS])
        one_hi = sb("one_hi", [P, 2, W, HIST_A], BF16)
        one_lo = sb("one_lo", [P, 2, W, 128], BF16)
        zero_b = sb("zero_b", [P, 128], BF16)
        zero_i = sb("zero_i", [1, 512], I32)
        zero_f = sb("zero_f", [(NPAD - N) // 2, 2 * (TW + 1)])
        big = sb("big", [128, 2, TW])
        ones = sb("ones", [HIST_A, 128])
        below = sb("below", [HIST_A, HIST_A])
        cnt = sb("cnt", [HIST_A, 128])
        incl = sb("incl", [HIST_A, 128])
        deg = sb("deg", [HIST_A, 128])
        first = sb("first", [HIST_A, 128])
        bin_f = sb("bin_f", [HIST_A, 128])
        bin_i = sb("bin_i", [HIST_A, 128], I32)
        onehot = sb("onehot", [HIST_A, BINS, 128])
        run = sb("run", [HIST_A, BINS, 128])
        ones_w = sb("ones_w", [HIST_A, BINS * 128])
        bins = sb("bins", [HIST_A, BINS])
        lane = sb("lane", [HIST_A, BINS])
        off = sb("off", [HIST_A, BINS])
        rank = sb("rank", [HIST_A, 128])
        rank_i = sb("rank_i", [HIST_A, 128], I32)
        rank_t = sb("rank_t", [128, HIST_A], I32)
        node_i = sb("node_i", [128, HIST_A], I32)
        node_row = sb("node_row", [128, HIST_A, 4])
        p_cnt = ps("p_cnt")
        p_off = ps("p_off")
        p_bin = ps("p_bin")
        p_tr = ps("p_tr")
        s_dst, s_fill, s_pad, s_run, s_gp, s_dve = (sm(n) for n in
            ("dst", "fill", "pad", "run", "gp", "dve"))
        s_init = sm("init", swdge=True)
        s_one, s_used, s_cnt, s_tot, s_off, s_res, s_store, s_sqrt = (sm(n) for n in
            ("one", "used", "cnt", "tot", "off", "res", "store", "sqrt"))
        s_rank, s_row, s_lane, s_cum, s_tr, s_first = (sm(n) for n in ("rank", "row", "lane", "cum", "tr", "first"))
        block = c.enter_context(nc.Block())

        @block.sync
        def _(sp):
            sp.dma_start(dst[:, :], a["dst"].rearrange("(p k) -> p k", p=P)).then_inc(s_dst, 16)
            sp.dma_start(d["srcp"][1:E + 1].rearrange("(p k) -> p k", p=P),
                         a["src"].rearrange("(p k) -> p k", p=P)).then_inc(s_pad, 16)
            sp.wait_ge(s_fill, 1)
            sp.dma_start(d["srcp"][0:1].rearrange("(o k) -> o k", o=1), zero_i[0:1, 0:1]).then_inc(s_pad, 16)
            tail = RUN_ROWS + 64 - E - 1
            sp.dma_start(d["srcp"][E + 1:].rearrange("(o k) -> o k", o=1), zero_i[0:1, 0:tail]).then_inc(s_pad, 16)
            sp.wait_ge(s_pad, 48)
            runs_in = bass.AP(d["srcp"].tensor, 0, [[RUN_ROWS // 128, 128], [1, RUN_ROWS // 128], [1, SLOTS]])
            sp.dma_start(d["runs"].rearrange("(p r) s -> p r s", p=128), runs_in).then_inc(s_run, 16)
            sp.wait_ge(s_res, 1)
            sp.dma_start(d["dinv"].rearrange("(a b) -> a b", b=128), deg[:, :]).then_inc(s_store, 16)
            sp.wait_ge(s_rank, 1)
            sp.dma_start(d["rank"].rearrange("(a b) -> a b", b=128), rank_i[:, :]).then_inc(s_store, 16)
            sp.wait_ge(s_store, 32)
            sp.wait_ge(s_run, 16)

        @block.gpsimd
        def _(pool):
            nc.gpsimd.memset(zero_i[:, :], 0).then_inc(s_fill, 1)
            nc.gpsimd.iota(iota_i[:, :], pattern=[[1, 128]], base=0, channel_multiplier=0).then_inc(s_gp, 1)
            nc.gpsimd.iota(node_i[:, :], pattern=[[128, HIST_A]], base=0, channel_multiplier=1).then_inc(s_gp, 1)
            nc.gpsimd.memset(ident[:, :], 0.0).then_inc(s_gp, 1)
            nc.gpsimd.memset(below[:, :], 1.0).then_inc(s_gp, 1)
            pool.wait_ge(s_gp, 4)
            nc.gpsimd.affine_select(out=ident[:, :], in_=ident[:, :], compare_op=ALU.not_equal, fill=1.0,
                                    base=0, pattern=[[-1, 128]], channel_multiplier=1).then_inc(s_gp, 1)
            nc.gpsimd.affine_select(out=below[:, :], in_=below[:, :], compare_op=ALU.is_gt, fill=0.0,
                                    base=0, pattern=[[1, HIST_A]], channel_multiplier=-1).then_inc(s_gp, 1)
            nc.gpsimd.memset(zero_f[:, :], 0.0).then_inc(s_gp, 1)
            nc.gpsimd.memset(big[:, 0, :], 0.0).then_inc(s_gp, 1)
            nc.gpsimd.memset(big[:, 1, :], -BIG).then_inc(s_gp, 1)
            pool.wait_ge(s_gp, 9)
            pool.dma_start(d["tab"][N:NPAD, :].rearrange("(p r) w -> p (r w)", r=2), zero_f[:, :]).then_inc(s_init, 16)
            for g in range(NPAD // 128):
                for half in range(2):
                    for k in range(2):
                        pool.dma_start(d["agg"][g * 128:(g + 1) * 128, 2 * half + k, :],
                                       big[:, half, :]).then_inc(s_init, 16)
            pool.wait_ge(s_row, 1)
            for t in range(HIST_A):
                nc.gpsimd.indirect_dma_start(
                    out=d["order"][:, :], out_offset=bass.IndirectOffsetOnAxis(ap=rank_t[:, t:t + 1], axis=0),
                    in_=node_row[:, t, :], in_offset=None).then_inc(s_init, 16)
            pool.wait_ge(s_init, 16 * (1 + 4 * (NPAD // 128) + HIST_A))

        @block.vector
        def _(dve):
            ch = Chain(dve, s_dve)
            nc.vector.memset(ones[:, :], 1.0)
            nc.vector.memset(zero_b[:, :], 0.0)
            dve.wait_ge(s_gp, 2)
            nc.vector.tensor_copy(iota[:, :], iota_i[:, :])
            nc.vector.tensor_copy(iota_f[:, :], iota_i[0:HIST_A, 0:BINS])
            dve.wait_ge(s_dst, 16)
            nc.vector.tensor_single_scalar(hi_i[:, :], dst[:, :], 7, op=ALU.logical_shift_right)
            ch.link(nc.vector.tensor_single_scalar(lo_i[:, :], dst[:, :], 127, op=ALU.bitwise_and))
            nc.vector.tensor_copy(hi[:, :], hi_i[:, :])
            ch.link(nc.vector.tensor_copy(lo[:, :], lo_i[:, :]))

            def step(i, first_step):
                for b in range(2):
                    t = 2 * i + b
                    if not first_step:
                        dve.wait_ge(s_used, t - 1)
                    cols = bass.ds(t * W, W)
                    nc.vector.tensor_tensor(
                        one_hi[:, b], hi[:, cols].unsqueeze(2).to_broadcast([P, W, HIST_A]),
                        iota[:, 0:HIST_A].unsqueeze(1).to_broadcast([P, W, HIST_A]), ALU.is_equal)
                    nc.vector.tensor_tensor(
                        one_lo[:, b], lo[:, cols].unsqueeze(2).to_broadcast([P, W, 128]),
                        iota[:, :].unsqueeze(1).to_broadcast([P, W, 128]), ALU.is_equal).then_inc(s_one, 1)
            loop2(dve, None, PAIRS, 0, step)
            dve.wait_ge(s_cnt, 1)
            ch.link(nc.vector.tensor_copy(cnt[:, :], p_cnt[0:HIST_A, 0:128]))
            nc.vector.tensor_tensor_scan(incl[:, :], ones[:, :], cnt[:, :], 0.0, ALU.mult, ALU.add).then_inc(s_tot, 1)
            ch.link(nc.vector.tensor_scalar_add(deg[:, :], cnt[:, :], 1.0))
            nc.vector.reciprocal(deg[:, :], deg[:, :]).then_inc(s_sqrt, 1)
            dve.wait_ge(s_tot, 1)
            ch.link(nc.vector.tensor_tensor(first[:, :], incl[:, :], cnt[:, :], ALU.subtract))
            dve.wait_ge(s_off, 1)
            nc.vector.tensor_scalar(first[:, :], first[:, :], p_off[0:HIST_A, 0:1], None, ALU.add).then_inc(s_first, 1)
            v = nc.vector
            v.memset(ones_w[:, :], 1.0)
            ch.link(v.tensor_scalar(bin_f[:, :], cnt[:, :], 2.0 * STEP, None, ALU.add))
            ch.link(v.tensor_copy(bin_i[:, :], bin_f[:, :]))
            ch.link(v.tensor_single_scalar(bin_i[:, :], bin_i[:, :], 2, op=ALU.logical_shift_right))
            ch.link(v.tensor_copy(bin_f[:, :], bin_i[:, :]))
            ch.link(v.tensor_scalar(bin_f[:, :], bin_f[:, :], float(BINS), -1.0, ALU.min, ALU.mult))
            ch.link(v.tensor_scalar(bin_f[:, :], bin_f[:, :], float(BINS), None, ALU.add))
            ids = iota_f[:, 0:BINS].unsqueeze(2).to_broadcast([HIST_A, BINS, 128])
            ch.link(v.tensor_tensor(onehot[:, :, :], bin_f[:, :].unsqueeze(1).to_broadcast([HIST_A, BINS, 128]), ids, ALU.is_equal))
            ch.link(v.tensor_tensor_scan(run[:, :, :].rearrange("a e b -> a (e b)"), ones_w[:, :],
                                         onehot[:, :, :].rearrange("a e b -> a (e b)"), 0.0, ALU.mult, ALU.add))
            v.tensor_copy(lane[:, 0:1], run[:, 0:1, 127])
            v.tensor_tensor(lane[:, 1:], run[:, 1:, 127], run[:, 0:BINS - 1, 127], ALU.subtract).then_inc(s_lane, 1)
            dve.wait_ge(s_cum, 1)
            ch.link(v.tensor_copy(bins[:, :], p_bin[0:HIST_A, BINS:2 * BINS]))
            ch.link(v.tensor_tensor_scan(off[:, :], ones[:, 0:BINS], bins[:, :], 0.0, ALU.mult, ALU.add))
            ch.link(v.tensor_tensor(off[:, :], off[:, :], bins[:, :], ALU.subtract))
            ch.link(v.tensor_tensor(off[:, :], off[:, :], p_bin[0:HIST_A, 0:BINS], ALU.add))
            ch.link(v.tensor_tensor(off[:, 1:], off[:, 1:], run[:, 0:BINS - 1, 127], ALU.subtract))
            ch.link(v.tensor_tensor(run[:, :, :], run[:, :, :], onehot[:, :, :], ALU.subtract))
            ch.link(v.tensor_tensor(run[:, :, :], run[:, :, :], off[:, :].unsqueeze(2).to_broadcast([HIST_A, BINS, 128]), ALU.add))
            ch.link(v.tensor_tensor(run[:, :, :], run[:, :, :], onehot[:, :, :], ALU.mult))
            ch.link(v.reduce_sum(rank[:, :], run[:, :, :].rearrange("a e b -> a b e"), axis=AX))
            v.tensor_copy(rank_i[:, :], rank[:, :]).then_inc(s_rank, 1)
            dve.wait_ge(s_tr, 1)
            v.tensor_copy(rank_t[:, :], p_tr[:, 0:HIST_A])
            v.tensor_copy(node_row[:, :, 0], p_tr[:, 64:64 + HIST_A])
            v.tensor_copy(node_row[:, :, 1], p_tr[:, 128:128 + HIST_A])
            v.tensor_copy(node_row[:, :, 3], node_i[:, :])
            v.tensor_copy(node_row[:, :, 2], node_i[:, :]).then_inc(s_row, 1)

        @block.scalar
        def _(act):
            act.wait_ge(s_sqrt, 1)
            nc.scalar.activation(deg[:, :], deg[:, :], ACT.Sqrt).then_inc(s_res, 1)

        @block.tensor
        def _(pe):
            def step(i, first_step):
                for b in range(2):
                    t = 2 * i + b
                    pe.wait_ge(s_one, t + 1)
                    for w in range(W):
                        last = nc.tensor.matmul(p_cnt[0:HIST_A, 0:128], one_hi[:, b, w, :], one_lo[:, b, w, :],
                                                start=first_step and b == 0 and w == 0, stop=False)
                    last.then_inc(s_used, 1)
            loop2(pe, None, PAIRS, 0, step)
            nc.tensor.matmul(p_cnt[0:HIST_A, 0:128], zero_b[:, 0:HIST_A], zero_b[:, :], start=False,
                             stop=True).then_inc(s_cnt, 1)
            pe.wait_ge(s_tot, 1)
            pe.wait_ge(s_gp, 6)
            nc.tensor.matmul(p_off[0:HIST_A, 0:1], below[:, :], incl[:, 127:128], start=True,
                             stop=True).then_inc(s_off, 1)
            pe.wait_ge(s_lane, 1)
            nc.tensor.matmul(p_bin[0:HIST_A, 0:BINS], below[:, :], lane[:, :], start=True, stop=True)
            nc.tensor.matmul(p_bin[0:HIST_A, BINS:2 * BINS], ones[:, 0:HIST_A], lane[:, :], start=True, stop=True).then_inc(s_cum, 1)
            pe.wait_ge(s_first, 1)
            nc.tensor.transpose(p_tr[:, 64:64 + HIST_A], cnt[:, :], ident[0:HIST_A, 0:HIST_A])
            nc.tensor.transpose(p_tr[:, 128:128 + HIST_A], first[:, :], ident[0:HIST_A, 0:HIST_A])
            pe.wait_ge(s_rank, 1)
            nc.tensor.transpose(p_tr[:, 0:HIST_A], rank[:, :], ident[0:HIST_A, 0:HIST_A]).then_inc(s_tr, 1)


def phase_nodes(nc, phase, a, d, ident, x_sb, mv, rstd, kvbd):
    KV = 2 * C
    G = 2 * HEADS
    with phase("n", clear=True) as (c, sb, ps, sm):
        wb = sb("wb", [128, CH, L, BW])
        wqkv = sb("wqkv", [128, CH, 3 * C])
        b_kv = sb("b_kv", [P, 3 * C])
        ln_g = sb("ln_g", [P, 2, HC])
        ln_b = sb("ln_b", [P, 2, HC])
        dinv = sb("dinv", [P, NT])
        st = sb("st", [P, NT, 6])
        std = sb("std", [P, NT])
        half = sb("half", [P, NT])
        xn = sb("xn", [P, 2, C])
        xt = sb("xt", [128, 2, CH * P])
        rows = sb("rows", [P, 2, TW + 1])
        kv = sb("kv", [P, 2, KV])
        sq = sb("sq", [P, 2, KV])
        gs = sb("gs", [P, 2, G])
        gv = sb("gv", [P, 2, G])
        gd = sb("gd", [P, 2, G])
        kvg = sb("kvg", [P, 2, KV])
        kn = sb("kn", [P, 2, 2, C])
        zero = sb("zero", [P, C])
        p_t = [ps(f"p_t{b}") for b in range(2)]
        p_b = [ps(f"p_b{b}") for b in range(2)]
        p_k = [ps(f"p_k{b}") for b in range(2)]
        p_kv = ps("p_kv")
        s_x, s_w, s_bias, s_dve, s_act, s_pool = (sm(n) for n in ("x", "w", "bias", "dve", "act", "pool"))
        s_var, s_std, s_xn, s_tp, s_xt, s_bp, s_kp, s_row = (sm(n) for n in
            ("var", "std", "xn", "tp", "xt", "bp", "kp", "row"))
        s_sq, s_cen, s_gd, s_gstd, s_nrm, s_kn, s_kva, s_zero, s_din, s_end, s_kvd = (sm(n) for n in
            ("sq", "cen", "gd", "gstd", "nrm", "kn", "kva", "zero", "din", "end", "kvd"))
        s_tabw = [sm(f"tabw{b}") for b in range(2)]
        s_xtw = [sm(f"xtw{b}") for b in range(2)]
        block = c.enter_context(nc.Block())
        tab = d["tab"][0:N, :].rearrange("(p t) w -> p t w", t=NT)

        @block.sync
        def _(sp):
            sp.dma_start(x_sb[:, :, :], a["x"].rearrange("(p t) c -> p t c", t=NT)).then_inc(s_x, 16)
            for k in range(CH):
                sp.dma_start(wb[:, k], a["L0_gnn_Wb"][:, k * 128:(k + 1) * 128, :].rearrange("l p w -> p l w")).then_inc(s_w, 16)
                sp.dma_start(wqkv[:, k], a["L0_mix_w_qkv"][k * 128:(k + 1) * 128, :]).then_inc(s_w, 16)
            sp.dma_start(b_kv[:, :], a["L0_mix_b_qkv"].rearrange("(o n) -> o n", o=1).to_broadcast([P, 3 * C])).then_inc(s_bias, 16)
            for j, n in enumerate("kv"):
                sp.dma_start(ln_g[:, j, :], a[f"L0_mix_{n}ln_g"].rearrange("(o n) -> o n", o=1).to_broadcast([P, HC])).then_inc(s_bias, 16)
                sp.dma_start(ln_b[:, j, :], a[f"L0_mix_{n}ln_b"].rearrange("(o n) -> o n", o=1).to_broadcast([P, HC])).then_inc(s_bias, 16)
            sp.dma_start(dinv[:, :], d["dinv"][0:N].rearrange("(p t) -> p t", t=NT)).then_inc(s_din, 16)

            def step(i, first_step):
                for b in range(2):
                    t = 2 * i + b
                    sp.wait_ge(s_xt, t + 1)
                    sp.dma_start(d["xnt"][bass.ds(t, 1)].rearrange("o p c -> (o p) c"), xt[:, b]).then_inc(s_xtw[b], 16)
                    sp.wait_ge(s_row, t + 1)
                    sp.dma_start(tab[:, bass.ds(t, 1), :].rearrange("p o w -> p (o w)"), rows[:, b]).then_inc(s_tabw[b], 16)
            loop2(sp, None, NT // 2, 0, step)
            for b in range(2):
                sp.wait_ge(s_xtw[b], 16 * (NT // 2))
                sp.wait_ge(s_tabw[b], 16 * (NT // 2))

        @block.vector
        def _(dve):
            ch = Chain(dve, s_dve)
            nc.vector.memset(zero[:, :], 0.0)
            nc.vector.memset(kn[:, :, :, :], 0.0).then_inc(s_zero, 1)
            dve.wait_ge(s_x, 16)
            with dve.Fori(0, NT) as t:
                nc.vector.bn_stats(st[:, bass.ds(t, 1), :].rearrange("p o s -> p (o s)"),
                                   x_sb[:, bass.ds(t, 1), :].rearrange("p o c -> p (o c)"))
            dve.drain()
            halves_to_mean_var(nc, ch, st, mv, half)
            nc.vector.tensor_scalar_add(std[:, :], mv[:, :, 1], EPS).then_inc(s_var, 1)
            dve.wait_ge(s_std, 1)
            ch.link(nc.vector.reciprocal(rstd[:, :], std[:, :]))
            dve.wait_ge(s_bias, 80)
            dve.wait_ge(s_din, 16)

            def grouped(t3):
                return t3.rearrange("p (g c) -> p g c", c=HC)

            def spread(t2):
                return t2.unsqueeze(2).to_broadcast([P, G, HC])

            def normalise(t, b, first):
                if not first:
                    dve.wait_ge(s_tp, t - 1)
                nc.vector.tensor_scalar(xn[:, b, :], x_sb[:, bass.ds(t, 1), :].rearrange("p o c -> p (o c)"),
                                        mv[:, bass.ds(t, 1), 0], rstd[:, bass.ds(t, 1)], ALU.subtract,
                                        ALU.mult).then_inc(s_xn, 1)

            def centre(t, b, first):
                dve.wait_ge(s_kp, t + 1)
                if not first:
                    dve.wait_ge(s_nrm, t - 1)
                bias = b_kv[:, :].rearrange("p (h s) -> p h s", s=3 * HC)[:, :, HC:]
                ch.link(nc.vector.tensor_tensor(kv[:, b, :].rearrange("p (h s) -> p h s", s=2 * HC),
                                                p_k[b][0:P, :].rearrange("p (h s) -> p h s", s=2 * HC), bias, ALU.add))
                ch.link(nc.vector.reduce_sum(gs[:, b, :], grouped(kv[:, b, :]), axis=AX))
                ch.link(nc.vector.tensor_scalar(gs[:, b, :], gs[:, b, :], 1.0 / HC, None, ALU.mult))
                nc.vector.tensor_tensor(grouped(kv[:, b, :]), grouped(kv[:, b, :]), spread(gs[:, b, :]),
                                        ALU.subtract).then_inc(s_cen, 1)

            def variance(t, b):
                dve.wait_ge(s_sq, t + 1)
                ch.link(nc.vector.reduce_sum(gv[:, b, :], grouped(sq[:, b, :]), axis=AX))
                nc.vector.tensor_scalar(gv[:, b, :], gv[:, b, :], 1.0 / HC, EPS, ALU.mult, ALU.add).then_inc(s_gd, 1)

            def scale(t, b, first):
                dve.wait_ge(s_gstd, t + 1)
                if not first:
                    dve.wait_ge(s_kn, t - 1)
                ch.link(nc.vector.reciprocal(gd[:, b, :], gv[:, b, :]))
                nc.vector.tensor_tensor(grouped(kvg[:, b, :]), grouped(kv[:, b, :]), spread(gd[:, b, :]),
                                        ALU.mult).then_inc(s_nrm, 1)

            normalise(0, 0, True)
            normalise(1, 1, True)

            def step(i, has):
                for b in range(2):
                    t = 2 * i + b
                    if has(b, -2):
                        scale(t - 2, b, not has(b, -4))
                    if has(b, -1):
                        variance(t - 1, 1 - b)
                    if has(b, 2):
                        normalise(t + 2, b, False)
                    centre(t, b, not has(b, -2))
            pipelined(dve, ch, NT // 2, 2, 1, 2 * 5, step)
            scale(NT - 2, 0, False)
            variance(NT - 1, 1)
            scale(NT - 1, 1, False)
            nc.vector.memset(kvbd[:, :, :], 0.0).then_inc(s_kvd, 1)
            dve.wait_ge(s_kvd, 1)
            dve.wait_ge(s_end, 1)
            for h in range(CH):
                for q in range(4):
                    r = slice(32 * q, 32 * q + 32)
                    nc.vector.tensor_scalar(kvbd[r, h, r], p_kv[r, h * 128 + 32 * q:h * 128 + 32 * q + 32],
                                            1.0 / N, None, ALU.mult)

        @block.gpsimd
        def _(pool):
            pool.wait_ge(s_zero, 1)
            pool.wait_ge(s_bias, 80)

            def both(t2):
                return t2.unsqueeze(1).to_broadcast([P, HEADS, HC])

            def step(i, first):
                for b in range(2):
                    t = 2 * i + b
                    pool.wait_ge(s_nrm, t + 1)
                    if not first:
                        pool.wait_ge(s_kva, t - 1)
                    src = kvg[:, b, :].rearrange("p (h s c) -> p h s c", s=2, c=HC)
                    for j in range(2):
                        last = nc.gpsimd.tensor_tensor(src[:, :, j, :], src[:, :, j, :], both(ln_g[:, j, :]), ALU.mult)
                    last.then_inc(s_pool, 1)
                    pool.wait_ge(s_pool, t + 1)
                    for j in range(2):
                        last = nc.gpsimd.tensor_tensor(kn[:, b, j, :].rearrange("p (h c) -> p h c", c=HC),
                                                       src[:, :, j, :], both(ln_b[:, j, :]), ALU.add)
                    last.then_inc(s_kn, 1)
            loop2(pool, None, NT // 2, 0, step)

        @block.scalar
        def _(act):
            act.wait_ge(s_var, 1)
            nc.scalar.activation(std[:, :], std[:, :], ACT.Sqrt).then_inc(s_std, 1)

            def transposed(t, b, i, first):
                act.wait_ge(s_tp, t + 1)
                if not first:
                    act.wait_ge(s_xtw[b], 16 * i)
                    act.wait_ge(s_kp, t - 1)
                nc.scalar.activation(xt[:, b, :], p_t[b][:, 0:CH * P], ACT.Copy).then_inc(s_xt, 1)

            act.wait_ge(s_din, 16)
            transposed(0, 0, 0, True)

            def step(i, has):
                for b in range(2):
                    t = 2 * i + b
                    if has(b, 1):
                        transposed(t + 1, 1 - b, i + b, not has(b, -1))
                    act.wait_ge(s_bp, t + 1)
                    if has(b, -2):
                        act.wait_ge(s_tabw[b], 16 * i)
                    nc.scalar.activation(rows[:, b, 0:TW], p_b[b][0:P, 0:TW], ACT.Copy)
                    nc.scalar.activation(rows[:, b, TW:TW + 1], dinv[:, bass.ds(t, 1)], ACT.Copy).then_inc(s_row, 1)
                    if has(b, -1):
                        act.wait_ge(s_gd, t)
                        nc.scalar.activation(gv[:, 1 - b, :], gv[:, 1 - b, :], ACT.Sqrt).then_inc(s_gstd, 1)
                    act.wait_ge(s_cen, t + 1)
                    if has(b, -2):
                        act.wait_ge(s_gd, t - 1)
                    nc.scalar.activation(sq[:, b, :], kv[:, b, :], ACT.Square).then_inc(s_sq, 1)
            pipelined(act, None, NT // 2, 1, 1, 0, step)
            act.wait_ge(s_gd, NT)
            nc.scalar.activation(gv[:, 1, :], gv[:, 1, :], ACT.Sqrt).then_inc(s_gstd, 1)

        @block.tensor
        def _(pe):
            pe.wait_ge(s_w, 64)
            pe.wait_ge(s_zero, 1)
            nc.tensor.matmul(p_kv[:, 0:C], zero[:, 0:128], zero[:, :], start=True, stop=False)

            def kv_sum(b):
                for h in range(CH):
                    last = nc.tensor.matmul(p_kv[:, h * 128:(h + 1) * 128], kn[:, b, 0, h * 128:(h + 1) * 128],
                                            kn[:, b, 1, h * 128:(h + 1) * 128], start=False, stop=False)
                return last

            def transposes(t, b, first):
                pe.wait_ge(s_xn, t + 1)
                if not first:
                    pe.wait_ge(s_xt, t - 1)
                for k in range(CH):
                    last = nc.tensor.transpose(p_t[b][:, k * P:(k + 1) * P], xn[:, b, k * 128:(k + 1) * 128], ident[0:P, 0:P])
                last.then_inc(s_tp, 1)

            transposes(0, 0, True)

            def step(i, has):
                for b in range(2):
                    t = 2 * i + b
                    if has(b, 1):
                        transposes(t + 1, 1 - b, not has(b, -1))
                    pe.wait_ge(s_xt, t + 1)
                    if has(b, -2):
                        pe.wait_ge(s_row, t - 1)
                        pe.wait_ge(s_cen, t - 1)
                    for k in range(CH):
                        last = nc.tensor.matmul(p_b[b][0:P, 0:TW], xt[:, b, k * P:(k + 1) * P],
                                                wb[:, k].rearrange("p l w -> p (l w)"), start=k == 0, stop=k == CH - 1)
                    last.then_inc(s_bp, 1)
                    for k in range(CH):
                        rhs = wqkv[:, k, :].rearrange("p (h s) -> p h s", s=3 * HC)[:, :, HC:]
                        last = nc.tensor.matmul(p_k[b][0:P, :].rearrange("p (h s) -> p h s", s=2 * HC),
                                                xt[:, b, k * P:(k + 1) * P], rhs, start=k == 0, stop=k == CH - 1)
                    last.then_inc(s_kp, 1)
                    if has(b, -3):
                        pe.wait_ge(s_kn, t - 2)
                        kv_sum(1 - b).then_inc(s_kva, 1)
            pipelined(pe, None, NT // 2, 2, 1, 0, step)
            for t in range(NT - 3, NT):
                pe.wait_ge(s_kn, t + 1)
                kv_sum(t % 2).then_inc(s_kva, 1)
            nc.tensor.matmul(p_kv[:, 0:C], zero[:, 0:128], zero[:, :], start=False, stop=True).then_inc(s_end, 1)


def phase_edges(nc, phase, a, d, ident):
    COLS = GROUPS * CHUNKS
    CPI = SET * STEP
    with phase("e", clear=True) as (c, sb, ps, sm):
        raw = sb("raw", [GROUPS, NG, 4])
        two = sb("two", [GROUPS, 3, 2, NG])
        most_in = sb("most_in", [SETS, SET * NG, 4])
        most = sb("most", [SETS, 1])
        cnt = sb("cnt", [128, GROUPS])
        start = sb("start", [128, GROUPS])
        start_c = sb("start_c", [128, GROUPS])
        start_i = sb("start_i", [128, GROUPS], I32)
        own = sb("own", [128, GROUPS])
        slot_i = sb("slot_i", [128, CHUNKS], I32)
        slot = sb("slot", [128, CHUNKS])
        not_own = sb("not_own", [128, CHUNKS])
        half = sb("half", [128, 1])
        runs = sb("runs", [128, GROUPS, SLOTS], I32)
        valid = sb("valid", [128, COLS])
        take = sb("take", [128, COLS])
        idx = sb("idx", [128, GROUPS, CHUNKS], I32)
        row = sb("row", [1, SETS])
        row_c = sb("row_c", [1, SETS])
        one = sb("one", [1, SETS])
        iters_i = sb("iters_i", [1, SETS], I32)
        iters = sb("iters", [1, SETS])
        upto = sb("upto", [1, SETS])
        base_i = sb("base_i", [1, SETS], I32)
        carry = sb("carry", [1, 1])
        top = sb("top", [1, 4])
        pass_i = sb("pass_i", [1, 1], I32)
        e2 = sb("e2", [128, NG])
        zero_b = sb("zero_b", [128, TW], BF16)
        ibuf = sb("ibuf", [128, STEP, SET], I32)
        g = sb("g", [128, CPI, TW + 1])
        dg = sb("dg", [128, CPI, 128])
        sum_in = sb("sum_in", [128, SET, TW])
        max_in = sb("max_in", [128, SET, TW])
        acc = sb("acc", [128, SET, TW])
        sum_out = sb("sum_out", [128, SET, TW])
        max_out = sb("max_out", [128, SET, TW])
        p_s = [ps(f"p_s{q}") for q in range(SET)]
        p_tr = ps("p_tr")
        p_row = ps("p_row")
        (s_in, s_dve, s_gp, s_tr, s_two, s_start, s_table, s_npass, s_e2, s_act, s_acc0, s_stored) = (sm(n) for n in
            ("in", "dve", "gp", "tr", "two", "start", "table", "npass", "e2", "act", "acc0", "stored"))
        s_ib, s_pe, s_max, s_dg, s_set, s_ev, s_acc, s_pass, s_sum_ld, s_max_ld, s_st, s_sum_used = (sm(n) for n in
            ("ib", "pe", "max", "dg", "set", "ev", "acc", "pass", "sum_ld", "max_ld", "st", "sum_used"))
        s_runs = sm("runs", swdge=True)
        s_g = [sm(f"g{j}", swdge=True) for j in range(CPI)]
        block = c.enter_context(nc.Block())

        def passes(eng):
            eng.wait_ge(s_npass, 1)
            return eng.value_load(pass_i[0:1, 0:1], min_val=1, max_val=E // SLOTS + 2)

        def set_iters(eng, t):
            n = eng.value_load(iters_i[0:1, bass.ds(t, 1)], min_val=1, max_val=CHUNKS // STEP)
            first = eng.value_load(base_i[0:1, bass.ds(t, 1)], min_val=0, max_val=1 << 19)
            return n, first

        @block.sync
        def _(sp):
            sp.dma_start(raw[:, :, :], d["order"].rearrange("(g l) c -> g l c", l=NG)).then_inc(s_in, 16)
            sp.dma_start(most_in[:, :, :], d["order"].rearrange("(s l) c -> s l c", l=SET * NG)).then_inc(s_in, 16)

            def part(t, r):
                return d["agg"].rearrange("(s q l) r w -> l s q r w", q=SET, l=NG)[:, bass.ds(t, 1), :, r, :].rearrange("l o q w -> l (o q) w")

            def halves(t, buf, r, sem, load):
                for h in range(2):
                    mem = buf[h * NG:(h + 1) * NG, :, :]
                    if load:
                        sp.dma_start(mem, part(t, r + h)).then_inc(sem, 16)
                    else:
                        sp.dma_start(part(t, r + h), mem).then_inc(sem, 16)

            def load(t):
                halves(t, sum_in, 0, s_sum_ld, True)
                halves(t, max_in, 2, s_max_ld, True)

            def store(t, k):
                sp.wait_ge(s_ev, k + 2)
                halves(t, sum_out, 0, s_st, False)
                sp.wait_ge(s_acc, k + 1)
                halves(t, max_out, 2, s_st, False)
                sp.wait_ge(s_st, 64 * (k + 1))
                sp.nop(nofuse=True)
                sp.sem_inc(s_stored, 1)

            sp.sem_inc(s_stored, 1)
            n_pass = passes(sp)
            with sp.Fori(0, n_pass) as p:
                load(0)
                with sp.Fori(0, SETS - 1) as t:
                    k = p * SETS + t
                    sp.wait_ge(s_sum_used, k + 1)
                    sp.wait_ge(s_acc0, k + 1)
                    load(t + 1)
                    store(t, k)
                store(SETS - 1, p * SETS + (SETS - 1))
                sp.sem_inc(s_pass, 1)

        @block.gpsimd
        def _(pool):
            nc.gpsimd.memset(half[0:NG, :], 0.0).then_inc(s_gp, 1)
            nc.gpsimd.memset(half[NG:128, :], 1.0).then_inc(s_gp, 1)
            for h in range(2):
                nc.gpsimd.iota(slot_i[h * NG:(h + 1) * NG, :], pattern=[[2, CHUNKS]], base=h, channel_multiplier=0).then_inc(s_gp, 1)
            n_pass = passes(pool)
            with pool.Fori(0, n_pass) as p:
                pool.wait_ge(s_start, p + 1)
                pool.nop(nofuse=True)
                for t in range(GROUPS):
                    nc.gpsimd.indirect_dma_start(
                        out=runs[:, t, :], out_offset=None, in_=d["runs"][:, :],
                        in_offset=bass.IndirectOffsetOnAxis(ap=start_i[:, t:t + 1], axis=0)).then_inc(s_runs, 16)
                pool.wait_ge(s_table, p + 1)
                pool.nop(nofuse=True)
                with pool.Fori(0, SETS) as t:
                    n, first = set_iters(pool, t)
                    with pool.Fori(0, n) as i:
                        it = first + i
                        for j in range(STEP):
                            pool.wait_ge(s_pe, it * CPI + SET * (j + 1))
                            pool.wait_ge(s_max, it * CPI + SET * (j + 1))
                            cols = idx[:, bass.ds(t * SET, SET), bass.ds(i * STEP + j, 1)].rearrange("p q o -> p (q o)")
                            nc.gpsimd.tensor_copy(ibuf[:, j, :], cols).then_inc(s_ib, 1)
                            pool.wait_ge(s_ib, it * STEP + (j + 1))
                            pool.nop(nofuse=True)
                            for q in range(SET):
                                x = j * SET + q
                                nc.gpsimd.indirect_dma_start(
                                    out=g[:, x, :], out_offset=None, in_=d["tab"][:, :],
                                    in_offset=bass.IndirectOffsetOnAxis(ap=ibuf[:, j, q:q + 1], axis=0)).then_inc(s_g[x], 16)

        @block.vector
        def _(dve):
            ch = Chain(dve, s_dve)
            v = nc.vector
            dve.sem_inc(s_max, CPI)
            v.memset(one[:, :], 1.0)
            v.memset(zero_b[:, :], 0.0)
            v.memset(carry[:, :], 0.0)
            for h in range(2):
                lanes = slice(h * NG, (h + 1) * NG)
                last = v.tensor_copy(e2[lanes, :], ident[lanes, lanes])
            last.then_inc(s_e2, 1)
            dve.wait_ge(s_in, 32)
            v.reduce_max(most[:, :], most_in[:, :, 0], axis=AX)
            for k in range(3):
                for h in range(2):
                    last = v.tensor_copy(two[:, k, h, :], raw[:, :, k])
            last.then_inc(s_two, 1)
            dve.wait_ge(s_gp, 4)
            ch.link(v.tensor_copy(slot[:, :], slot_i[:, :]))
            dve.wait_ge(s_tr, 1)
            v.tensor_copy(cnt[:, :], p_tr[:, 0:GROUPS])
            v.tensor_scalar(start[:, :], p_tr[:, 128:128 + GROUPS], half[:, 0:1], None, ALU.add)
            v.tensor_copy(own[:, :], p_tr[:, 256:256 + GROUPS])
            ch.link(v.tensor_copy(row[:, :], p_row[0:1, 0:SETS]))
            ch.link(v.reduce_max(top[:, 0:1], row[:, :], axis=AX))
            ch.link(v.tensor_scalar(top[:, 1:2], top[:, 0:1], SLOTS + 0.5, 1.0 / SLOTS, ALU.add, ALU.mult))
            ch.link(v.tensor_copy(pass_i[:, :], top[:, 1:2]))
            ch.link(v.tensor_copy(top[:, 2:3], pass_i[:, :]))
            ch.link(v.tensor_tensor(top[:, 3:4], top[:, 2:3], top[:, 1:2], ALU.is_gt))
            ch.link(v.tensor_tensor(top[:, 2:3], top[:, 2:3], top[:, 3:4], ALU.subtract))
            v.tensor_copy(pass_i[:, :], top[:, 2:3]).then_inc(s_npass, 1)
            n_pass = passes(dve)
            before = ch.n
            PER_PASS = 14

            def wide(t2):
                return t2.unsqueeze(2).to_broadcast([128, GROUPS, CHUNKS])

            def over(t2):
                return t2.unsqueeze(1).to_broadcast([128, GROUPS, CHUNKS])

            def cube(t2):
                return t2.rearrange("p (g k) -> p g k", k=CHUNKS)

            with dve.Fori(0, n_pass) as p:
                ch.base = p * PER_PASS
                ch.link(v.tensor_scalar(start_c[:, :], start[:, :], float(E), None, ALU.min))
                v.tensor_copy(start_i[:, :], start_c[:, :]).then_inc(s_start, 1)
                ch.link(v.tensor_scalar(row_c[:, :], row[:, :], 2.0 * STEP, 2.0 * STEP, ALU.add, ALU.max))
                ch.link(v.tensor_scalar(row_c[:, :], row_c[:, :], float(SLOTS), None, ALU.min))
                ch.link(v.tensor_copy(iters_i[:, :], row_c[:, :]))
                ch.link(v.tensor_single_scalar(iters_i[:, :], iters_i[:, :], 2, op=ALU.logical_shift_right))
                ch.link(v.tensor_copy(iters[:, :], iters_i[:, :]))
                ch.link(v.tensor_tensor_scan(upto[:, :], one[:, :], iters[:, :], carry[:, 0:1], ALU.mult, ALU.add))
                ch.link(v.tensor_tensor(iters[:, :], upto[:, :], iters[:, :], ALU.subtract))
                v.tensor_copy(base_i[:, :], iters[:, :])
                ch.link(v.tensor_copy(carry[:, :], upto[:, SETS - 1:SETS]))
                v.tensor_tensor(cube(valid[:, :]), over(slot[:, :]), wide(cnt[:, :]), ALU.is_le)
                ch.link(v.tensor_scalar(not_own[:, :], slot[:, :], 0.5, None, ALU.is_gt))
                ch.link(v.tensor_tensor(cube(take[:, :]), cube(valid[:, :]), over(not_own[:, :]), ALU.mult))
                dve.wait_ge(s_runs, 16 * GROUPS * (p + 1))
                edge = runs[:, :, :].rearrange("p g (k s) -> p g k s", s=2)[:, :, :, 0]
                ch.link(v.tensor_tensor(edge, edge, wide(own[:, :]), ALU.subtract))
                ch.link(v.tensor_tensor(cube(take[:, :]), cube(take[:, :]), edge, ALU.mult))
                v.tensor_tensor(idx[:, :, :], cube(take[:, :]), wide(own[:, :]), ALU.add).then_inc(s_table, 1)
                dve.wait_ge(s_table, p + 1)
                dve.nop(nofuse=True)

                with dve.Fori(0, SETS) as t:
                    k = p * SETS + t
                    n, first = set_iters(dve, t)
                    dve.wait_ge(s_max_ld, 32 * (k + 1))
                    v.tensor_copy(acc[:, :, :], max_in[:, :, :]).then_inc(s_acc0, 1)
                    dve.wait_ge(s_acc0, k + 1)
                    dve.nop(nofuse=True)
                    with dve.Fori(0, n) as i:
                        it = first + i
                        for x in range(CPI):
                            dve.wait_ge(s_g[x], 16 * (it + 1))
                            dve.wait_ge(s_max, it * CPI + (CPI + x + 1 - SET))
                            v.tensor_tensor(acc[:, x % SET, :], acc[:, x % SET, :], g[:, x, 0:TW], ALU.max).then_inc(s_max, 1)
                    dve.wait_ge(s_max, (first + n) * CPI + CPI)
                    dve.nop(nofuse=True)
                    dve.wait_ge(s_stored, k + 1)
                    v.tensor_copy(max_out[:, :, :], acc[:, :, :]).then_inc(s_acc, 1)
                    dve.wait_ge(s_acc, k + 1)
                    dve.nop(nofuse=True)
                dve.wait_ge(s_pass, p + 1)
                v.tensor_scalar(start[:, :], start[:, :], float(SLOTS), None, ALU.add)
                v.tensor_scalar(row[:, :], row[:, :], -float(SLOTS), None, ALU.add)
                ch.link(v.tensor_scalar(slot[:, :], slot[:, :], float(SLOTS), None, ALU.add))
                assert ch.n - before == PER_PASS, ch.n - before

        @block.scalar
        def _(act):
            act.sem_inc(s_ev, 1)
            act.wait_ge(s_e2, 1)
            n_pass = passes(act)
            with act.Fori(0, n_pass) as p:
                act.wait_ge(s_table, p + 1)
                act.nop(nofuse=True)
                with act.Fori(0, SETS) as t:
                    k = p * SETS + t
                    n, first = set_iters(act, t)
                    with act.Fori(0, n) as i:
                        it = first + i
                        for j in range(STEP):
                            for q in range(SET):
                                x = j * SET + q
                                act.wait_ge(s_pe, it * CPI + (x + 1))
                                nc.scalar.activation(dg[:, x, 0:NG], e2[:, :], ACT.Copy,
                                                     scale=valid[:, bass.ds(t * (SET * CHUNKS) + q * CHUNKS + i * STEP + j, 1)]).then_inc(s_act, 1)
                            for q in range(SET):
                                x = j * SET + q
                                act.wait_ge(s_g[x], 16 * (it + 1))
                                act.wait_ge(s_act, it * CPI + (x + 1))
                                nc.scalar.activation(dg[:, x, NG:2 * NG], dg[:, x, 0:NG], ACT.Copy,
                                                     scale=g[:, x, TW:TW + 1]).then_inc(s_dg, 1)
                    act.wait_ge(s_set, k + 1)
                    act.wait_ge(s_stored, k + 1)
                    for q in range(SET):
                        last = nc.scalar.activation(sum_out[:, q, :], p_s[q][:, 0:TW], ACT.Copy)
                    last.then_inc(s_ev, 1)

        @block.tensor
        def _(pe):
            pe.sem_inc(s_pe, CPI)
            pe.wait_ge(s_two, 1)
            for k in range(3):
                nc.tensor.transpose(p_tr[:, k * 128:k * 128 + GROUPS], two[:, k].rearrange("g h l -> g (h l)"),
                                    ident[0:GROUPS, 0:GROUPS])
            nc.tensor.transpose(p_row[0:1, 0:SETS], most[:, :], ident[0:SETS, 0:SETS]).then_inc(s_tr, 1)
            n_pass = passes(pe)
            with pe.Fori(0, n_pass) as p:
                pe.wait_ge(s_table, p + 1)
                pe.nop(nofuse=True)
                with pe.Fori(0, SETS) as t:
                    k = p * SETS + t
                    n, first = set_iters(pe, t)
                    pe.wait_ge(s_sum_ld, 32 * (k + 1))
                    pe.wait_ge(s_ev, k + 1)
                    for q in range(SET):
                        last = nc.tensor.matmul(p_s[q][:, 0:TW], ident[:, :], sum_in[:, q, :], start=True, stop=False)
                    last.then_inc(s_sum_used, 1)
                    with pe.Fori(0, n) as i:
                        it = first + i
                        for x in range(CPI):
                            pe.wait_ge(s_dg, it * CPI + (x + 1))
                            nc.tensor.matmul(p_s[x % SET][:, 0:TW], dg[:, x, :], g[:, x, 0:TW], start=False,
                                             stop=False).then_inc(s_pe, 1)
                    for q in range(SET):
                        last = nc.tensor.matmul(p_s[q][:, 0:TW], zero_b[:, 0:128], zero_b[:, :], start=False, stop=True)
                    last.then_inc(s_set, 1)


def phase_conv(nc, phase, a, d, ident, stats):
    K = 3 * BASES
    LH = L * HEADS
    H2 = 2 * L
    DVE_PARTS = ((0, 2), (1, 2), (2, 2), (0, 0))
    POOL_PARTS = tuple((l, r) for l in range(L) for r in range(2) if (l, r) != (0, 0))
    with phase("c") as (c, sb, ps, sm):
        wc = sb("wc", [128, CH, L, 128])
        bc = sb("bc", [P, L * 128])
        cb = sb("cb", [P, L * C])
        dinv = sb("dinv", [P, NT])
        invdeg = sb("invdeg", [P, NT])
        rank = sb("rank", [P, NT], I32)
        ibuf = sb("ibuf", [P, 2], I32)
        xt = sb("xt", [128, 2, CH * P])
        ag = sb("ag", [P, 2, 4, TW])
        w16 = sb("w16", [P, 2, LH * 16])
        w12 = sb("w12", [P, 2, LH, K])
        prod = sb("prod", [P, 2, L, HEADS, K, HC])
        h = sb("h", [P, 2, L * C])
        ht = sb("ht", [128, 2, H2 * P])
        p_w = [ps(f"p_w{b}") for b in range(2)]
        p_s = [ps(f"p_s{b}") for b in range(2)]
        p_h = [[ps(f"p_h{b}{q}") for q in range(2)] for b in range(2)]
        (s_const, s_dve, s_cw, s_w16, s_w12, s_wa, s_mx, s_pd, s_pp, s_red, s_ps, s_h, s_tp, s_ht, s_st, s_rank,
         s_ib) = (sm(n) for n in
            ("const", "dve", "cw", "w16", "w12", "wa", "mx", "pd", "pp", "red", "ps", "h", "tp", "ht", "st", "rank",
             "ib"))
        s_ld = [sm(f"ld{b}") for b in range(2)]
        s_ag = [sm(f"ag{b}", swdge=True) for b in range(2)]
        s_out = [sm(f"out{b}") for b in range(2)]
        block = c.enter_context(nc.Block())
        agg = d["agg"].rearrange("n r w -> n (r w)")

        def product(eng, b, l, r):
            return eng.tensor_tensor(
                prod[:, b, l, :, r * BASES:(r + 1) * BASES, :],
                w12[:, b, l * HEADS:(l + 1) * HEADS, r * BASES:(r + 1) * BASES].unsqueeze(3).to_broadcast([P, HEADS, BASES, HC]),
                ag[:, b, r, l * BW:(l + 1) * BW].rearrange("p (k c) -> p k c", c=HC).unsqueeze(1).to_broadcast([P, HEADS, BASES, HC]),
                ALU.mult)

        @block.sync
        def _(sp):
            for k in range(CH):
                sp.dma_start(wc[:, k], a["L0_gnn_Wc"][:, k * 128:(k + 1) * 128, :].rearrange("l p w -> p l w")).then_inc(s_const, 16)
            for t, name in ((bc, "L0_gnn_bc"), (cb, "L0_gnn_conv_bias")):
                sp.dma_start(t[:, :], a[name].rearrange("(o l) n -> o (l n)", o=1).to_broadcast([P, t.shape[1]])).then_inc(s_const, 16)
            sp.dma_start(rank[:, :], d["rank"][0:N].rearrange("(p t) -> p t", t=NT)).then_inc(s_rank, 16)
            sp.dma_start(dinv[:, :], d["dinv"][0:N].rearrange("(p t) -> p t", t=NT)).then_inc(s_const, 16)

            def step(i, first):
                for b in range(2):
                    t = 2 * i + b
                    if not first:
                        sp.wait_ge(s_cw, t - 1)
                    sp.dma_start(xt[:, b], d["xnt"][bass.ds(t, 1)].rearrange("o p c -> (o p) c")).then_inc(s_ld[b], 16)
            loop2(sp, None, NT // 2, 0, step)

        @block.scalar
        def _(act):
            act.wait_ge(s_const, 80)

            def weights(t, b, first):
                act.wait_ge(s_w16, t + 1)
                if not first:
                    act.wait_ge(s_pd, t - 1)
                    act.wait_ge(s_pp, t - 1)
                w = w16[:, b, :].rearrange("p (x r k) -> p x r k", r=4, k=BASES)
                nc.scalar.activation(w12[:, b, :, BASES:2 * BASES], w[:, :, 3], ACT.Copy, scale=dinv[:, bass.ds(t, 1)])
                nc.scalar.activation(w12[:, b, :, 2 * BASES:], w[:, :, 1], ACT.Copy).then_inc(s_wa, 1)

            def store(t, b, i, first):
                act.wait_ge(s_tp, t + 1)
                if not first:
                    act.wait_ge(s_out[b], 16 * i)
                    act.wait_ge(s_st, t - 1)
                nc.scalar.activation(ht[:, b, 0:4 * P], p_h[b][0][:, 0:4 * P], ACT.Copy)
                nc.scalar.activation(ht[:, b, 4 * P:], p_h[b][1][:, 0:2 * P], ACT.Copy).then_inc(s_ht, 1)
                act.wait_ge(s_ht, t + 1)
                act.dma_start(d["ht"][bass.ds(t, 1)].rearrange("o p c -> (o p) c"), ht[:, b]).then_inc(s_out[b], 16)

            weights(0, 0, True)

            def step(i, first, last=False):
                for b in range(2):
                    t = 2 * i + b
                    if not (last and b):
                        weights(t + 1, 1 - b, first and b == 0)
                    if not (first and b == 0):
                        store(t - 1, 1 - b, i + b - 1, first)
            step(0, True)
            with act.Fori(1, NT // 2 - 1) as i:
                step(i, False)
            step(NT // 2 - 1, False, True)
            store(NT - 1, 1, NT // 2 - 1, False)
            for b in range(2):
                act.wait_ge(s_out[b], 16 * (NT // 2))

        @block.gpsimd
        def _(pool):
            def gather(t, b, first):
                if not first:
                    pool.wait_ge(s_pd, t - 1)
                    pool.wait_ge(s_pp, t - 1)
                nc.gpsimd.tensor_copy(ibuf[:, b:b + 1], rank[:, bass.ds(t, 1)]).then_inc(s_ib, 1)
                pool.wait_ge(s_ib, t + 1)
                pool.nop(nofuse=True)
                nc.gpsimd.indirect_dma_start(out=ag[:, b].rearrange("p r w -> p (r w)"), out_offset=None, in_=agg[:, :],
                                             in_offset=bass.IndirectOffsetOnAxis(ap=ibuf[:, b:b + 1], axis=0)).then_inc(s_ag[b], 16)

            pool.wait_ge(s_rank, 16)
            gather(0, 0, True)

            def step(i, first, last=False):
                for b in range(2):
                    t = 2 * i + b
                    if not (last and b):
                        gather(t + 1, 1 - b, first and b == 0)
                    pool.wait_ge(s_ag[b], 16 * (i + 1))
                    pool.wait_ge(s_w12, t + 1)
                    pool.wait_ge(s_wa, t + 1)
                    if not first:
                        pool.wait_ge(s_red, t - 1)
                        pool.wait_ge(s_ps, t - 1)
                    for l, r in POOL_PARTS:
                        prods = product(nc.gpsimd, b, l, r)
                    prods.then_inc(s_pp, 1)
            step(0, True)
            with pool.Fori(1, NT // 2 - 1) as i:
                step(i, False)
            step(NT // 2 - 1, False, True)

        @block.vector
        def _(dve):
            ch = Chain(dve, s_dve)
            v = nc.vector
            dve.wait_ge(s_const, 80)
            ch.link(v.tensor_tensor(invdeg[:, :], dinv[:, :], dinv[:, :], ALU.mult))

            def products(t, b, i, first):
                dve.wait_ge(s_cw, t + 1)
                if not first:
                    dve.wait_ge(s_wa, t - 1)
                    dve.wait_ge(s_pp, t - 1)
                v.tensor_tensor(w16[:, b, :], p_w[b][0:P, 0:LH * 16], bc[:, :], ALU.add).then_inc(s_w16, 1)
                dve.wait_ge(s_w16, t + 1)
                w = w16[:, b, :].rearrange("p (x r k) -> p x r k", r=4, k=BASES)
                v.scalar_tensor_tensor(w12[:, b, :, 0:BASES], w[:, :, 0], invdeg[:, bass.ds(t, 1)], w[:, :, 2],
                                       ALU.mult, ALU.add).then_inc(s_w12, 1)
                dve.wait_ge(s_ag[b], 16 * (i + 1))
                v.tensor_tensor(ag[:, b, 2, :], ag[:, b, 2, :], ag[:, b, 3, :], ALU.max).then_inc(s_mx, 1)
                dve.wait_ge(s_mx, t + 1)
                dve.wait_ge(s_w12, t + 1)
                dve.wait_ge(s_wa, t + 1)
                if not first:
                    dve.wait_ge(s_red, t - 1)
                    dve.wait_ge(s_ps, t - 1)
                for l, r in DVE_PARTS:
                    last = product(v, b, l, r)
                last.then_inc(s_pd, 1)

            def layer0(t, b, first):
                dve.wait_ge(s_pd, t + 1)
                dve.wait_ge(s_pp, t + 1)
                if not first:
                    dve.wait_ge(s_tp, t - 1)
                v.reduce_sum(h[:, b, 0:C].rearrange("p (h c) -> p h c", c=HC),
                             prod[:, b, 0].rearrange("p h k c -> p h c k"), axis=AX).then_inc(s_red, 1)

            def statistics(t, b):
                dve.wait_ge(s_ht, t + 1)
                for k in range(H2):
                    last = v.bn_stats(stats[:, k, bass.ds(t, 1), :].rearrange("p o s -> p (o s)"),
                                      ht[:, b, k * P:(k + 1) * P])
                last.then_inc(s_st, 1)

            def biased(t, b):
                dve.wait_ge(s_red, t + 1)
                v.tensor_tensor(h[:, b, 0:C], h[:, b, 0:C], cb[:, 0:C], ALU.add)
                dve.wait_ge(s_ps, t + 1)
                v.tensor_tensor(h[:, b, C:], p_s[b][0:P, :], cb[:, C:], ALU.add).then_inc(s_h, 1)

            products(0, 0, 0, True)

            def step(i, first, last=False):
                for b in range(2):
                    t = 2 * i + b
                    if not (last and b):
                        products(t + 1, 1 - b, i + b, first and b == 0)
                    layer0(t, b, first)
                    if not (first and b == 0):
                        statistics(t - 1, 1 - b)
                    biased(t, b)
            step(0, True)
            with dve.Fori(1, NT // 2 - 1) as i:
                step(i, False)
            step(NT // 2 - 1, False, True)
            statistics(NT - 1, 1)

        @block.tensor
        def _(pe):
            pe.wait_ge(s_const, 80)

            def combine_weights(t, b, i, first):
                pe.wait_ge(s_ld[b], 16 * (i + 1))
                if not first:
                    pe.wait_ge(s_w16, t - 1)
                for k in range(CH):
                    last = nc.tensor.matmul(p_w[b][0:P, 0:TW], xt[:, b, k * P:(k + 1) * P],
                                            wc[:, k].rearrange("p l w -> p (l w)"), start=k == 0, stop=k == CH - 1)
                last.then_inc(s_cw, 1)

            def transposes(t, b, first):
                pe.wait_ge(s_h, t + 1)
                if not first:
                    pe.wait_ge(s_ht, t - 1)
                for k in range(H2):
                    last = nc.tensor.transpose(p_h[b][k // 4][:, (k % 4) * P:(k % 4 + 1) * P],
                                               h[:, b, k * 128:(k + 1) * 128], ident[0:P, 0:P])
                last.then_inc(s_tp, 1)

            def sums(t, b, first):
                pe.wait_ge(s_pd, t + 1)
                pe.wait_ge(s_pp, t + 1)
                if not first:
                    pe.wait_ge(s_h, t - 1)
                for k in range(K):
                    last = nc.tensor.matmul(p_s[b][0:P, :], ident[0:P, 0:P], prod[:, b, 1:L, :, k, :],
                                            start=k == 0, stop=k == K - 1)
                last.then_inc(s_ps, 1)

            combine_weights(0, 0, 0, True)

            def step(i, first, last=False):
                for b in range(2):
                    t = 2 * i + b
                    if not (last and b):
                        combine_weights(t + 1, 1 - b, i + b, first and b == 0)
                    if not (first and b == 0):
                        transposes(t - 1, 1 - b, first)
                    sums(t, b, first)
            step(0, True)
            with pe.Fori(1, NT // 2 - 1) as i:
                step(i, False)
            step(NT // 2 - 1, False, True)
            transposes(NT - 1, 1, False)


def phase_mix(nc, phase, a, d, ident, x_sb, mv, rstd, kvbd, stats, xst):
    H2 = 2 * L
    KF = 2 + H2
    ZB = 4
    XB = 10
    with phase("m") as (c, sb, ps, sm):
        fcw = sb("fcw", [128, KF, C])
        wq = sb("wq", [128, CH, C])
        w1 = sb("w1", [128, CH, C])
        w2 = sb("w2", [128, CH, C])
        b_q = sb("b_q", [128, CH])
        b1 = sb("b1", [128, CH])
        gam = sb("gam", [128, H2])
        bet = sb("bet", [128, H2])
        fcb = sb("fcb", [P, C])
        b2 = sb("b2", [P, C])
        bmv = sb("bmv", [128, H2, 2])
        bs = sb("bs", [128, H2])
        bb = sb("bb", [128, H2])
        wqt = sb("wqt", [128, CH, C])
        rt = sb("rt", [128, CH, C])
        m1 = sb("m1", [128, CH, C])
        u = sb("u", [128, CH])
        c1 = sb("c1", [128, CH])
        xt = sb("xt", [128, 2, CH * P])
        ht = sb("ht", [128, 2, H2 * P])
        z = sb("z", [128, 2, H2 * P])
        gt = sb("gt", [128, 2, CH * P])
        xn = sb("xn", [P, 2, C])
        zeros = sb("zeros", [128, ZB * C])
        p_a = ps("p_a")
        p_b = ps("p_b")
        p_g = [ps(f"p_g{b}") for b in range(2)]
        p_o = [ps(f"p_o{b}") for b in range(2)]
        (s_c, s_dve, s_wqt, s_wqtc, s_rt, s_rtc, s_m1, s_m1c, s_u, s_uc, s_c1, s_c1c, s_bn, s_bns, s_bn2) = (sm(n) for n in
            ("c", "dve", "wqt", "wqtc", "rt", "rtc", "m1", "m1c", "u", "uc", "c1", "c1c", "bn", "bns", "bn2"))
        s_z, s_y, s_gp, s_gt, s_o, s_res, s_zero = (sm(n) for n in ("z", "y", "gp", "gt", "o", "res", "zero"))
        s_out = sm("out", swdge=True)
        s_ld = [sm(f"ld{b}") for b in range(2)]
        block = c.enter_context(nc.Block())

        @block.sync
        def _(sp):
            def rows128(name):
                return a[name].rearrange("(k p) n -> p k n", p=128)
            for k in range(CH):
                sp.dma_start(wq[:, k, :].rearrange("p (h s) -> p h s", s=HC),
                             a["L0_mix_w_qkv"][k * 128:(k + 1) * 128, :].rearrange("p (h s) -> p h s", s=3 * HC)[:, :, 0:HC]).then_inc(s_c, 16)
            sp.dma_start(w1[:, :, :], rows128("L0_mix_w1")).then_inc(s_c, 16)
            sp.dma_start(w2[:, :, :], rows128("L0_mix_w2")).then_inc(s_c, 16)
            sp.dma_start(fcw[:, :, :], rows128("L0_gnn_fc_W")).then_inc(s_c, 16)
            for k in range(CH):
                for h in range(4):
                    at = (4 * k + h) * 3 * HC
                    sp.dma_start(b_q[32 * h:32 * h + 32, k:k + 1],
                                 a["L0_mix_b_qkv"][at:at + HC].rearrange("(p o) -> p o", o=1)).then_inc(s_c, 16)
                sp.dma_start(b1[:, k:k + 1], a["L0_mix_b1"][k * 128:(k + 1) * 128].rearrange("(p o) -> p o", o=1)).then_inc(s_c, 16)
            for l in range(L):
                for k in range(CH):
                    sl = slice(k * 128, (k + 1) * 128)
                    q = l * CH + k
                    sp.dma_start(gam[:, q:q + 1], a["L0_gnn_bn_gamma"][l, sl].rearrange("(p o) -> p o", o=1)).then_inc(s_c, 16)
                    sp.dma_start(bet[:, q:q + 1], a["L0_gnn_bn_beta"][l, sl].rearrange("(p o) -> p o", o=1)).then_inc(s_c, 16)
            sp.dma_start(fcb[:, :], a["L0_gnn_fc_b"].rearrange("(o n) -> o n", o=1).to_broadcast([P, C])).then_inc(s_c, 16)
            sp.dma_start(b2[:, :], a["L0_mix_b2"].rearrange("(o n) -> o n", o=1).to_broadcast([P, C])).then_inc(s_c, 16)

            def step(i, first):
                for b in range(2):
                    t = 2 * i + b
                    if not first:
                        sp.wait_ge(s_o, t - 1)
                    sp.dma_start(ht[:, b], d["ht"][bass.ds(t, 1)].rearrange("o p c -> (o p) c")).then_inc(s_ld[b], 16)
                    sp.dma_start(xt[:, b], d["xnt"][bass.ds(t, 1)].rearrange("o p c -> (o p) c")).then_inc(s_ld[b], 16)
            loop2(sp, None, NT // 2, 0, step)

        @block.gpsimd
        def _(pool):
            nc.gpsimd.memset(zeros[:, :], 0.0).then_inc(s_zero, 1)
            pool.wait_ge(s_zero, 1)
            for g in range(0, BLOCKS + 1, ZB):
                n = min(ZB, BLOCKS + 1 - g)
                pool.dma_start(d["xg"][g * 128:(g + n) * 128, :].rearrange("(p r) c -> p (r c)", p=128),
                               zeros[:, 0:n * C]).then_inc(s_out, 16)
            for j in range(0, NT, XB):
                pool.wait_ge(s_res, j + XB)
                pool.dma_start(d["x2"].rearrange("(p t) c -> p t c", t=NT)[:, j:j + XB, :],
                               x_sb[:, j:j + XB, :]).then_inc(s_out, 16)
            pool.wait_ge(s_out, 16 * (-(-(BLOCKS + 1) // ZB) + NT // XB))

        N_CONST = 16 * (5 + 2 * 5 + 2 * H2 + 2)

        @block.vector
        def _(dve):
            ch = Chain(dve, s_dve)
            v = nc.vector
            dve.wait_ge(s_c, N_CONST)
            for k in range(H2):
                v.bn_aggr(bmv[:, k, :], stats[:, k, :, :].rearrange("p t s -> p (t s)"))
            ch.link(v.tensor_tensor(fcb[:, :], fcb[:, :], b2[:, :], ALU.add))
            v.tensor_scalar_add(bs[:, :], bmv[:, :, 1], EPS).then_inc(s_bn, 1)
            dve.wait_ge(s_bns, 1)
            ch.link(v.reciprocal(bb[:, :], bs[:, :]))
            ch.link(v.tensor_tensor(bs[:, :], bb[:, :], gam[:, :], ALU.mult))
            ch.link(v.tensor_tensor(bb[:, :], bs[:, :], bmv[:, :, 0], ALU.mult))
            v.tensor_tensor(bb[:, :], bet[:, :], bb[:, :], ALU.subtract).then_inc(s_bn2, 1)
            dve.wait_ge(s_wqt, 1)
            v.tensor_copy(wqt[:, 0, :], p_a[:, 0:C])
            v.tensor_copy(wqt[:, 1, :], p_a[:, C:2 * C]).then_inc(s_wqtc, 1)
            dve.wait_ge(s_rt, 1)
            ch.link(v.tensor_copy(rt[:, :, :], p_b[:, :].rearrange("p (k c) -> p k c", k=CH)))
            v.tensor_tensor(rt[:, 0, 0:128], rt[:, 0, 0:128], ident[:, :], ALU.add)
            v.tensor_tensor(rt[:, 1, 128:C], rt[:, 1, 128:C], ident[:, :], ALU.add).then_inc(s_rtc, 1)
            dve.wait_ge(s_m1, 1)
            v.tensor_copy(m1[:, :, :], p_a[:, :].rearrange("p (k c) -> p k c", k=CH)).then_inc(s_m1c, 1)
            dve.wait_ge(s_u, 1)
            v.tensor_copy(u[:, :], p_b[:, 0:CH]).then_inc(s_uc, 1)
            dve.wait_ge(s_c1, 1)
            v.tensor_tensor(c1[:, :], p_b[:, 8:8 + CH], b1[:, :], ALU.add).then_inc(s_c1c, 1)

            def step(i, first):
                for b in range(2):
                    t = 2 * i + b
                    dve.wait_ge(s_z, t + 1)
                    v.scalar_tensor_tensor(z[:, b, :], z[:, b, :], SLOPE, z[:, b, :], ALU.mult, ALU.max).then_inc(s_y, 1)
                    xrow = x_sb[:, bass.ds(t, 1), :].rearrange("p o c -> p (o c)")
                    ch.link(v.tensor_scalar(xn[:, b, :], xrow, mv[:, bass.ds(t, 1), 0], rstd[:, bass.ds(t, 1)], ALU.subtract, ALU.mult))
                    ch.link(v.tensor_tensor(xn[:, b, :], xn[:, b, :], xrow, ALU.add))
                    ch.link(v.tensor_tensor(xn[:, b, :], xn[:, b, :], fcb[:, :], ALU.add))
                    dve.wait_ge(s_o, t + 1)
                    v.tensor_tensor(xrow, p_o[b][0:P, 0:C], xn[:, b, :], ALU.add).then_inc(s_res, 1)
                    dve.wait_ge(s_res, t + 1)
                    v.bn_stats(xst[:, bass.ds(t, 1), :].rearrange("p o s -> p (o s)"), xrow)
            loop2(dve, ch, NT // 2, 2 * 3, step)

        @block.scalar
        def _(act):
            act.wait_ge(s_bn, 1)
            nc.scalar.activation(bs[:, :], bs[:, :], ACT.Sqrt).then_inc(s_bns, 1)
            act.wait_ge(s_bn2, 1)
            act.wait_ge(s_c1c, 1)

            def step(i, first):
                for b in range(2):
                    t = 2 * i + b
                    act.wait_ge(s_ld[b], 32 * (i + 1))
                    if not first:
                        act.wait_ge(s_o, t - 1)
                    for k in range(H2):
                        sl = slice(k * P, (k + 1) * P)
                        last = nc.scalar.activation(z[:, b, sl], ht[:, b, sl], ACT.Identity, bias=bb[:, k:k + 1], scale=bs[:, k:k + 1])
                    last.then_inc(s_z, 1)
                    act.wait_ge(s_gp, t + 1)
                    for k in range(CH):
                        sl = slice(k * P, (k + 1) * P)
                        last = nc.scalar.activation(gt[:, b, sl], p_g[b][:, sl], ACT.Gelu, bias=c1[:, k:k + 1])
                    last.then_inc(s_gt, 1)
            loop2(act, None, NT // 2, 0, step)

        @block.tensor
        def _(pe):
            pe.wait_ge(s_c, N_CONST)
            for half in range(CH):
                for k in range(CH):
                    src = wq[:, k, half * 128:(half + 1) * 128]
                    last = nc.tensor.transpose(p_a[:, half * C + k * 128:half * C + (k + 1) * 128], src, ident[:, :])
            last.then_inc(s_wqt, 1)
            pe.wait_ge(s_wqtc, 1)
            for half in range(CH):
                last = nc.tensor.matmul(p_b[:, half * C:(half + 1) * C], kvbd[:, half, :], wqt[:, half, :], start=True, stop=True)
            last.then_inc(s_rt, 1)
            pe.wait_ge(s_rtc, 1)
            for k in range(CH):
                for half in range(CH):
                    last = nc.tensor.matmul(p_a[:, k * C:(k + 1) * C], rt[:, half, k * 128:(k + 1) * 128], w1[:, half, :],
                                            start=half == 0, stop=half == CH - 1)
            last.then_inc(s_m1, 1)
            for half in range(CH):
                last = nc.tensor.matmul(p_b[:, half:half + 1], kvbd[:, half, :], b_q[:, half:half + 1], start=True, stop=True)
            last.then_inc(s_u, 1)
            pe.wait_ge(s_uc, 1)
            for k in range(CH):
                for half in range(CH):
                    last = nc.tensor.matmul(p_b[:, 8 + k:9 + k], w1[:, half, k * 128:(k + 1) * 128], u[:, half:half + 1],
                                            start=half == 0, stop=half == CH - 1)
            last.then_inc(s_c1, 1)
            pe.wait_ge(s_m1c, 1)

            def step(i, first):
                for b in range(2):
                    t = 2 * i + b
                    pe.wait_ge(s_ld[b], 32 * (i + 1))
                    if not first:
                        pe.wait_ge(s_gt, t - 1)
                    for f in range(CH):
                        for k in range(CH):
                            last = nc.tensor.matmul(p_g[b][:, f * P:(f + 1) * P], m1[:, k, f * 128:(f + 1) * 128],
                                                    xt[:, b, k * P:(k + 1) * P], start=k == 0, stop=k == CH - 1)
                    last.then_inc(s_gp, 1)
                    if not first:
                        pe.wait_ge(s_res, t - 1)
                    for k in range(CH):
                        nc.tensor.matmul(p_o[b][0:P, 0:C], xt[:, b, k * P:(k + 1) * P], fcw[:, k, :], start=k == 0, stop=False)
                    pe.wait_ge(s_y, t + 1)
                    for k in range(H2):
                        nc.tensor.matmul(p_o[b][0:P, 0:C], z[:, b, k * P:(k + 1) * P], fcw[:, CH + k, :], start=False, stop=False)
                    pe.wait_ge(s_gt, t + 1)
                    for k in range(CH):
                        last = nc.tensor.matmul(p_o[b][0:P, 0:C], gt[:, b, k * P:(k + 1) * P], w2[:, k, :], start=False, stop=k == CH - 1)
                    last.then_inc(s_o, 1)
            loop2(pe, None, NT // 2, 0, step)


def phase_route(nc, phase, a, d, ident, x_sb, st, pos, gate, blk, w1, b1, w2_lo):
    X = EXPERTS
    T8 = NT * X
    with phase("r") as (c, sb, ps, sm):
        wr = sb("wr", [128, CH, X])
        br = sb("br", [P, X])
        half = sb("half", [P, NT])
        mv = sb("mv", [P, NT, 2])
        mv2 = sb("mv2", [P, NT, 2])
        r1 = sb("r1", [P, NT])
        r2 = sb("r2", [P, NT])
        xt = sb("xt", [128, 2, CH * P])
        lg = sb("lg", [P, NT, X])
        lane_i = sb("lane_i", [P, X], I32)
        e_id = sb("e_id", [P, X])
        red = sb("red", [P, NT])
        tsum = sb("tsum", [P, NT])
        top1 = sb("top1", [P, NT])
        top2 = sb("top2", [P, NT])
        m1 = sb("m1", [P, NT, X])
        pick = sb("pick", [P, 2, NT, X])
        both = sb("both", [P, X, NT])
        ones = sb("ones", [P, T8])
        run = sb("run", [P, X, NT])
        lane = sb("lane", [P, X])
        lower = sb("lower", [P, P])
        fill = sb("fill", [P, X])
        fill_i = sb("fill_i", [P, X], I32)
        end = sb("end", [P, X])
        off = sb("off", [P, X])
        blk_i = sb("blk_i", [1, BLOCKS], I32)
        blk_f = sb("blk_f", [1, BLOCKS])
        blk_g = sb("blk_g", [1, BLOCKS, X])
        ibuf = sb("ibuf", [P, 2, 2], I32)
        xe = sb("xe", [P, 2, C])
        ln = sb("ln", [2 * X, 2, 128])
        lnt = sb("lnt", [128, 2, 2 * X])
        shift = sb("shift", [128, CH * X, 128])
        pick_row = sb("pick_row", [X, X, 128])
        b1_in = sb("b1_in", [X, HID])
        p_ln = ps("p_ln")
        p_w = [ps(f"p_w{q}") for q in range(2)]
        p_t = [ps(f"p_t{b}") for b in range(2)]
        p_l = [ps(f"p_l{b}") for b in range(2)]
        p_c = ps("p_c")
        (s_c, s_gp, s_dve, s_var, s_std, s_xo, s_tp, s_xt, s_lp, s_lg, s_var2, s_std2, s_ex, s_exd, s_lane,
         s_cnt, s_pos, s_xe, s_ib, s_keep, s_ln, s_w1, s_w2, s_lt) = (sm(n) for n in
            ("c", "gp", "dve", "var", "std", "xo", "tp", "xt", "lp", "lg", "var2", "std2", "ex", "exd", "lane",
             "cnt", "pos", "xe", "ib", "keep", "ln", "w1", "w2", "lt"))
        s_ltc, s_sh, s_wp, s_wc, s_scl = (sm(n) for n in ("ltc", "sh", "wp", "wc", "scl"))
        s_stat = sm("stat")
        s_sc = [sm(f"sc{b}", swdge=True) for b in range(2)]
        block = c.enter_context(nc.Block())

        @block.sync
        def _(sp):
            sp.dma_start(wr[:, :, :], a["L0_ffn_Wr"].rearrange("(k p) n -> p k n", p=128)).then_inc(s_c, 16)
            sp.dma_start(br[:, :], a["L0_ffn_br"].rearrange("(o n) -> o n", o=1).to_broadcast([P, X])).then_inc(s_c, 16)
            for j, n in enumerate(("g", "b")):
                sp.dma_start(ln[:, j, :], a[f"L0_ffn_ln_{n}"].rearrange("e (k p) -> (e k) p", p=128)).then_inc(s_ln, 16)
            sp.dma_start(b1_in[:, :], a["L0_ffn_b1"]).then_inc(s_ln, 16)
            for k in range(CH):
                sp.dma_start(w1[:, k, :].rearrange("p (e h) -> p e h", e=X),
                             a["L0_ffn_W1"][:, k * 128:(k + 1) * 128, :].rearrange("e p h -> p e h")).then_inc(s_w1, 16)
            for k in range(W2_LO):
                sp.wait_ge(s_xe, -(-(k + 1) * X * C // C))
                sp.dma_start(w2_lo[:, k, :].rearrange("p (e c) -> p e c", e=X),
                             a["L0_ffn_W2"][:, k * 128:(k + 1) * 128, :].rearrange("e p c -> p e c")).then_inc(s_w2, 16)
            sp.wait_ge(s_w2, 16 * W2_LO)

        @block.gpsimd
        def _(pool):
            g = nc.gpsimd
            g.iota(lane_i[:, :], pattern=[[1, X]], base=0, channel_multiplier=0).then_inc(s_gp, 1)
            g.iota(blk_i[:, :], pattern=[[128, BLOCKS]], base=0, channel_multiplier=0).then_inc(s_gp, 1)
            g.memset(lower[:, :], 1.0).then_inc(s_gp, 1)
            pool.wait_ge(s_gp, 3)
            g.affine_select(out=lower[:, :], in_=lower[:, :], compare_op=ALU.is_gt, fill=0.0, base=0,
                            pattern=[[1, P]], channel_multiplier=-1).then_inc(s_gp, 1)

            def keep_tile(i, first):
                for b in range(2):
                    t = 2 * i + b
                    pool.wait_ge(s_xo, t + 1)
                    g.tensor_copy(x_sb[:, bass.ds(t, 1), :].rearrange("p o c -> p (o c)"), xe[:, b, :]).then_inc(s_keep, 1)
            loop2(pool, None, NT // 2, 0, keep_tile)
            pool.wait_ge(s_pos, 1)

            def step(i, first):
                for b in range(2):
                    t = 2 * i + b
                    if not first:
                        pool.wait_ge(s_sc[b], 32 * i)
                    g.tensor_copy(ibuf[:, b, :], pos[:, :, bass.ds(t, 1)].rearrange("p k o -> p (k o)")).then_inc(s_ib, 1)
                    pool.wait_ge(s_ib, t + 1)
                    pool.nop(nofuse=True)
                    pool.wait_ge(s_xe, t + 1)
                    pool.nop(nofuse=True)
                    for k in range(2):
                        g.indirect_dma_start(out=d["xg"][:, :], out_offset=bass.IndirectOffsetOnAxis(ap=ibuf[:, b, k:k + 1], axis=0),
                                             in_=xe[:, b, :], in_offset=None).then_inc(s_sc[b], 16)
            loop2(pool, None, NT // 2, 0, step)
            for b in range(2):
                pool.wait_ge(s_sc[b], 32 * (NT // 2))

        @block.scalar
        def _(act):
            act.wait_ge(s_var, 1)
            nc.scalar.activation(r1[:, :], r1[:, :], ACT.Sqrt).then_inc(s_std, 1)

            def step(i, first):
                for b in range(2):
                    t = 2 * i + b
                    act.wait_ge(s_tp, t + 1)
                    if not first:
                        act.wait_ge(s_lp, t - 1)
                    nc.scalar.activation(xt[:, b, :], p_t[b][:, 0:CH * P], ACT.Copy).then_inc(s_xt, 1)
            loop2(act, None, NT // 2, 0, step)
            act.wait_ge(s_var2, 1)
            nc.scalar.activation(r2[:, :], r2[:, :], ACT.Sqrt).then_inc(s_std2, 1)
            act.wait_ge(s_ex, 1)
            nc.scalar.activation(lg[:, :, :], lg[:, :, :], ACT.Exp).then_inc(s_exd, 1)
            act.wait_ge(s_lt, 1)
            nc.scalar.activation(lnt[:, :, :], p_ln[:, 0:4 * X].rearrange("p (j r) -> p j r", j=2), ACT.Copy).then_inc(s_ltc, 1)
            act.wait_ge(s_ltc, 1)
            for r in range(CH * X):
                nc.scalar.activation(shift[:, r, :], lnt[:, 1, r:r + 1].to_broadcast([128, 128]), ACT.Copy)
            for e in range(X):
                last = nc.scalar.activation(pick_row[:, e, :], ident[0:X, e:e + 1].to_broadcast([X, 128]), ACT.Copy)
            last.then_inc(s_sh, 1)
            for e in range(X):
                for q in range(2):
                    act.wait_ge(s_wp, 2 * e + q + 1)
                    nc.scalar.activation(b1[:, e * HID + q * 512:e * HID + (q + 1) * 512], p_w[q][:, :], ACT.Copy).then_inc(s_wc, 1)
                for k in range(CH):
                    sl = slice(e * HID, (e + 1) * HID)
                    nc.scalar.activation(w1[:, k, sl], w1[:, k, sl], ACT.Copy, scale=lnt[:, 0, CH * e + k:CH * e + k + 1])

        @block.tensor
        def _(pe):
            pe.wait_ge(s_c, 32)

            def transposes(t, b, first):
                pe.wait_ge(s_xo, t + 1)
                if not first:
                    pe.wait_ge(s_xt, t - 1)
                for k in range(CH):
                    last = nc.tensor.transpose(p_t[b][:, k * P:(k + 1) * P],
                                               xe[:, b, k * 128:(k + 1) * 128], ident[0:P, 0:P])
                last.then_inc(s_tp, 1)

            transposes(0, 0, True)

            def step(i, has):
                for b in range(2):
                    t = 2 * i + b
                    if has(b, 1):
                        transposes(t + 1, 1 - b, not has(b, -1))
                    pe.wait_ge(s_xt, t + 1)
                    if has(b, -2):
                        pe.wait_ge(s_lg, t - 1)
                    for k in range(CH):
                        last = nc.tensor.matmul(p_l[b][0:P, 0:X], xt[:, b, k * P:(k + 1) * P], wr[:, k, :], start=k == 0, stop=k == CH - 1)
                    last.then_inc(s_lp, 1)
            pipelined(pe, None, NT // 2, 1, 1, 0, step)

            def bias_rows(e):
                for q in range(2):
                    if e > 0:
                        pe.wait_ge(s_wc, 2 * (e - 1) + q + 1)
                    cols = slice(q * 512, (q + 1) * 512)
                    for k in range(CH):
                        nc.tensor.matmul(p_w[q][:, :], shift[:, CH * e + k, :], w1[:, k, e * HID + q * 512:e * HID + (q + 1) * 512],
                                         start=k == 0, stop=False)
                    nc.tensor.matmul(p_w[q][:, :], pick_row[:, e, :], b1_in[:, cols], start=False, stop=True).then_inc(s_wp, 1)

            pe.wait_ge(s_ln, 48)
            for j in range(2):
                last = nc.tensor.transpose(p_ln[:, j * 2 * X:(j + 1) * 2 * X], ln[:, j, :], ident[0:2 * X, 0:2 * X])
            last.then_inc(s_lt, 1)
            pe.wait_ge(s_sh, 1)
            pe.wait_ge(s_w1, 16 * CH)
            for e in range(X // 2):
                bias_rows(e)
            pe.wait_ge(s_lane, 1)
            pe.wait_ge(s_gp, 4)
            nc.tensor.matmul(p_c[0:P, 0:X], lower[:, :], lane[:, :], start=True, stop=True)
            nc.tensor.matmul(p_c[0:P, 8:8 + X], ones[:, 0:P], lane[:, :], start=True, stop=True).then_inc(s_cnt, 1)
            for e in range(X // 2, X):
                bias_rows(e)

        @block.vector
        def _(dve):
            ch = Chain(dve, s_dve)
            v = nc.vector
            v.memset(ones[:, :], 1.0)
            halves_to_mean_var(nc, ch, st, mv, half)
            v.tensor_scalar_add(r1[:, :], mv[:, :, 1], EPS).then_inc(s_var, 1)
            dve.wait_ge(s_std, 1)
            ch.link(v.reciprocal(r1[:, :], r1[:, :]))
            dve.wait_ge(s_c, 32)

            def cols(t3, t):
                return t3[:, bass.ds(t, 1), :].rearrange("p o c -> p (o c)")

            def normalise(t, b, first):
                if not first:
                    dve.wait_ge(s_tp, t - 1)
                    dve.wait_ge(s_keep, t - 1)
                v.tensor_scalar(xe[:, b, :], cols(x_sb, t), mv[:, bass.ds(t, 1), 0], r1[:, bass.ds(t, 1)], ALU.subtract, ALU.mult).then_inc(s_xo, 1)
                dve.wait_ge(s_xo, t + 1)
                v.bn_stats(cols(st, t), xe[:, b, :]).then_inc(s_stat, 1)

            normalise(0, 0, True)
            normalise(1, 1, True)

            def step(i, has):
                for b in range(2):
                    t = 2 * i + b
                    if has(b, 2):
                        dve.wait_ge(s_stat, t + 1)
                        normalise(t + 2, b, False)
                    dve.wait_ge(s_lp, t + 1)
                    v.tensor_tensor(cols(lg, t), p_l[b][0:P, 0:X], br[:, :], ALU.add).then_inc(s_lg, 1)
            pipelined(dve, None, NT // 2, 1, 1, 0, step)
            dve.drain()
            halves_to_mean_var(nc, ch, st, mv2, half)
            v.tensor_scalar_add(r2[:, :], mv2[:, :, 1], EPS).then_inc(s_var2, 1)
            dve.wait_ge(s_std2, 1)
            v.reciprocal(r2[:, :], r2[:, :])

            def by_token(t2):
                return t2.unsqueeze(2).to_broadcast([P, NT, X])

            ch.link(v.reduce_max(red[:, :], lg[:, :, :], axis=AX))
            v.tensor_tensor(lg[:, :, :], lg[:, :, :], by_token(red[:, :]), ALU.subtract).then_inc(s_ex, 1)
            dve.wait_ge(s_gp, 4)
            v.tensor_copy(e_id[:, :], lane_i[:, :])
            ch.link(v.tensor_copy(blk_f[:, :], blk_i[:, :]))
            dve.wait_ge(s_exd, 1)
            ch.link(v.reduce_sum(tsum[:, :], lg[:, :, :], axis=AX))
            ch.link(v.reciprocal(tsum[:, :], tsum[:, :]))
            ch.link(v.tensor_tensor(lg[:, :, :], lg[:, :, :], by_token(tsum[:, :]), ALU.mult))
            ids = e_id[:, :].unsqueeze(1).to_broadcast([P, NT, X])
            for k, top in enumerate((top1, top2)):
                ch.link(v.reduce_max(top[:, :], lg[:, :, :], axis=AX))
                ch.link(v.tensor_tensor(m1[:, :, :], lg[:, :, :], by_token(top[:, :]), ALU.not_equal))
                ch.link(v.scalar_tensor_tensor(m1[:, :, :], m1[:, :, :], 2.0 * X, ids, ALU.mult, ALU.add))
                ch.link(v.tensor_reduce(red[:, :], m1[:, :, :], axis=AX, op=ALU.min))
                ch.link(v.tensor_tensor(pick[:, k], ids, by_token(red[:, :]), ALU.is_equal))
                if k == 0:
                    ch.link(v.scalar_tensor_tensor(lg[:, :, :], pick[:, k], -2.0, lg[:, :, :], ALU.mult, ALU.add))
            ch.link(v.tensor_tensor(tsum[:, :], top1[:, :], top2[:, :], ALU.add))
            ch.link(v.reciprocal(tsum[:, :], tsum[:, :]))
            v.tensor_tensor(gate[:, 0, :], top1[:, :], tsum[:, :], ALU.mult)
            v.tensor_tensor(gate[:, 1, :], top2[:, :], tsum[:, :], ALU.mult)
            ch.link(v.tensor_tensor(both[:, :, :].rearrange("p e t -> p t e"), pick[:, 0], pick[:, 1], ALU.add))
            ch.link(v.tensor_tensor_scan(run[:, :, :].rearrange("p e t -> p (e t)"), ones[:, :],
                                         both[:, :, :].rearrange("p e t -> p (e t)"), 0.0, ALU.mult, ALU.add))
            v.tensor_copy(off[:, 0:1], run[:, 0:1, NT - 1])
            ch.link(v.tensor_copy(lane[:, 0:1], run[:, 0:1, NT - 1]))
            v.tensor_tensor(lane[:, 1:X], run[:, 1:X, NT - 1], run[:, 0:X - 1, NT - 1], ALU.subtract).then_inc(s_lane, 1)
            dve.wait_ge(s_cnt, 1)
            ch.link(v.tensor_scalar(fill[:, :], p_c[0:P, 8:8 + X], 127.0, None, ALU.add))
            ch.link(v.tensor_copy(fill_i[:, :], fill[:, :]))
            ch.link(v.tensor_single_scalar(fill_i[:, :], fill_i[:, :], 7, op=ALU.logical_shift_right))
            ch.link(v.tensor_copy(fill[:, :], fill_i[:, :]))
            ch.link(v.tensor_scalar(fill[:, :], fill[:, :], 128.0, None, ALU.mult))
            ch.link(v.tensor_tensor_scan(end[:, :], ones[:, 0:X], fill[:, :], 0.0, ALU.mult, ALU.add))
            ch.link(v.tensor_tensor(off[:, :], end[:, :], fill[:, :], ALU.subtract))
            ch.link(v.tensor_tensor(off[:, :], off[:, :], p_c[0:P, 0:X], ALU.add))
            ch.link(v.tensor_tensor(off[:, 1:X], off[:, 1:X], run[:, 0:X - 1, NT - 1], ALU.subtract))
            ch.link(v.tensor_tensor(run[:, :, :], run[:, :, :], both[:, :, :], ALU.subtract))
            ch.link(v.tensor_tensor(run[:, :, :], run[:, :, :], off[:, :].unsqueeze(2).to_broadcast([P, X, NT]), ALU.add))
            for k in range(2):
                ch.link(v.tensor_tensor(m1[:, :, :], pick[:, k], run[:, :, :].rearrange("p e t -> p t e"), ALU.mult))
                ch.link(v.reduce_sum(red[:, :], m1[:, :, :], axis=AX))
                last = v.tensor_copy(pos[:, k, :], red[:, :])
                ch.link(last)
            v.memset(half[:, 0:1], 0.0).then_inc(s_pos, 1)
            ch.link(v.tensor_tensor(blk_g[:, :, :], blk_f[:, :].unsqueeze(2).to_broadcast([1, BLOCKS, X]),
                                    end[0:1, :].unsqueeze(1).to_broadcast([1, BLOCKS, X]), ALU.is_ge))
            ch.link(v.reduce_sum(blk_f[:, :], blk_g[:, :, :], axis=AX))
            ch.link(v.tensor_scalar(blk_f[:, :], blk_f[:, :], float(X - 1), None, ALU.min))
            ch.link(v.tensor_copy(blk[:, :], blk_f[:, :]))

            dve.wait_ge(s_keep, NT)

            def norm(i, first):
                for b in range(2):
                    t = 2 * i + b
                    if not first:
                        dve.wait_ge(s_sc[b], 32 * i)
                    v.tensor_scalar(xe[:, b, :], cols(x_sb, t), mv2[:, bass.ds(t, 1), 0], r2[:, bass.ds(t, 1)],
                                    ALU.subtract, ALU.mult).then_inc(s_xe, 1)
            loop2(dve, None, NT // 2, 0, norm)


def phase_experts(nc, phase, a, d, ident, blk, w1, b1, w2_lo):
    X = EXPERTS
    with phase("f") as (c, sb, ps, sm):
        w2_hi = sb("w2_hi", [128, KH - W2_LO, X * C])
        b2 = sb("b2", [128, X * C])
        xin = sb("xin", [128, 2, C])
        xt = sb("xt", [128, 2, C])
        hs = sb("hs", [128, 2, HID])
        ht = sb("ht", [128, HID])
        ys = sb("ys", [128, 2, C])
        p_x = ps("p_x")
        p_y = ps("p_y")
        p_h = [[ps(f"p_h{b}{q}") for q in range(2)] for b in range(2)]
        p_t = [ps(f"p_t{q}") for q in range(2)]
        s_w2, s_b, s_xtp, s_xt, s_h, s_hb, s_ge, s_tp, s_ta, s_tv, s_y, s_ys = (sm(n) for n in
            ("w2", "b", "xtp", "xt", "h", "hb", "ge", "tp", "ta", "tv", "y", "ys"))
        s_x = [sm(f"x{b}") for b in range(2)]
        s_st = [sm(f"st{b}", swdge=True) for b in range(2)]
        block = c.enter_context(nc.Block())
        xg = d["xg"].rearrange("(t p) c -> p t c", p=128)
        yg = d["yg"].rearrange("(t p) c -> p t c", p=128)

        def expert(eng, t):
            return eng.value_load(blk[0:1, bass.ds(t, 1)], min_val=0, max_val=X - 1)

        @block.sync
        def _(sp):
            def load(t, b):
                sp.dma_start(xin[:, b, :], xg[:, bass.ds(t, 1), :].rearrange("p o c -> p (o c)")).then_inc(s_x[b], 16)

            def step(i, first):
                for b in range(2):
                    t = 2 * i + b
                    if not first:
                        sp.wait_ge(s_xtp, t - 1)
                    load(t, b)
            step(0, True)
            for k in range(W2_LO, KH):
                sp.dma_start(w2_hi[:, k - W2_LO, :].rearrange("p (e c) -> p e c", e=X),
                             a["L0_ffn_W2"][:, k * 128:(k + 1) * 128, :].rearrange("e p c -> p e c")).then_inc(s_w2, 16)
            sp.dma_start(b2[:, :], a["L0_ffn_b2"].rearrange("(o e) h -> o (e h)", o=1).to_broadcast([128, X * C])).then_inc(s_b, 16)
            with sp.Fori(1, BLOCKS // 2) as i:
                step(i, False)
            sp.wait_ge(s_xtp, BLOCKS - 1)
            load(BLOCKS, 0)

        @block.gpsimd
        def _(pool):
            def step(i, first):
                for b in range(2):
                    t = 2 * i + b
                    pool.wait_ge(s_ys, t + 1)
                    pool.dma_start(yg[:, bass.ds(t, 1), :].rearrange("p o c -> p (o c)"), ys[:, b, :]).then_inc(s_st[b], 16)
            loop2(pool, None, BLOCKS // 2, 0, step)
            for b in range(2):
                pool.wait_ge(s_st[b], 16 * (BLOCKS // 2))

        @block.tensor
        def _(pe):
            def x_transposed(i, b):
                pe.wait_ge(s_x[b], 16 * (i + 1))
                for k in range(CH):
                    last = nc.tensor.transpose(p_x[:, k * 128:(k + 1) * 128], xin[:, b, k * 128:(k + 1) * 128], ident[:, :])
                last.then_inc(s_xtp, 1)

            def hidden(t, b, first):
                e = expert(pe, t)
                if not first:
                    pe.wait_ge(s_hb, t - 1)
                pe.wait_ge(s_xt, t + 1)
                for q in range(2):
                    for k in range(CH):
                        last = nc.tensor.matmul(p_h[b][q][:, :], xt[:, b, k * 128:(k + 1) * 128],
                                                w1[:, k, bass.ds(e * HID + q * 512, 512)], start=k == 0, stop=k == CH - 1)
                    last.then_inc(s_h, 1)

            def h_transposed(t, b, first):
                pe.wait_ge(s_ge, t + 1)
                if not first:
                    pe.wait_ge(s_ta, t)
                    pe.wait_ge(s_tv, t)
                for k in range(KH):
                    last = nc.tensor.transpose(p_t[k // 4][:, (k % 4) * 128:(k % 4 + 1) * 128],
                                               hs[:, b, k * 128:(k + 1) * 128], ident[:, :])
                last.then_inc(s_tp, 1)

            def down(t, b, first):
                e = expert(pe, t)
                pe.wait_ge(s_ta, t + 1)
                pe.wait_ge(s_tv, t + 1)
                if not first:
                    pe.wait_ge(s_ys, t)
                for k in range(KH):
                    last = nc.tensor.matmul(p_y[:, 0:C], ht[:, k * 128:(k + 1) * 128],
                                            (w2_lo[:, k] if k < W2_LO else w2_hi[:, k - W2_LO])[:, bass.ds(e * C, C)],
                                            start=k == 0, stop=k == KH - 1)
                last.then_inc(s_y, 1)

            x_transposed(0, 0)

            def step(i, first):
                for b in range(2):
                    t = 2 * i + b
                    if not (first and b == 0):
                        h_transposed(t - 1, 1 - b, first)
                    hidden(t, b, first)
                    x_transposed(i + b, 1 - b)
                    if not (first and b == 0):
                        down(t - 1, 1 - b, first)
            pe.wait_ge(s_w2, 16 * (KH - W2_LO))
            loop2(pe, None, BLOCKS // 2, 0, step)
            h_transposed(BLOCKS - 1, 1, False)
            down(BLOCKS - 1, 1, False)

        @block.scalar
        def _(act):
            def x_copy(t, b):
                act.wait_ge(s_xtp, t + 1)
                nc.scalar.activation(xt[:, b, :], p_x[:, 0:C], ACT.Copy).then_inc(s_xt, 1)

            def h_copy(t):
                act.wait_ge(s_tp, t + 1)
                nc.scalar.activation(ht[:, 0:512], p_t[0][:, :], ACT.Copy).then_inc(s_ta, 1)

            x_copy(0, 0)

            def step(i, first):
                for b in range(2):
                    t = 2 * i + b
                    if not (first and b == 0):
                        if not (first and b == 1):
                            act.wait_ge(s_y, t - 1)
                        h_copy(t - 1)
                    x_copy(t + 1, 1 - b)
                    act.wait_ge(s_hb, t + 1)
                    nc.scalar.activation(hs[:, b, :], hs[:, b, :], ACT.Gelu).then_inc(s_ge, 1)
            loop2(act, None, BLOCKS // 2, 0, step)
            act.wait_ge(s_y, BLOCKS - 1)
            h_copy(BLOCKS - 1)

        @block.vector
        def _(dve):
            v = nc.vector
            dve.wait_ge(s_b, 16)

            def h_copy(t, first):
                dve.wait_ge(s_tp, t + 1)
                if not first:
                    dve.wait_ge(s_y, t)
                v.tensor_copy(ht[:, 512:], p_t[1][:, :]).then_inc(s_tv, 1)

            def result(t, b, i, first):
                e = expert(dve, t)
                dve.wait_ge(s_y, t + 1)
                if not first:
                    dve.wait_ge(s_st[b], 16 * i)
                v.tensor_tensor(ys[:, b, :], p_y[:, 0:C], b2[:, bass.ds(e * C, C)], ALU.add).then_inc(s_ys, 1)

            def step(i, first):
                for b in range(2):
                    t = 2 * i + b
                    if not (first and b == 0):
                        h_copy(t - 1, first)
                    e = expert(dve, t)
                    if not first:
                        dve.wait_ge(s_tp, t - 1)
                    for q in range(2):
                        dve.wait_ge(s_h, 2 * t + (q + 1))
                        last = v.tensor_tensor(hs[:, b, q * 512:(q + 1) * 512], p_h[b][q][:, :],
                                               b1[:, bass.ds(e * HID + q * 512, 512)], ALU.add)
                    last.then_inc(s_hb, 1)
                    if not (first and b == 0):
                        result(t - 1, 1 - b, i + b - 1 if not first else 0, first)
            loop2(dve, None, BLOCKS // 2, 0, step)
            h_copy(BLOCKS - 1, False)
            result(BLOCKS - 1, 1, BLOCKS // 2 - 1, False)


def phase_combine(nc, phase, d, out, pos, gate):
    with phase("o") as (c, sb, ps, sm):
        x2 = sb("x2", [P, NT, C])
        ibuf = sb("ibuf", [P, 2, 2], I32)
        y = sb("y", [P, 2, 2, C])
        s_x, s_ib, s_one, s_out, s_done = (sm(n) for n in ("x", "ib", "one", "out", "done"))
        s_y = [sm(f"y{b}", swdge=True) for b in range(2)]
        block = c.enter_context(nc.Block())

        @block.sync
        def _(sp):
            sp.dma_start(x2[:, :, :], d["x2"].rearrange("(p t) c -> p t c", t=NT)).then_inc(s_x, 16)
            sp.wait_ge(s_out, NT)
            sp.dma_start(out.rearrange("(p t) c -> p t c", t=NT), x2[:, :, :]).then_inc(s_done, 16)
            sp.wait_ge(s_done, 16)

        @block.gpsimd
        def _(pool):
            def step(i, first):
                for b in range(2):
                    t = 2 * i + b
                    if not first:
                        pool.wait_ge(s_out, t - 1)
                    nc.gpsimd.tensor_copy(ibuf[:, b, :], pos[:, :, bass.ds(t, 1)].rearrange("p k o -> p (k o)")).then_inc(s_ib, 1)
                    pool.wait_ge(s_ib, t + 1)
                    pool.nop(nofuse=True)
                    for k in range(2):
                        nc.gpsimd.indirect_dma_start(out=y[:, b, k, :], out_offset=None, in_=d["yg"][:, :],
                                                     in_offset=bass.IndirectOffsetOnAxis(ap=ibuf[:, b, k:k + 1], axis=0)).then_inc(s_y[b], 16)
            loop2(pool, None, NT // 2, 0, step)

        @block.vector
        def _(dve):
            dve.wait_ge(s_x, 16)

            def step(i, first):
                for b in range(2):
                    t = 2 * i + b
                    row = x2[:, bass.ds(t, 1), :].rearrange("p o c -> p (o c)")
                    dve.wait_ge(s_y[b], 32 * (i + 1))
                    nc.vector.scalar_tensor_tensor(row, y[:, b, 0, :], gate[:, 0, bass.ds(t, 1)], row, ALU.mult, ALU.add).then_inc(s_one, 1)
                    dve.wait_ge(s_one, t + 1)
                    nc.vector.scalar_tensor_tensor(row, y[:, b, 1, :], gate[:, 1, bass.ds(t, 1)], row, ALU.mult, ALU.add).then_inc(s_out, 1)
            loop2(dve, None, NT // 2, 0, step)


_INS = ['x', 'src', 'dst', 'L0_gnn_Wb', 'L0_gnn_Wc', 'L0_gnn_bc', 'L0_gnn_conv_bias', 'L0_gnn_bn_gamma',
        'L0_gnn_bn_beta', 'L0_gnn_fc_W', 'L0_gnn_fc_b', 'L0_mix_w_qkv', 'L0_mix_b_qkv', 'L0_mix_kln_g',
        'L0_mix_kln_b', 'L0_mix_vln_g', 'L0_mix_vln_b', 'L0_mix_w1', 'L0_mix_b1', 'L0_mix_w2', 'L0_mix_b2',
        'L0_ffn_Wr', 'L0_ffn_br', 'L0_ffn_ln_g', 'L0_ffn_ln_b', 'L0_ffn_W1', 'L0_ffn_b1', 'L0_ffn_W2',
        'L0_ffn_b2']


def kernel(**inputs):
    import numpy as _np
    import concourse.bacc as _bacc
    from concourse import mybir as _mybir
    from concourse.bass_utils import run_bass_kernel_spmd as _run

    nc = _bacc.Bacc("TRN2", target_bir_lowering=False, num_devices=1)
    arrays, args = {}, {}
    for name in _INS:
        array = _np.ascontiguousarray(inputs[name])
        arrays[f"in_{name}"] = array
        args[name] = nc.dram_tensor(f"in_{name}", array.shape, _mybir.dt.from_np(array.dtype), kind="ExternalInput").ap()
    out = nc.dram_tensor("out_0", (N, C), _mybir.dt.float32, kind="ExternalOutput").ap()
    build(nc, args, out)
    result = _run(nc, [arrays], core_ids=[0])
    return result.results[0]["out_0"]
```

```python
import concourse.bass as bass
from concourse import mybir
from contextlib import ExitStack, contextmanager

FP32 = mybir.dt.float32
BF16 = mybir.dt.bfloat16
I32 = mybir.dt.int32
ALU = mybir.AluOpType
ACT = mybir.ActivationFunctionType
AX = mybir.AxisListType.X

N = 6250
E = 100000
C = 256
CH = C // 128
P = 125
NT = N // P
L = 3
HEADS = 8
BASES = 4
HC = C // HEADS
BW = BASES * HC
TW = L * BW
EPS = 1e-5
SLOPE = 0.01

NG = 64
SET = 4
SETS = 25
GROUPS = SET * SETS
NPAD = NG * GROUPS
HIST_A = NPAD // 128
SLOTS = 48
CHUNKS = SLOTS // 2
STEP = 2
BINS = 16
RUN_ROWS = 128 * 784
BIG = 3.0e38

EXPERTS = 8
HID = 1024
BLOCKS = -(-2 * N // 128) + EXPERTS
ROWS = BLOCKS * 128
KH = HID // 128
W2_LO = NT * C // (EXPERTS * C)


class Chain:

    def __init__(self, eng, sem):
        self.eng, self.sem, self.base, self.n = eng, sem, 0, 0

    def link(self, ins):
        self.mark(ins)
        self.wait()

    def mark(self, ins):
        ins.then_inc(self.sem, 1)
        self.n += 1

    def wait(self):
        self.eng.wait_ge(self.sem, self.base + self.n)

    @contextmanager
    def loop(self, i, first, per):
        n0 = self.n
        self.base = (i - first) * per
        yield
        assert self.n - n0 == per, (self.n - n0, per)
        self.n = n0
        self.base = 0

    def looped(self, steps, per):
        self.n += steps * per


def loop2(eng, chain, pairs, per, body):
    n0 = chain.n if chain else 0
    body(0, True)
    if chain:
        assert chain.n - n0 == per, ("links of a step", chain.n - n0, per)
    with eng.Fori(1, pairs) as i:
        if chain:
            with chain.loop(i, 1, per):
                body(i, False)
        else:
            body(i, False)
    if chain:
        chain.looped(pairs - 1, per)


def pipelined(eng, chain, pairs, head, tail, per, body):
    def at(i):
        return lambda b, k: 0 <= 2 * i + b + k < 2 * pairs
    for i in range(head):
        body(i, at(i))
    with eng.Fori(head, pairs - tail) as i:
        if chain:
            with chain.loop(i, head, per):
                body(i, lambda b, k: True)
        else:
            body(i, lambda b, k: True)
    if chain:
        chain.looped(pairs - head - tail, per)
    for i in range(pairs - tail, pairs):
        body(i, at(i))


def halves_to_mean_var(nc, ch, st, mv, half):
    dve = nc.vector
    ch.link(dve.tensor_tensor(half[:, :], st[:, :, 1], st[:, :, 4], ALU.subtract))
    ch.link(dve.tensor_scalar(half[:, :], half[:, :], 0.5, None, ALU.mult))
    ch.link(dve.tensor_tensor(mv[:, :, 0], st[:, :, 4], half[:, :], ALU.add))
    ch.link(dve.tensor_tensor(half[:, :], half[:, :], half[:, :], ALU.mult))
    ch.link(dve.tensor_tensor(mv[:, :, 1], st[:, :, 2], st[:, :, 5], ALU.add))
    ch.link(dve.scalar_tensor_tensor(mv[:, :, 1], mv[:, :, 1], 1.0 / C, half[:, :], ALU.mult, ALU.add))


def build(nc, a, out):
    def dram(name, shape, dt=FP32):
        return nc.dram_tensor(name, shape, dt, kind="Internal").ap()

    d = dict(
        order=dram("order_d", [NPAD, 4]), rank=dram("rank_d", [NPAD], I32), dinv=dram("dinv_d", [NPAD]),
        srcp=dram("srcp_d", [RUN_ROWS + 64], I32), runs=dram("runs_d", [RUN_ROWS, SLOTS], I32),
        tab=dram("tab_d", [NPAD, TW + 1]), xnt=dram("xnt_d", [NT, 128, CH * P]),
        cw=dram("cw_d", [N, TW]),
        agg=dram("agg_d", [NPAD + SET * NG, 4, TW]), ht=dram("ht_d", [NT, 128, 2 * L * P]),
        xg=dram("xg_d", [ROWS + 128, C]), yg=dram("yg_d", [ROWS, C]), x2=dram("x2_d", [N, C]),
    )

    top = ExitStack()

    @contextmanager
    def phase(tag, clear=False):
        with ExitStack() as c:
            sems = []

            def sb(name, shape, dt=FP32):
                return c.enter_context(nc.sbuf_tensor(f"{tag}_{name}", shape, dt))

            def ps(name, shape=(128, 512), dt=FP32):
                return c.enter_context(nc.psum_tensor(f"{tag}_{name}", list(shape), dt))

            def sm(name, swdge=False):
                if swdge:
                    return top.enter_context(nc.semaphore(f"{tag}_{name}"))
                sems.append(c.enter_context(nc.semaphore(f"{tag}_{name}")))
                return sems[-1]

            with ExitStack() as work:
                yield work, sb, ps, sm
            if clear:
                with nc.Block() as block:
                    @block.sync
                    def _(sp):
                        for s in sems:
                            sp.sem_clear(s)

    with top:
        def keep(stack, name, shape, dt=FP32):
            return stack.enter_context(nc.sbuf_tensor(name, shape, dt))

        ident = keep(top, "ident", [128, 128])
        pos = keep(top, "pos", [P, 2, NT], I32)
        gate = keep(top, "gate", [P, 2, NT])
        blk = keep(top, "blk", [1, BLOCKS], I32)
        pairs = keep(top, "pairs", [1, 1], I32)
        with ExitStack() as nodes:
            x_mem = keep(nodes, "x_mem", [128, NT * C])
            x_sb = x_mem[0:P, :].rearrange("p (t c) -> p t c", c=C)
            xst = keep(nodes, "x_stats", [P, NT, 6])
            with ExitStack() as early:
                mv = keep(early, "mv", [P, NT, 2])
                rstd = keep(early, "rstd", [P, NT])
                kvbd = keep(early, "kvbd", [128, CH, 128])
                rank_t = keep(early, "rank_t", [128, HIST_A], I32)
                node_row = keep(early, "node_row", [128, HIST_A, 4])
                phase_histogram(nc, phase, a, d, ident, x_sb, rank_t, node_row)
                phase_nodes(nc, phase, a, d, ident, x_sb, mv, rstd, kvbd, rank_t, node_row)
                phase_edges(nc, phase, a, d, ident)
                stats = keep(early, "bn_stats", [128, 2 * L, NT, 6])
                mixw = mix_weights(lambda name, shape: keep(early, name, shape))
                phase_conv(nc, phase, a, d, ident, stats, mixw)
                phase_mix(nc, phase, a, d, ident, x_sb, mv, rstd, kvbd, stats, xst, mixw)
            w1 = keep(nodes, "w1", [128, CH, EXPERTS * HID])
            b1 = keep(nodes, "b1", [128, EXPERTS * HID])
            w2_lo = x_mem[:, 0:W2_LO * EXPERTS * C].rearrange("p (k n) -> p k n", k=W2_LO)
            phase_route(nc, phase, a, d, ident, x_sb, xst, pos, gate, blk, pairs, w1, b1, w2_lo)
            phase_experts(nc, phase, a, d, ident, blk, pairs, w1, b1, w2_lo)
        phase_combine(nc, phase, d, out, pos, gate)


def phase_histogram(nc, phase, a, d, ident, x_sb, rank_t, node_row):
    COLS = E // P
    W = 16
    PAIRS = COLS // W // 2
    with phase("h", clear=True) as (c, sb, ps, sm):
        dst = sb("dst", [P, COLS], I32)
        hi_i = sb("hi_i", [P, COLS], I32)
        lo_i = sb("lo_i", [P, COLS], I32)
        hi = sb("hi", [P, COLS], BF16)
        lo = sb("lo", [P, COLS], BF16)
        iota_i = sb("iota_i", [P, 128], I32)
        iota = sb("iota", [P, 128], BF16)
        iota_f = sb("iota_f", [HIST_A, BINS])
        one_hi = sb("one_hi", [P, 2, W, HIST_A], BF16)
        diff = sb("diff", [P, 2, W, HIST_A], BF16)
        unit = sb("unit", [P, 1])
        one_lo = sb("one_lo", [P, 2, W, 128], BF16)
        zero_b = sb("zero_b", [P, 128], BF16)
        zero_i = sb("zero_i", [1, 512], I32)
        zero_f = sb("zero_f", [(NPAD - N) // 2, 2 * (TW + 1)])
        big = sb("big", [128, 2, TW])
        ones = sb("ones", [HIST_A, 128])
        below = sb("below", [HIST_A, HIST_A])
        cnt = sb("cnt", [HIST_A, 128])
        incl = sb("incl", [HIST_A, 128])
        deg = sb("deg", [HIST_A, 128])
        first = sb("first", [HIST_A, 128])
        bin_f = sb("bin_f", [HIST_A, 128])
        bin_i = sb("bin_i", [HIST_A, 128], I32)
        onehot = sb("onehot", [HIST_A, BINS, 128])
        run = sb("run", [HIST_A, BINS, 128])
        ones_w = sb("ones_w", [HIST_A, BINS * 128])
        bins = sb("bins", [HIST_A, BINS])
        lane = sb("lane", [HIST_A, BINS])
        off = sb("off", [HIST_A, BINS])
        rank = sb("rank", [HIST_A, 128])
        rank_i = sb("rank_i", [HIST_A, 128], I32)
        node_i = sb("node_i", [128, HIST_A], I32)
        p_cnt = ps("p_cnt")
        p_off = ps("p_off")
        p_bin = ps("p_bin")
        p_tr = ps("p_tr")
        s_dst, s_fill, s_pad, s_run, s_gp, s_dve = (sm(n) for n in
            ("dst", "fill", "pad", "run", "gp", "dve"))
        s_init = sm("init", swdge=True)
        s_one, s_used, s_cnt, s_tot, s_off, s_res, s_store, s_sqrt = (sm(n) for n in
            ("one", "used", "cnt", "tot", "off", "res", "store", "sqrt"))
        s_rank, s_lane, s_cum, s_tr, s_first = (sm(n) for n in ("rank", "lane", "cum", "tr", "first"))
        s_hi, s_diff, s_sqr, s_onehi, s_x = (sm(n) for n in ("hi", "diff", "sqr", "onehi", "x"))
        block = c.enter_context(nc.Block())

        @block.sync
        def _(sp):
            sp.dma_start(dst[:, :], a["dst"].rearrange("(p k) -> p k", p=P)).then_inc(s_dst, 16)
            sp.dma_start(d["srcp"][1:E + 1].rearrange("(p k) -> p k", p=P),
                         a["src"].rearrange("(p k) -> p k", p=P)).then_inc(s_pad, 16)
            sp.wait_ge(s_fill, 1)
            sp.dma_start(d["srcp"][0:1].rearrange("(o k) -> o k", o=1), zero_i[0:1, 0:1]).then_inc(s_pad, 16)
            tail = RUN_ROWS + 64 - E - 1
            sp.dma_start(d["srcp"][E + 1:].rearrange("(o k) -> o k", o=1), zero_i[0:1, 0:tail]).then_inc(s_pad, 16)
            sp.wait_ge(s_pad, 48)
            runs_in = bass.AP(d["srcp"].tensor, 0, [[RUN_ROWS // 128, 128], [1, RUN_ROWS // 128], [1, SLOTS]])
            sp.dma_start(d["runs"].rearrange("(p r) s -> p r s", p=128), runs_in).then_inc(s_run, 16)
            sp.dma_start(x_sb[:, :, :], a["x"].rearrange("(p t) c -> p t c", t=NT)).then_inc(s_x, 16)
            sp.wait_ge(s_res, 1)
            sp.dma_start(d["dinv"].rearrange("(a b) -> a b", b=128), deg[:, :]).then_inc(s_store, 16)
            sp.wait_ge(s_rank, 1)
            sp.dma_start(d["rank"].rearrange("(a b) -> a b", b=128), rank_i[:, :]).then_inc(s_store, 16)
            sp.wait_ge(s_store, 32)
            sp.wait_ge(s_run, 16)
            sp.wait_ge(s_x, 16)

        @block.gpsimd
        def _(pool):
            nc.gpsimd.memset(zero_i[:, :], 0).then_inc(s_fill, 1)
            nc.gpsimd.iota(iota_i[:, :], pattern=[[1, 128]], base=0, channel_multiplier=0).then_inc(s_gp, 1)
            nc.gpsimd.iota(node_i[:, :], pattern=[[128, HIST_A]], base=0, channel_multiplier=1).then_inc(s_gp, 1)
            nc.gpsimd.memset(ident[:, :], 0.0).then_inc(s_gp, 1)
            nc.gpsimd.memset(below[:, :], 1.0).then_inc(s_gp, 1)
            pool.wait_ge(s_gp, 4)
            nc.gpsimd.affine_select(out=ident[:, :], in_=ident[:, :], compare_op=ALU.not_equal, fill=1.0,
                                    base=0, pattern=[[-1, 128]], channel_multiplier=1).then_inc(s_gp, 1)
            nc.gpsimd.affine_select(out=below[:, :], in_=below[:, :], compare_op=ALU.is_gt, fill=0.0,
                                    base=0, pattern=[[1, HIST_A]], channel_multiplier=-1).then_inc(s_gp, 1)
            nc.gpsimd.memset(zero_f[:, :], 0.0).then_inc(s_gp, 1)
            nc.gpsimd.memset(big[:, 0, :], 0.0).then_inc(s_gp, 1)
            nc.gpsimd.memset(big[:, 1, :], -BIG).then_inc(s_gp, 1)
            nc.gpsimd.memset(unit[:, :], 1.0).then_inc(s_gp, 1)
            pool.wait_ge(s_gp, 10)
            pool.dma_start(d["tab"][N:NPAD, :].rearrange("(p r) w -> p (r w)", r=2), zero_f[:, :]).then_inc(s_init, 16)
            for g in range(0, SET * NG, 128):
                for half in range(2):
                    for k in range(2):
                        pool.dma_start(d["agg"][NPAD + g:NPAD + g + 128, 2 * half + k, :],
                                       big[:, half, :]).then_inc(s_init, 16)

            def differences(i, first_step):
                for b in range(2):
                    t = 2 * i + b
                    if first_step:
                        pool.wait_ge(s_hi, 1)
                    else:
                        pool.wait_ge(s_sqr, t - 1)
                    nc.gpsimd.tensor_tensor(
                        diff[:, b], hi[:, bass.ds(t * W, W)].unsqueeze(2).to_broadcast([P, W, HIST_A]),
                        iota[:, 0:HIST_A].unsqueeze(1).to_broadcast([P, W, HIST_A]), ALU.subtract).then_inc(s_diff, 1)
            loop2(pool, None, PAIRS, 0, differences)
            pool.wait_ge(s_init, 16 * (1 + 4 * (SET * NG // 128)))

        @block.vector
        def _(dve):
            ch = Chain(dve, s_dve)
            nc.vector.memset(ones[:, :], 1.0)
            nc.vector.memset(zero_b[:, :], 0.0)
            dve.wait_ge(s_gp, 2)
            nc.vector.tensor_copy(iota[:, :], iota_i[:, :])
            nc.vector.tensor_copy(iota_f[:, :], iota_i[0:HIST_A, 0:BINS])
            dve.wait_ge(s_dst, 16)
            nc.vector.tensor_single_scalar(hi_i[:, :], dst[:, :], 7, op=ALU.logical_shift_right)
            ch.link(nc.vector.tensor_single_scalar(lo_i[:, :], dst[:, :], 127, op=ALU.bitwise_and))
            nc.vector.tensor_copy(hi[:, :], hi_i[:, :]).then_inc(s_hi, 1)
            ch.link(nc.vector.tensor_copy(lo[:, :], lo_i[:, :]))

            def step(i, first_step):
                for b in range(2):
                    t = 2 * i + b
                    if not first_step:
                        dve.wait_ge(s_used, t - 1)
                    cols = bass.ds(t * W, W)
                    nc.vector.tensor_tensor(
                        one_lo[:, b], lo[:, cols].unsqueeze(2).to_broadcast([P, W, 128]),
                        iota[:, :].unsqueeze(1).to_broadcast([P, W, 128]), ALU.is_equal).then_inc(s_one, 1)
            loop2(dve, None, PAIRS, 0, step)
            dve.wait_ge(s_cnt, 1)
            ch.link(nc.vector.tensor_copy(cnt[:, :], p_cnt[0:HIST_A, 0:128]))
            nc.vector.tensor_tensor_scan(incl[:, :], ones[:, :], cnt[:, :], 0.0, ALU.mult, ALU.add).then_inc(s_tot, 1)
            ch.link(nc.vector.tensor_scalar_add(deg[:, :], cnt[:, :], 1.0))
            nc.vector.reciprocal(deg[:, :], deg[:, :]).then_inc(s_sqrt, 1)
            dve.wait_ge(s_tot, 1)
            ch.link(nc.vector.tensor_tensor(first[:, :], incl[:, :], cnt[:, :], ALU.subtract))
            dve.wait_ge(s_off, 1)
            nc.vector.tensor_scalar(first[:, :], first[:, :], p_off[0:HIST_A, 0:1], None, ALU.add).then_inc(s_first, 1)
            v = nc.vector
            v.memset(ones_w[:, :], 1.0)
            ch.link(v.tensor_scalar(bin_f[:, :], cnt[:, :], 2.0 * STEP, None, ALU.add))
            ch.link(v.tensor_copy(bin_i[:, :], bin_f[:, :]))
            ch.link(v.tensor_single_scalar(bin_i[:, :], bin_i[:, :], 2, op=ALU.logical_shift_right))
            ch.link(v.tensor_copy(bin_f[:, :], bin_i[:, :]))
            ch.link(v.tensor_scalar(bin_f[:, :], bin_f[:, :], float(BINS), -1.0, ALU.min, ALU.mult))
            ch.link(v.tensor_scalar(bin_f[:, :], bin_f[:, :], float(BINS), None, ALU.add))
            ids = iota_f[:, 0:BINS].unsqueeze(2).to_broadcast([HIST_A, BINS, 128])
            ch.link(v.tensor_tensor(onehot[:, :, :], bin_f[:, :].unsqueeze(1).to_broadcast([HIST_A, BINS, 128]), ids, ALU.is_equal))
            ch.link(v.tensor_tensor_scan(run[:, :, :].rearrange("a e b -> a (e b)"), ones_w[:, :],
                                         onehot[:, :, :].rearrange("a e b -> a (e b)"), 0.0, ALU.mult, ALU.add))
            v.tensor_copy(lane[:, 0:1], run[:, 0:1, 127])
            v.tensor_tensor(lane[:, 1:], run[:, 1:, 127], run[:, 0:BINS - 1, 127], ALU.subtract).then_inc(s_lane, 1)
            dve.wait_ge(s_cum, 1)
            ch.link(v.tensor_copy(bins[:, :], p_bin[0:HIST_A, BINS:2 * BINS]))
            ch.link(v.tensor_tensor_scan(off[:, :], ones[:, 0:BINS], bins[:, :], 0.0, ALU.mult, ALU.add))
            ch.link(v.tensor_tensor(off[:, :], off[:, :], bins[:, :], ALU.subtract))
            ch.link(v.tensor_tensor(off[:, :], off[:, :], p_bin[0:HIST_A, 0:BINS], ALU.add))
            ch.link(v.tensor_tensor(off[:, 1:], off[:, 1:], run[:, 0:BINS - 1, 127], ALU.subtract))
            ch.link(v.tensor_tensor(run[:, :, :], run[:, :, :], onehot[:, :, :], ALU.subtract))
            ch.link(v.tensor_tensor(run[:, :, :], run[:, :, :], off[:, :].unsqueeze(2).to_broadcast([HIST_A, BINS, 128]), ALU.add))
            ch.link(v.tensor_tensor(run[:, :, :], run[:, :, :], onehot[:, :, :], ALU.mult))
            ch.link(v.reduce_sum(rank[:, :], run[:, :, :].rearrange("a e b -> a b e"), axis=AX))
            v.tensor_copy(rank_i[:, :], rank[:, :]).then_inc(s_rank, 1)
            dve.wait_ge(s_tr, 1)
            v.tensor_copy(rank_t[:, :], p_tr[:, 0:HIST_A])
            v.tensor_copy(node_row[:, :, 0], p_tr[:, 64:64 + HIST_A])
            v.tensor_copy(node_row[:, :, 1], p_tr[:, 128:128 + HIST_A])
            v.tensor_copy(node_row[:, :, 3], node_i[:, :])
            v.tensor_copy(node_row[:, :, 2], node_i[:, :])

        @block.scalar
        def _(act):
            act.wait_ge(s_gp, 10)

            def ones_hi(i, first_step):
                for b in range(2):
                    t = 2 * i + b
                    act.wait_ge(s_diff, t + 1)
                    if not first_step:
                        act.wait_ge(s_used, t - 1)
                    nc.scalar.activation(one_hi[:, b], diff[:, b], ACT.Square).then_inc(s_sqr, 1)
                    act.wait_ge(s_sqr, t + 1)
                    nc.scalar.activation(one_hi[:, b], one_hi[:, b], ACT.Relu, bias=unit[:, 0:1], scale=-1.0).then_inc(s_onehi, 1)
            loop2(act, None, PAIRS, 0, ones_hi)
            act.wait_ge(s_sqrt, 1)
            nc.scalar.activation(deg[:, :], deg[:, :], ACT.Sqrt).then_inc(s_res, 1)

        @block.tensor
        def _(pe):
            def step(i, first_step):
                for b in range(2):
                    t = 2 * i + b
                    pe.wait_ge(s_one, t + 1)
                    pe.wait_ge(s_onehi, t + 1)
                    for w in range(W):
                        last = nc.tensor.matmul(p_cnt[0:HIST_A, 0:128], one_hi[:, b, w, :], one_lo[:, b, w, :],
                                                start=first_step and b == 0 and w == 0, stop=False)
                    last.then_inc(s_used, 1)
            loop2(pe, None, PAIRS, 0, step)
            nc.tensor.matmul(p_cnt[0:HIST_A, 0:128], zero_b[:, 0:HIST_A], zero_b[:, :], start=False,
                             stop=True).then_inc(s_cnt, 1)
            pe.wait_ge(s_tot, 1)
            pe.wait_ge(s_gp, 6)
            nc.tensor.matmul(p_off[0:HIST_A, 0:1], below[:, :], incl[:, 127:128], start=True,
                             stop=True).then_inc(s_off, 1)
            pe.wait_ge(s_lane, 1)
            nc.tensor.matmul(p_bin[0:HIST_A, 0:BINS], below[:, :], lane[:, :], start=True, stop=True)
            nc.tensor.matmul(p_bin[0:HIST_A, BINS:2 * BINS], ones[:, 0:HIST_A], lane[:, :], start=True, stop=True).then_inc(s_cum, 1)
            pe.wait_ge(s_first, 1)
            nc.tensor.transpose(p_tr[:, 64:64 + HIST_A], cnt[:, :], ident[0:HIST_A, 0:HIST_A])
            nc.tensor.transpose(p_tr[:, 128:128 + HIST_A], first[:, :], ident[0:HIST_A, 0:HIST_A])
            pe.wait_ge(s_rank, 1)
            nc.tensor.transpose(p_tr[:, 0:HIST_A], rank[:, :], ident[0:HIST_A, 0:HIST_A]).then_inc(s_tr, 1)


def phase_nodes(nc, phase, a, d, ident, x_sb, mv, rstd, kvbd, rank_t, node_row):
    KV = 2 * C
    G = 2 * HEADS
    with phase("n", clear=True) as (c, sb, ps, sm):
        wb = sb("wb", [128, CH, L, BW])
        wc = sb("wc", [128, CH, L, 128])
        cw = sb("cw", [P, 2, TW])
        wqkv = sb("wqkv", [128, CH, 3 * C])
        b_kv = sb("b_kv", [P, 3 * C])
        ln_g = sb("ln_g", [P, 2, HC])
        ln_b = sb("ln_b", [P, 2, HC])
        dinv = sb("dinv", [P, NT])
        st = sb("st", [P, NT, 6])
        std = sb("std", [P, NT])
        half = sb("half", [P, NT])
        xn = sb("xn", [P, 2, C])
        xt = sb("xt", [128, 2, CH * P])
        rows = sb("rows", [P, 2, TW + 1])
        kv = sb("kv", [P, 2, KV])
        sq = sb("sq", [P, 2, KV])
        gs = sb("gs", [P, 2, G])
        gv = sb("gv", [P, 2, G])
        gd = sb("gd", [P, 2, G])
        kvg = sb("kvg", [P, 2, KV])
        kn = sb("kn", [P, 2, 2, C])
        zero = sb("zero", [P, C])
        p_t = [ps(f"p_t{b}") for b in range(2)]
        p_b = [ps(f"p_b{b}") for b in range(2)]
        p_k = [ps(f"p_k{b}") for b in range(2)]
        p_kv = ps("p_kv")
        p_c = ps("p_c")
        s_w, s_bias, s_dve, s_pool = (sm(n) for n in ("w", "bias", "dve", "pool"))
        s_var, s_std, s_xn, s_tp, s_xt, s_bp, s_kp, s_row = (sm(n) for n in
            ("var", "std", "xn", "tp", "xt", "bp", "kp", "row"))
        s_sq, s_cen, s_gd, s_gstd, s_nrm, s_kn, s_kva, s_zero, s_din, s_end, s_kvd = (sm(n) for n in
            ("sq", "cen", "gd", "gstd", "nrm", "kn", "kva", "zero", "din", "end", "kvd"))
        s_order = sm("order", swdge=True)
        s_cp, s_cr, s_rec = (sm(n) for n in ("cp", "cr", "rec"))
        s_cww = [sm(f"cww{b}") for b in range(2)]
        s_tabw = [sm(f"tabw{b}") for b in range(2)]
        s_xtw = [sm(f"xtw{b}") for b in range(2)]
        block = c.enter_context(nc.Block())
        cws = d["cw"].rearrange("(p t) w -> p t w", t=NT)
        tab = d["tab"][0:N, :].rearrange("(p t) w -> p t w", t=NT)

        @block.sync
        def _(sp):
            for k in range(CH):
                sp.dma_start(wb[:, k], a["L0_gnn_Wb"][:, k * 128:(k + 1) * 128, :].rearrange("l p w -> p l w")).then_inc(s_w, 16)
                sp.dma_start(wc[:, k], a["L0_gnn_Wc"][:, k * 128:(k + 1) * 128, :].rearrange("l p w -> p l w")).then_inc(s_w, 16)
                sp.dma_start(wqkv[:, k], a["L0_mix_w_qkv"][k * 128:(k + 1) * 128, :]).then_inc(s_w, 16)
            sp.dma_start(b_kv[:, :], a["L0_mix_b_qkv"].rearrange("(o n) -> o n", o=1).to_broadcast([P, 3 * C])).then_inc(s_bias, 16)
            for j, n in enumerate("kv"):
                sp.dma_start(ln_g[:, j, :], a[f"L0_mix_{n}ln_g"].rearrange("(o n) -> o n", o=1).to_broadcast([P, HC])).then_inc(s_bias, 16)
                sp.dma_start(ln_b[:, j, :], a[f"L0_mix_{n}ln_b"].rearrange("(o n) -> o n", o=1).to_broadcast([P, HC])).then_inc(s_bias, 16)
            sp.dma_start(dinv[:, :], d["dinv"][0:N].rearrange("(p t) -> p t", t=NT)).then_inc(s_din, 16)

            def store_weights(t, b):
                sp.wait_ge(s_cr, t + 1)
                sp.dma_start(cws[:, bass.ds(t, 1), :].rearrange("p o w -> p (o w)"), cw[:, b]).then_inc(s_cww[b], 16)

            def step(i, first_step):
                for b in range(2):
                    t = 2 * i + b
                    sp.wait_ge(s_xt, t + 1)
                    sp.dma_start(d["xnt"][bass.ds(t, 1)].rearrange("o p c -> (o p) c"), xt[:, b]).then_inc(s_xtw[b], 16)
                    sp.wait_ge(s_row, t + 1)
                    sp.dma_start(tab[:, bass.ds(t, 1), :].rearrange("p o w -> p (o w)"), rows[:, b]).then_inc(s_tabw[b], 16)
                    if not (first_step and b == 0):
                        store_weights(t - 1, 1 - b)
            loop2(sp, None, NT // 2, 0, step)
            store_weights(NT - 1, 1)
            for b in range(2):
                sp.wait_ge(s_xtw[b], 16 * (NT // 2))
                sp.wait_ge(s_tabw[b], 16 * (NT // 2))
                sp.wait_ge(s_cww[b], 16 * (NT // 2))

        @block.vector
        def _(dve):
            ch = Chain(dve, s_dve)
            nc.vector.memset(zero[:, :], 0.0)
            nc.vector.memset(kn[:, :, :, :], 0.0).then_inc(s_zero, 1)
            with dve.Fori(0, NT) as t:
                nc.vector.bn_stats(st[:, bass.ds(t, 1), :].rearrange("p o s -> p (o s)"),
                                   x_sb[:, bass.ds(t, 1), :].rearrange("p o c -> p (o c)"))
            dve.drain()
            halves_to_mean_var(nc, ch, st, mv, half)
            nc.vector.tensor_scalar_add(std[:, :], mv[:, :, 1], EPS).then_inc(s_var, 1)
            dve.wait_ge(s_std, 1)
            ch.link(nc.vector.reciprocal(rstd[:, :], std[:, :]))
            dve.wait_ge(s_bias, 80)
            dve.wait_ge(s_din, 16)

            def grouped(t3):
                return t3.rearrange("p (g c) -> p g c", c=HC)

            def spread(t2):
                return t2.unsqueeze(2).to_broadcast([P, G, HC])

            def normalise(t, b, first):
                if not first:
                    dve.wait_ge(s_tp, t - 1)
                nc.vector.tensor_scalar(xn[:, b, :], x_sb[:, bass.ds(t, 1), :].rearrange("p o c -> p (o c)"),
                                        mv[:, bass.ds(t, 1), 0], rstd[:, bass.ds(t, 1)], ALU.subtract,
                                        ALU.mult).then_inc(s_xn, 1)

            def centre(t, b, first):
                dve.wait_ge(s_kp, t + 1)
                if not first:
                    dve.wait_ge(s_nrm, t - 1)
                bias = b_kv[:, :].rearrange("p (h s) -> p h s", s=3 * HC)[:, :, HC:]
                ch.link(nc.vector.tensor_tensor(kv[:, b, :].rearrange("p (h s) -> p h s", s=2 * HC),
                                                p_k[b][0:P, :].rearrange("p (h s) -> p h s", s=2 * HC), bias, ALU.add))
                ch.link(nc.vector.reduce_sum(gs[:, b, :], grouped(kv[:, b, :]), axis=AX))
                ch.link(nc.vector.tensor_scalar(gs[:, b, :], gs[:, b, :], 1.0 / HC, None, ALU.mult))
                nc.vector.tensor_tensor(grouped(kv[:, b, :]), grouped(kv[:, b, :]), spread(gs[:, b, :]),
                                        ALU.subtract).then_inc(s_cen, 1)

            def variance(t, b):
                dve.wait_ge(s_sq, t + 1)
                ch.link(nc.vector.reduce_sum(gv[:, b, :], grouped(sq[:, b, :]), axis=AX))
                nc.vector.tensor_scalar(gv[:, b, :], gv[:, b, :], 1.0 / HC, EPS, ALU.mult, ALU.add).then_inc(s_gd, 1)

            def scale(t, b, first):
                dve.wait_ge(s_gstd, t + 1)
                if not first:
                    dve.wait_ge(s_nrm, t - 1)
                nc.vector.reciprocal(gd[:, b, :], gv[:, b, :]).then_inc(s_rec, 1)

            normalise(0, 0, True)
            normalise(1, 1, True)

            def step(i, has):
                for b in range(2):
                    t = 2 * i + b
                    if has(b, -2):
                        scale(t - 2, b, not has(b, -4))
                    if has(b, -1):
                        variance(t - 1, 1 - b)
                    if has(b, 2):
                        normalise(t + 2, b, False)
                    centre(t, b, not has(b, -2))
            pipelined(dve, ch, NT // 2, 2, 1, 2 * 4, step)
            scale(NT - 2, 0, False)
            variance(NT - 1, 1)
            scale(NT - 1, 1, False)
            nc.vector.memset(kvbd[:, :, :], 0.0).then_inc(s_kvd, 1)
            dve.wait_ge(s_kvd, 1)
            dve.wait_ge(s_end, 1)
            for h in range(CH):
                for q in range(4):
                    r = slice(32 * q, 32 * q + 32)
                    nc.vector.tensor_scalar(kvbd[r, h, r], p_kv[r, h * 128 + 32 * q:h * 128 + 32 * q + 32],
                                            1.0 / N, None, ALU.mult)

        @block.gpsimd
        def _(pool):
            for t in range(HIST_A):
                nc.gpsimd.indirect_dma_start(
                    out=d["order"][:, :], out_offset=bass.IndirectOffsetOnAxis(ap=rank_t[:, t:t + 1], axis=0),
                    in_=node_row[:, t, :], in_offset=None).then_inc(s_order, 16)
            pool.wait_ge(s_zero, 1)
            pool.wait_ge(s_bias, 80)

            def both(t2):
                return t2.unsqueeze(1).to_broadcast([P, HEADS, HC])

            def step(i, first):
                for b in range(2):
                    t = 2 * i + b
                    pool.wait_ge(s_rec, t + 1)
                    if not first:
                        pool.wait_ge(s_kn, t - 1)
                    nc.gpsimd.tensor_tensor(kvg[:, b, :].rearrange("p (g c) -> p g c", c=HC),
                                            kv[:, b, :].rearrange("p (g c) -> p g c", c=HC),
                                            gd[:, b, :].unsqueeze(2).to_broadcast([P, G, HC]), ALU.mult).then_inc(s_nrm, 1)
                    pool.wait_ge(s_nrm, t + 1)
                    if not first:
                        pool.wait_ge(s_kva, t - 1)
                    src = kvg[:, b, :].rearrange("p (h s c) -> p h s c", s=2, c=HC)
                    for j in range(2):
                        last = nc.gpsimd.tensor_tensor(src[:, :, j, :], src[:, :, j, :], both(ln_g[:, j, :]), ALU.mult)
                    last.then_inc(s_pool, 1)
                    pool.wait_ge(s_pool, t + 1)
                    for j in range(2):
                        last = nc.gpsimd.tensor_tensor(kn[:, b, j, :].rearrange("p (h c) -> p h c", c=HC),
                                                       src[:, :, j, :], both(ln_b[:, j, :]), ALU.add)
                    last.then_inc(s_kn, 1)
            loop2(pool, None, NT // 2, 0, step)
            pool.wait_ge(s_order, 16 * HIST_A)

        @block.scalar
        def _(act):
            act.wait_ge(s_var, 1)
            nc.scalar.activation(std[:, :], std[:, :], ACT.Sqrt).then_inc(s_std, 1)

            def transposed(t, b, i, first):
                act.wait_ge(s_tp, t + 1)
                if not first:
                    act.wait_ge(s_xtw[b], 16 * i)
                    act.wait_ge(s_cp, t - 1)
                nc.scalar.activation(xt[:, b, :], p_t[b][:, 0:CH * P], ACT.Copy).then_inc(s_xt, 1)

            def combination(t, b, i, first):
                act.wait_ge(s_cp, t + 1)
                if not first:
                    act.wait_ge(s_cww[b], 16 * i)
                nc.scalar.activation(cw[:, b, :], p_c[0:P, 0:TW], ACT.Copy).then_inc(s_cr, 1)

            act.wait_ge(s_din, 16)
            transposed(0, 0, 0, True)

            def step(i, has):
                for b in range(2):
                    t = 2 * i + b
                    if has(b, 1):
                        transposed(t + 1, 1 - b, i + b, not has(b, -1))
                    if has(b, -1):
                        combination(t - 1, 1 - b, i + b - 1, not has(b, -3))
                    act.wait_ge(s_bp, t + 1)
                    if has(b, -2):
                        act.wait_ge(s_tabw[b], 16 * i)
                    nc.scalar.activation(rows[:, b, 0:TW], p_b[b][0:P, 0:TW], ACT.Copy)
                    nc.scalar.activation(rows[:, b, TW:TW + 1], dinv[:, bass.ds(t, 1)], ACT.Copy).then_inc(s_row, 1)
                    if has(b, -1):
                        act.wait_ge(s_gd, t)
                        nc.scalar.activation(gv[:, 1 - b, :], gv[:, 1 - b, :], ACT.Sqrt).then_inc(s_gstd, 1)
                    act.wait_ge(s_cen, t + 1)
                    if has(b, -2):
                        act.wait_ge(s_gd, t - 1)
                    nc.scalar.activation(sq[:, b, :], kv[:, b, :], ACT.Square).then_inc(s_sq, 1)
            pipelined(act, None, NT // 2, 2, 1, 0, step)
            combination(NT - 1, 1, NT // 2 - 1, False)
            act.wait_ge(s_gd, NT)
            nc.scalar.activation(gv[:, 1, :], gv[:, 1, :], ACT.Sqrt).then_inc(s_gstd, 1)

        @block.tensor
        def _(pe):
            pe.wait_ge(s_w, 96)
            pe.wait_ge(s_zero, 1)
            nc.tensor.matmul(p_kv[:, 0:C], zero[:, 0:128], zero[:, :], start=True, stop=False)

            def kv_sum(b):
                for h in range(CH):
                    last = nc.tensor.matmul(p_kv[:, h * 128:(h + 1) * 128], kn[:, b, 0, h * 128:(h + 1) * 128],
                                            kn[:, b, 1, h * 128:(h + 1) * 128], start=False, stop=False)
                return last

            def transposes(t, b, first):
                pe.wait_ge(s_xn, t + 1)
                if not first:
                    pe.wait_ge(s_xt, t - 1)
                for k in range(CH):
                    last = nc.tensor.transpose(p_t[b][:, k * P:(k + 1) * P], xn[:, b, k * 128:(k + 1) * 128], ident[0:P, 0:P])
                last.then_inc(s_tp, 1)

            transposes(0, 0, True)

            def step(i, has):
                for b in range(2):
                    t = 2 * i + b
                    if has(b, 1):
                        transposes(t + 1, 1 - b, not has(b, -1))
                    pe.wait_ge(s_xt, t + 1)
                    if has(b, -2):
                        pe.wait_ge(s_row, t - 1)
                        pe.wait_ge(s_cen, t - 1)
                    for k in range(CH):
                        last = nc.tensor.matmul(p_b[b][0:P, 0:TW], xt[:, b, k * P:(k + 1) * P],
                                                wb[:, k].rearrange("p l w -> p (l w)"), start=k == 0, stop=k == CH - 1)
                    last.then_inc(s_bp, 1)
                    for k in range(CH):
                        rhs = wqkv[:, k, :].rearrange("p (h s) -> p h s", s=3 * HC)[:, :, HC:]
                        last = nc.tensor.matmul(p_k[b][0:P, :].rearrange("p (h s) -> p h s", s=2 * HC),
                                                xt[:, b, k * P:(k + 1) * P], rhs, start=k == 0, stop=k == CH - 1)
                    last.then_inc(s_kp, 1)
                    if has(b, -1):
                        pe.wait_ge(s_cr, t)
                    for k in range(CH):
                        last = nc.tensor.matmul(p_c[0:P, 0:TW], xt[:, b, k * P:(k + 1) * P],
                                                wc[:, k].rearrange("p l w -> p (l w)"), start=k == 0, stop=k == CH - 1)
                    last.then_inc(s_cp, 1)
                    if has(b, -3):
                        pe.wait_ge(s_kn, t - 2)
                        kv_sum(1 - b).then_inc(s_kva, 1)
            pipelined(pe, None, NT // 2, 2, 1, 0, step)
            for t in range(NT - 3, NT):
                pe.wait_ge(s_kn, t + 1)
                kv_sum(t % 2).then_inc(s_kva, 1)
            nc.tensor.matmul(p_kv[:, 0:C], zero[:, 0:128], zero[:, :], start=False, stop=True).then_inc(s_end, 1)


def phase_edges(nc, phase, a, d, ident):
    COLS = GROUPS * CHUNKS
    CPI = SET * STEP
    with phase("e", clear=True) as (c, sb, ps, sm):
        raw = sb("raw", [GROUPS, NG, 4])
        two = sb("two", [GROUPS, 3, 2, NG])
        most_in = sb("most_in", [SETS, SET * NG, 4])
        most = sb("most", [SETS, 1])
        cnt = sb("cnt", [128, GROUPS])
        start = sb("start", [128, GROUPS])
        start_c = sb("start_c", [128, GROUPS])
        start_i = sb("start_i", [128, GROUPS], I32)
        own = sb("own", [128, GROUPS])
        slot_i = sb("slot_i", [128, CHUNKS], I32)
        slot = sb("slot", [128, CHUNKS])
        not_own = sb("not_own", [128, CHUNKS])
        half = sb("half", [128, 1])
        runs = sb("runs", [128, GROUPS, SLOTS], I32)
        valid = sb("valid", [128, COLS])
        take = sb("take", [128, COLS])
        idx = sb("idx", [128, GROUPS, CHUNKS], I32)
        row = sb("row", [1, SETS])
        row_c = sb("row_c", [1, SETS])
        one = sb("one", [1, SETS])
        iters_i = sb("iters_i", [1, SETS], I32)
        iters = sb("iters", [1, SETS])
        upto = sb("upto", [1, SETS])
        base_i = sb("base_i", [1, SETS], I32)
        carry = sb("carry", [1, 1])
        top = sb("top", [1, 4])
        pass_i = sb("pass_i", [1, 1], I32)
        from_i = sb("from_i", [1, SETS], I32)
        set_i = sb("set_i", [1, SETS], I32)
        e2 = sb("e2", [128, NG])
        zero_b = sb("zero_b", [128, TW], BF16)
        ibuf = sb("ibuf", [128, STEP, SET], I32)
        g = sb("g", [128, CPI, TW + 1])
        dg = sb("dg", [128, CPI, 128])
        sum_in = sb("sum_in", [128, SET, TW])
        max_in = sb("max_in", [128, SET, TW])
        acc = sb("acc", [128, SET, TW])
        sum_out = sb("sum_out", [128, SET, TW])
        max_out = sb("max_out", [128, SET, TW])
        p_s = [ps(f"p_s{q}") for q in range(SET)]
        p_tr = ps("p_tr")
        p_row = ps("p_row")
        (s_in, s_dve, s_gp, s_tr, s_two, s_start, s_table, s_npass, s_e2, s_act, s_acc0, s_stored) = (sm(n) for n in
            ("in", "dve", "gp", "tr", "two", "start", "table", "npass", "e2", "act", "acc0", "stored"))
        s_ib, s_pe, s_max, s_dg, s_set, s_ev, s_acc, s_pass, s_sum_ld, s_max_ld, s_st, s_sum_used = (sm(n) for n in
            ("ib", "pe", "max", "dg", "set", "ev", "acc", "pass", "sum_ld", "max_ld", "st", "sum_used"))
        s_from = sm("from")
        s_runs = sm("runs", swdge=True)
        s_g = [sm(f"g{j}", swdge=True) for j in range(CPI)]
        block = c.enter_context(nc.Block())

        def passes(eng):
            eng.wait_ge(s_npass, 1)
            return eng.value_load(pass_i[0:1, 0:1], min_val=1, max_val=E // SLOTS + 2)

        def set_iters(eng, t):
            n = eng.value_load(iters_i[0:1, bass.ds(t, 1)], min_val=1, max_val=CHUNKS // STEP)
            first = eng.value_load(base_i[0:1, bass.ds(t, 1)], min_val=0, max_val=1 << 19)
            return n, first

        @block.sync
        def _(sp):
            sp.dma_start(raw[:, :, :], d["order"].rearrange("(g l) c -> g l c", l=NG)).then_inc(s_in, 16)
            sp.dma_start(most_in[:, :, :], d["order"].rearrange("(s l) c -> s l c", l=SET * NG)).then_inc(s_in, 16)

            def part(t, r):
                return d["agg"].rearrange("(s q l) r w -> l s q r w", q=SET, l=NG)[:, bass.ds(t, 1), :, r, :].rearrange("l o q w -> l (o q) w")

            def halves(t, buf, r, sem, load):
                for h in range(2):
                    mem = buf[h * NG:(h + 1) * NG, :, :]
                    if load:
                        sp.dma_start(mem, part(t, r + h)).then_inc(sem, 16)
                    else:
                        sp.dma_start(part(t, r + h), mem).then_inc(sem, 16)

            def load(t):
                t = sp.value_load(from_i[0:1, bass.ds(t, 1)], min_val=0, max_val=SETS)
                halves(t, sum_in, 0, s_sum_ld, True)
                halves(t, max_in, 2, s_max_ld, True)

            def store(t, k):
                sp.wait_ge(s_ev, k + 2)
                halves(t, sum_out, 0, s_st, False)
                sp.wait_ge(s_acc, k + 1)
                halves(t, max_out, 2, s_st, False)
                sp.wait_ge(s_st, 64 * (k + 1))
                sp.nop(nofuse=True)
                sp.sem_inc(s_stored, 1)

            sp.sem_inc(s_stored, 1)
            n_pass = passes(sp)
            with sp.Fori(0, n_pass) as p:
                sp.wait_ge(s_from, p + 1)
                sp.nop(nofuse=True)
                load(0)
                with sp.Fori(0, SETS - 1) as t:
                    k = p * SETS + t
                    sp.wait_ge(s_sum_used, k + 1)
                    sp.wait_ge(s_acc0, k + 1)
                    load(t + 1)
                    store(t, k)
                store(SETS - 1, p * SETS + (SETS - 1))
                sp.sem_inc(s_pass, 1)

        @block.gpsimd
        def _(pool):
            nc.gpsimd.memset(half[0:NG, :], 0.0).then_inc(s_gp, 1)
            nc.gpsimd.memset(half[NG:128, :], 1.0).then_inc(s_gp, 1)
            nc.gpsimd.iota(from_i[:, :], pattern=[[0, SETS]], base=SETS, channel_multiplier=0).then_inc(s_gp, 1)
            nc.gpsimd.iota(set_i[:, :], pattern=[[1, SETS]], base=0, channel_multiplier=0).then_inc(s_gp, 1)
            for h in range(2):
                nc.gpsimd.iota(slot_i[h * NG:(h + 1) * NG, :], pattern=[[2, CHUNKS]], base=h, channel_multiplier=0).then_inc(s_gp, 1)
            n_pass = passes(pool)
            with pool.Fori(0, n_pass) as p:
                pool.wait_ge(s_start, p + 1)
                pool.nop(nofuse=True)
                for t in range(GROUPS):
                    nc.gpsimd.indirect_dma_start(
                        out=runs[:, t, :], out_offset=None, in_=d["runs"][:, :],
                        in_offset=bass.IndirectOffsetOnAxis(ap=start_i[:, t:t + 1], axis=0)).then_inc(s_runs, 16)
                pool.wait_ge(s_table, p + 1)
                pool.nop(nofuse=True)
                with pool.Fori(0, SETS) as t:
                    n, first = set_iters(pool, t)
                    with pool.Fori(0, n) as i:
                        it = first + i
                        for j in range(STEP):
                            pool.wait_ge(s_pe, it * CPI + SET * (j + 1))
                            pool.wait_ge(s_max, it * CPI + SET * (j + 1))
                            cols = idx[:, bass.ds(t * SET, SET), bass.ds(i * STEP + j, 1)].rearrange("p q o -> p (q o)")
                            nc.gpsimd.tensor_copy(ibuf[:, j, :], cols).then_inc(s_ib, 1)
                            pool.wait_ge(s_ib, it * STEP + (j + 1))
                            pool.nop(nofuse=True)
                            for q in range(SET):
                                x = j * SET + q
                                nc.gpsimd.indirect_dma_start(
                                    out=g[:, x, :], out_offset=None, in_=d["tab"][:, :],
                                    in_offset=bass.IndirectOffsetOnAxis(ap=ibuf[:, j, q:q + 1], axis=0)).then_inc(s_g[x], 16)

        @block.vector
        def _(dve):
            ch = Chain(dve, s_dve)
            v = nc.vector
            dve.sem_inc(s_max, CPI)
            v.memset(one[:, :], 1.0)
            v.memset(zero_b[:, :], 0.0)
            v.memset(carry[:, :], 0.0)
            for h in range(2):
                lanes = slice(h * NG, (h + 1) * NG)
                last = v.tensor_copy(e2[lanes, :], ident[lanes, lanes])
            last.then_inc(s_e2, 1)
            dve.wait_ge(s_in, 32)
            v.reduce_max(most[:, :], most_in[:, :, 0], axis=AX)
            for k in range(3):
                for h in range(2):
                    last = v.tensor_copy(two[:, k, h, :], raw[:, :, k])
            last.then_inc(s_two, 1)
            dve.wait_ge(s_gp, 6)
            ch.link(v.tensor_copy(slot[:, :], slot_i[:, :]))
            dve.wait_ge(s_tr, 1)
            v.tensor_copy(cnt[:, :], p_tr[:, 0:GROUPS])
            v.tensor_scalar(start[:, :], p_tr[:, 128:128 + GROUPS], half[:, 0:1], None, ALU.add)
            v.tensor_copy(own[:, :], p_tr[:, 256:256 + GROUPS])
            ch.link(v.tensor_copy(row[:, :], p_row[0:1, 0:SETS]))
            ch.link(v.reduce_max(top[:, 0:1], row[:, :], axis=AX))
            ch.link(v.tensor_scalar(top[:, 1:2], top[:, 0:1], SLOTS + 0.5, 1.0 / SLOTS, ALU.add, ALU.mult))
            ch.link(v.tensor_copy(pass_i[:, :], top[:, 1:2]))
            ch.link(v.tensor_copy(top[:, 2:3], pass_i[:, :]))
            ch.link(v.tensor_tensor(top[:, 3:4], top[:, 2:3], top[:, 1:2], ALU.is_gt))
            ch.link(v.tensor_tensor(top[:, 2:3], top[:, 2:3], top[:, 3:4], ALU.subtract))
            v.tensor_copy(pass_i[:, :], top[:, 2:3]).then_inc(s_npass, 1)
            dve.sem_inc(s_from, 1)
            n_pass = passes(dve)
            before = ch.n
            PER_PASS = 14

            def wide(t2):
                return t2.unsqueeze(2).to_broadcast([128, GROUPS, CHUNKS])

            def over(t2):
                return t2.unsqueeze(1).to_broadcast([128, GROUPS, CHUNKS])

            def cube(t2):
                return t2.rearrange("p (g k) -> p g k", k=CHUNKS)

            with dve.Fori(0, n_pass) as p:
                ch.base = p * PER_PASS
                ch.link(v.tensor_scalar(start_c[:, :], start[:, :], float(E), None, ALU.min))
                v.tensor_copy(start_i[:, :], start_c[:, :]).then_inc(s_start, 1)
                ch.link(v.tensor_scalar(row_c[:, :], row[:, :], 2.0 * STEP, 2.0 * STEP, ALU.add, ALU.max))
                ch.link(v.tensor_scalar(row_c[:, :], row_c[:, :], float(SLOTS), None, ALU.min))
                ch.link(v.tensor_copy(iters_i[:, :], row_c[:, :]))
                ch.link(v.tensor_single_scalar(iters_i[:, :], iters_i[:, :], 2, op=ALU.logical_shift_right))
                ch.link(v.tensor_copy(iters[:, :], iters_i[:, :]))
                ch.link(v.tensor_tensor_scan(upto[:, :], one[:, :], iters[:, :], carry[:, 0:1], ALU.mult, ALU.add))
                ch.link(v.tensor_tensor(iters[:, :], upto[:, :], iters[:, :], ALU.subtract))
                v.tensor_copy(base_i[:, :], iters[:, :])
                ch.link(v.tensor_copy(carry[:, :], upto[:, SETS - 1:SETS]))
                v.tensor_tensor(cube(valid[:, :]), over(slot[:, :]), wide(cnt[:, :]), ALU.is_le)
                ch.link(v.tensor_scalar(not_own[:, :], slot[:, :], 0.5, None, ALU.is_gt))
                ch.link(v.tensor_tensor(cube(take[:, :]), cube(valid[:, :]), over(not_own[:, :]), ALU.mult))
                dve.wait_ge(s_runs, 16 * GROUPS * (p + 1))
                edge = runs[:, :, :].rearrange("p g (k s) -> p g k s", s=2)[:, :, :, 0]
                ch.link(v.tensor_tensor(edge, edge, wide(own[:, :]), ALU.subtract))
                ch.link(v.tensor_tensor(cube(take[:, :]), cube(take[:, :]), edge, ALU.mult))
                v.tensor_tensor(idx[:, :, :], cube(take[:, :]), wide(own[:, :]), ALU.add).then_inc(s_table, 1)
                dve.wait_ge(s_table, p + 1)
                dve.nop(nofuse=True)

                with dve.Fori(0, SETS) as t:
                    k = p * SETS + t
                    n, first = set_iters(dve, t)
                    dve.wait_ge(s_max_ld, 32 * (k + 1))
                    v.tensor_copy(acc[:, :, :], max_in[:, :, :]).then_inc(s_acc0, 1)
                    dve.wait_ge(s_acc0, k + 1)
                    dve.nop(nofuse=True)
                    with dve.Fori(0, n) as i:
                        it = first + i
                        for x in range(CPI):
                            dve.wait_ge(s_g[x], 16 * (it + 1))
                            dve.wait_ge(s_max, it * CPI + (CPI + x + 1 - SET))
                            v.tensor_tensor(acc[:, x % SET, :], acc[:, x % SET, :], g[:, x, 0:TW], ALU.max).then_inc(s_max, 1)
                    dve.wait_ge(s_max, (first + n) * CPI + CPI)
                    dve.nop(nofuse=True)
                    dve.wait_ge(s_stored, k + 1)
                    v.tensor_copy(max_out[:, :, :], acc[:, :, :]).then_inc(s_acc, 1)
                    dve.wait_ge(s_acc, k + 1)
                    dve.nop(nofuse=True)
                dve.wait_ge(s_pass, p + 1)
                v.tensor_copy(from_i[:, :], set_i[:, :]).then_inc(s_from, 1)
                v.tensor_scalar(start[:, :], start[:, :], float(SLOTS), None, ALU.add)
                v.tensor_scalar(row[:, :], row[:, :], -float(SLOTS), None, ALU.add)
                ch.link(v.tensor_scalar(slot[:, :], slot[:, :], float(SLOTS), None, ALU.add))
                assert ch.n - before == PER_PASS, ch.n - before

        @block.scalar
        def _(act):
            act.sem_inc(s_ev, 1)
            act.wait_ge(s_e2, 1)
            n_pass = passes(act)
            with act.Fori(0, n_pass) as p:
                act.wait_ge(s_table, p + 1)
                act.nop(nofuse=True)
                with act.Fori(0, SETS) as t:
                    k = p * SETS + t
                    n, first = set_iters(act, t)
                    with act.Fori(0, n) as i:
                        it = first + i
                        for j in range(STEP):
                            for q in range(SET):
                                x = j * SET + q
                                act.wait_ge(s_pe, it * CPI + (x + 1))
                                nc.scalar.activation(dg[:, x, 0:NG], e2[:, :], ACT.Copy,
                                                     scale=valid[:, bass.ds(t * (SET * CHUNKS) + q * CHUNKS + i * STEP + j, 1)]).then_inc(s_act, 1)
                            for q in range(SET):
                                x = j * SET + q
                                act.wait_ge(s_g[x], 16 * (it + 1))
                                act.wait_ge(s_act, it * CPI + (x + 1))
                                nc.scalar.activation(dg[:, x, NG:2 * NG], dg[:, x, 0:NG], ACT.Copy,
                                                     scale=g[:, x, TW:TW + 1]).then_inc(s_dg, 1)
                    act.wait_ge(s_set, k + 1)
                    act.wait_ge(s_stored, k + 1)
                    for q in range(SET):
                        last = nc.scalar.activation(sum_out[:, q, :], p_s[q][:, 0:TW], ACT.Copy)
                    last.then_inc(s_ev, 1)

        @block.tensor
        def _(pe):
            pe.sem_inc(s_pe, CPI)
            pe.wait_ge(s_two, 1)
            for k in range(3):
                nc.tensor.transpose(p_tr[:, k * 128:k * 128 + GROUPS], two[:, k].rearrange("g h l -> g (h l)"),
                                    ident[0:GROUPS, 0:GROUPS])
            nc.tensor.transpose(p_row[0:1, 0:SETS], most[:, :], ident[0:SETS, 0:SETS]).then_inc(s_tr, 1)
            n_pass = passes(pe)
            with pe.Fori(0, n_pass) as p:
                pe.wait_ge(s_table, p + 1)
                pe.nop(nofuse=True)
                with pe.Fori(0, SETS) as t:
                    k = p * SETS + t
                    n, first = set_iters(pe, t)
                    pe.wait_ge(s_sum_ld, 32 * (k + 1))
                    pe.wait_ge(s_ev, k + 1)
                    for q in range(SET):
                        last = nc.tensor.matmul(p_s[q][:, 0:TW], ident[:, :], sum_in[:, q, :], start=True, stop=False)
                    last.then_inc(s_sum_used, 1)
                    with pe.Fori(0, n) as i:
                        it = first + i
                        for x in range(CPI):
                            pe.wait_ge(s_dg, it * CPI + (x + 1))
                            nc.tensor.matmul(p_s[x % SET][:, 0:TW], dg[:, x, :], g[:, x, 0:TW], start=False,
                                             stop=False).then_inc(s_pe, 1)
                    for q in range(SET):
                        last = nc.tensor.matmul(p_s[q][:, 0:TW], zero_b[:, 0:128], zero_b[:, :], start=False, stop=True)
                    last.then_inc(s_set, 1)


def mix_weights(alloc):
    H2 = 2 * L
    return (
        alloc("mix_fcw", [128, 2 + H2, C]),
        alloc("mix_wq", [128, CH, C]),
        alloc("mix_w1", [128, CH, C]),
        alloc("mix_w2", [128, CH, C]),
        alloc("mix_b_q", [128, CH]),
        alloc("mix_b1", [128, CH]),
        alloc("mix_gam", [128, H2]),
        alloc("mix_bet", [128, H2]),
        alloc("mix_fcb", [P, C]),
        alloc("mix_b2", [P, C]),
    )


def load_mix_weights(sp, a, weights, sem):
    H2 = 2 * L
    fcw, wq, w1, w2, b_q, b1, gam, bet, fcb, b2 = weights

    def rows128(name):
        return a[name].rearrange("(k p) n -> p k n", p=128)
    for k in range(CH):
        sp.dma_start(wq[:, k, :].rearrange("p (h s) -> p h s", s=HC),
                     a["L0_mix_w_qkv"][k * 128:(k + 1) * 128, :].rearrange("p (h s) -> p h s", s=3 * HC)[:, :, 0:HC]).then_inc(sem, 16)
    sp.dma_start(w1[:, :, :], rows128("L0_mix_w1")).then_inc(sem, 16)
    sp.dma_start(w2[:, :, :], rows128("L0_mix_w2")).then_inc(sem, 16)
    sp.dma_start(fcw[:, :, :], rows128("L0_gnn_fc_W")).then_inc(sem, 16)
    for k in range(CH):
        for h in range(4):
            at = (4 * k + h) * 3 * HC
            sp.dma_start(b_q[32 * h:32 * h + 32, k:k + 1],
                         a["L0_mix_b_qkv"][at:at + HC].rearrange("(p o) -> p o", o=1)).then_inc(sem, 16)
        sp.dma_start(b1[:, k:k + 1], a["L0_mix_b1"][k * 128:(k + 1) * 128].rearrange("(p o) -> p o", o=1)).then_inc(sem, 16)
    for l in range(L):
        for k in range(CH):
            sl = slice(k * 128, (k + 1) * 128)
            q = l * CH + k
            sp.dma_start(gam[:, q:q + 1], a["L0_gnn_bn_gamma"][l, sl].rearrange("(p o) -> p o", o=1)).then_inc(sem, 16)
            sp.dma_start(bet[:, q:q + 1], a["L0_gnn_bn_beta"][l, sl].rearrange("(p o) -> p o", o=1)).then_inc(sem, 16)
    sp.dma_start(fcb[:, :], a["L0_gnn_fc_b"].rearrange("(o n) -> o n", o=1).to_broadcast([P, C])).then_inc(sem, 16)
    sp.dma_start(b2[:, :], a["L0_mix_b2"].rearrange("(o n) -> o n", o=1).to_broadcast([P, C])).then_inc(sem, 16)
    return 16 * (5 + 2 * 5 + 2 * H2 + 2)


def phase_conv(nc, phase, a, d, ident, stats, mixw):
    K = 3 * BASES
    LH = L * HEADS
    H2 = 2 * L
    SHARED = (2, 1)
    CUT = 1
    DVE_PARTS = ((0, 2, 0, HEADS), (1, 2, 0, HEADS), (2, 2, 0, HEADS), (0, 0, 0, HEADS), (*SHARED, 0, CUT))
    POOL_PARTS = ((0, 1, 0, HEADS), (1, 0, 0, HEADS), (1, 1, 0, HEADS), (2, 0, 0, HEADS), (*SHARED, CUT, HEADS))
    with phase("c") as (c, sb, ps, sm):
        bc = sb("bc", [P, L * 128])
        cb = sb("cb", [128, H2])
        dinv = sb("dinv", [P, NT])
        invdeg = sb("invdeg", [P, NT])
        rank = sb("rank", [P, NT], I32)
        ibuf = sb("ibuf", [P, 2], I32)
        cw = sb("cw", [P, 2, TW])
        ag = sb("ag", [P, 2, 4, TW])
        w16 = sb("w16", [P, 2, LH * 16])
        w12 = sb("w12", [P, 2, LH, K])
        prod = sb("prod", [P, 2, L, HEADS, K, HC])
        h = sb("h", [P, 2, L * C])
        ht = sb("ht", [128, 2, H2 * P])
        p_s = [ps(f"p_s{b}") for b in range(2)]
        p_h = [[ps(f"p_h{b}{q}") for q in range(2)] for b in range(2)]
        (s_const, s_dve, s_w16, s_w12, s_wa, s_mx, s_pd, s_pp, s_red, s_ps, s_h, s_tp, s_ht, s_st, s_rank,
         s_ib) = (sm(n) for n in
            ("const", "dve", "w16", "w12", "wa", "mx", "pd", "pp", "red", "ps", "h", "tp", "ht", "st", "rank",
             "ib"))
        s_mix = sm("mix")
        s_ld = [sm(f"ld{b}") for b in range(2)]
        s_ag = [sm(f"ag{b}", swdge=True) for b in range(2)]
        s_out = [sm(f"out{b}") for b in range(2)]
        block = c.enter_context(nc.Block())
        agg = d["agg"].rearrange("n r w -> n (r w)")
        cws = d["cw"].rearrange("(p t) w -> p t w", t=NT)

        def product(eng, b, l, r, h0, h1):
            n = h1 - h0
            return eng.tensor_tensor(
                prod[:, b, l, h0:h1, r * BASES:(r + 1) * BASES, :],
                w12[:, b, l * HEADS + h0:l * HEADS + h1, r * BASES:(r + 1) * BASES].unsqueeze(3).to_broadcast([P, n, BASES, HC]),
                ag[:, b, r, l * BW:(l + 1) * BW].rearrange("p (k c) -> p k c", c=HC).unsqueeze(1).to_broadcast([P, n, BASES, HC]),
                ALU.mult)

        @block.sync
        def _(sp):
            sp.dma_start(rank[:, :], d["rank"][0:N].rearrange("(p t) -> p t", t=NT)).then_inc(s_rank, 16)
            sp.dma_start(bc[:, :], a["L0_gnn_bc"].rearrange("(o l) n -> o (l n)", o=1).to_broadcast([P, L * 128])).then_inc(s_const, 16)
            for k in range(H2):
                at = slice(k % CH * 128, (k % CH + 1) * 128)
                sp.dma_start(cb[:, k:k + 1], a["L0_gnn_conv_bias"][k // CH, at].rearrange("(p o) -> p o", o=1)).then_inc(s_const, 16)
            sp.dma_start(dinv[:, :], d["dinv"][0:N].rearrange("(p t) -> p t", t=NT)).then_inc(s_const, 16)

            def step(i, first):
                for b in range(2):
                    t = 2 * i + b
                    if not first:
                        sp.wait_ge(s_w16, t - 1)
                    sp.dma_start(cw[:, b], cws[:, bass.ds(t, 1), :].rearrange("p o w -> p (o w)")).then_inc(s_ld[b], 16)
            step(0, True)
            mix_loaded = load_mix_weights(sp, a, mixw, s_mix)
            with sp.Fori(1, NT // 2) as i:
                step(i, False)
            sp.wait_ge(s_mix, mix_loaded)

        @block.scalar
        def _(act):
            act.wait_ge(s_const, 16 * (2 + H2))

            def weights(t, b, first):
                act.wait_ge(s_w16, t + 1)
                if not first:
                    act.wait_ge(s_pd, t - 1)
                    act.wait_ge(s_pp, t - 1)
                w = w16[:, b, :].rearrange("p (x r k) -> p x r k", r=4, k=BASES)
                nc.scalar.activation(w12[:, b, :, BASES:2 * BASES], w[:, :, 3], ACT.Copy, scale=dinv[:, bass.ds(t, 1)])
                nc.scalar.activation(w12[:, b, :, 2 * BASES:], w[:, :, 1], ACT.Copy).then_inc(s_wa, 1)

            def store(t, b, i, first):
                act.wait_ge(s_tp, t + 1)
                if not first:
                    act.wait_ge(s_out[b], 16 * i)
                    act.wait_ge(s_st, t - 1)
                for k in range(H2):
                    last = nc.scalar.activation(ht[:, b, k * P:(k + 1) * P], p_h[b][k // 4][:, (k % 4) * P:(k % 4 + 1) * P],
                                                ACT.Identity, bias=cb[:, k:k + 1])
                last.then_inc(s_ht, 1)
                act.wait_ge(s_ht, t + 1)
                act.dma_start(d["ht"][bass.ds(t, 1)].rearrange("o p c -> (o p) c"), ht[:, b]).then_inc(s_out[b], 16)

            def later_layers(t, b, first):
                act.wait_ge(s_ps, t + 1)
                if not first:
                    act.wait_ge(s_tp, t - 1)
                nc.scalar.activation(h[:, b, C:], p_s[b][0:P, :], ACT.Copy).then_inc(s_h, 1)

            weights(0, 0, True)
            weights(1, 1, True)

            def step(i, first, last=False):
                for b in range(2):
                    t = 2 * i + b
                    if not last:
                        weights(t + 2, b, False)
                    later_layers(t, b, first)
                    if not (first and b == 0):
                        store(t - 1, 1 - b, i + b - 1, first)
            step(0, True)
            with act.Fori(1, NT // 2 - 1) as i:
                step(i, False)
            step(NT // 2 - 1, False, True)
            store(NT - 1, 1, NT // 2 - 1, False)
            for b in range(2):
                act.wait_ge(s_out[b], 16 * (NT // 2))

        @block.gpsimd
        def _(pool):
            def gather(t, b, first):
                if not first:
                    pool.wait_ge(s_pd, t - 1)
                    pool.wait_ge(s_pp, t - 1)
                nc.gpsimd.tensor_copy(ibuf[:, b:b + 1], rank[:, bass.ds(t, 1)]).then_inc(s_ib, 1)
                pool.wait_ge(s_ib, t + 1)
                pool.nop(nofuse=True)
                nc.gpsimd.indirect_dma_start(out=ag[:, b].rearrange("p r w -> p (r w)"), out_offset=None, in_=agg[:, :],
                                             in_offset=bass.IndirectOffsetOnAxis(ap=ibuf[:, b:b + 1], axis=0)).then_inc(s_ag[b], 16)

            pool.wait_ge(s_rank, 16)
            gather(0, 0, True)

            def step(i, first, last=False):
                for b in range(2):
                    t = 2 * i + b
                    if not (last and b):
                        gather(t + 1, 1 - b, first and b == 0)
                    pool.wait_ge(s_ag[b], 16 * (i + 1))
                    pool.wait_ge(s_w12, t + 1)
                    pool.wait_ge(s_wa, t + 1)
                    if not first:
                        pool.wait_ge(s_red, t - 1)
                        pool.wait_ge(s_ps, t - 1)
                    for part in POOL_PARTS:
                        prods = product(nc.gpsimd, b, *part)
                    prods.then_inc(s_pp, 1)
            step(0, True)
            with pool.Fori(1, NT // 2 - 1) as i:
                step(i, False)
            step(NT // 2 - 1, False, True)

        @block.vector
        def _(dve):
            ch = Chain(dve, s_dve)
            v = nc.vector
            dve.wait_ge(s_const, 16 * (2 + H2))
            ch.link(v.tensor_tensor(invdeg[:, :], dinv[:, :], dinv[:, :], ALU.mult))

            def weights(t, b, i, first):
                dve.wait_ge(s_ld[b], 16 * (i + 1))
                if not first:
                    dve.wait_ge(s_wa, t - 1)
                    dve.wait_ge(s_pp, t - 1)
                v.tensor_tensor(w16[:, b, :], cw[:, b, :], bc[:, :], ALU.add).then_inc(s_w16, 1)
                dve.wait_ge(s_w16, t + 1)
                w = w16[:, b, :].rearrange("p (x r k) -> p x r k", r=4, k=BASES)
                v.scalar_tensor_tensor(w12[:, b, :, 0:BASES], w[:, :, 0], invdeg[:, bass.ds(t, 1)], w[:, :, 2],
                                       ALU.mult, ALU.add).then_inc(s_w12, 1)

            def products(t, b, i, first):
                dve.wait_ge(s_ag[b], 16 * (i + 1))
                v.tensor_tensor(ag[:, b, 2, :], ag[:, b, 2, :], ag[:, b, 3, :], ALU.max).then_inc(s_mx, 1)
                dve.wait_ge(s_mx, t + 1)
                dve.wait_ge(s_w12, t + 1)
                dve.wait_ge(s_wa, t + 1)
                if not first:
                    dve.wait_ge(s_red, t - 1)
                    dve.wait_ge(s_ps, t - 1)
                for part in DVE_PARTS:
                    last = product(v, b, *part)
                last.then_inc(s_pd, 1)

            def layer0(t, b, first):
                dve.wait_ge(s_pd, t + 1)
                dve.wait_ge(s_pp, t + 1)
                if not first:
                    dve.wait_ge(s_tp, t - 1)
                v.reduce_sum(h[:, b, 0:C].rearrange("p (h c) -> p h c", c=HC),
                             prod[:, b, 0].rearrange("p h k c -> p h c k"), axis=AX).then_inc(s_red, 1)

            def statistics(t, b):
                dve.wait_ge(s_ht, t + 1)
                for k in range(H2):
                    last = v.bn_stats(stats[:, k, bass.ds(t, 1), :].rearrange("p o s -> p (o s)"),
                                      ht[:, b, k * P:(k + 1) * P])
                last.then_inc(s_st, 1)

            weights(0, 0, 0, True)
            weights(1, 1, 0, True)
            products(0, 0, 0, True)

            def step(i, first, last=False):
                for b in range(2):
                    t = 2 * i + b
                    if not (last and b):
                        products(t + 1, 1 - b, i + b, first and b == 0)
                    layer0(t, b, first)
                    if not last:
                        weights(t + 2, b, i + 1, False)
                    if not first:
                        statistics(t - 2, b)
            step(0, True)
            with dve.Fori(1, NT // 2 - 1) as i:
                step(i, False)
            step(NT // 2 - 1, False, True)
            statistics(NT - 2, 0)
            statistics(NT - 1, 1)

        @block.tensor
        def _(pe):
            pe.wait_ge(s_const, 16 * (2 + H2))

            def transposes(t, b, first):
                pe.wait_ge(s_h, t + 1)
                pe.wait_ge(s_red, t + 1)
                if not first:
                    pe.wait_ge(s_ht, t - 1)
                for k in range(H2):
                    last = nc.tensor.transpose(p_h[b][k // 4][:, (k % 4) * P:(k % 4 + 1) * P],
                                               h[:, b, k * 128:(k + 1) * 128], ident[0:P, 0:P])
                last.then_inc(s_tp, 1)

            def sums(t, b, first):
                pe.wait_ge(s_pd, t + 1)
                pe.wait_ge(s_pp, t + 1)
                if not first:
                    pe.wait_ge(s_h, t - 1)
                for k in range(K):
                    last = nc.tensor.matmul(p_s[b][0:P, :], ident[0:P, 0:P], prod[:, b, 1:L, :, k, :],
                                            start=k == 0, stop=k == K - 1)
                last.then_inc(s_ps, 1)

            def step(i, first, last=False):
                for b in range(2):
                    t = 2 * i + b
                    sums(t, b, first)
                    if not (first and b == 0):
                        transposes(t - 1, 1 - b, first)
            step(0, True)
            with pe.Fori(1, NT // 2 - 1) as i:
                step(i, False)
            step(NT // 2 - 1, False, True)
            transposes(NT - 1, 1, False)


def phase_mix(nc, phase, a, d, ident, x_sb, mv, rstd, kvbd, stats, xst, weights):
    H2 = 2 * L
    ZB = 4
    YG = 2 * N // 128
    XB = 10
    fcw, wq, w1, w2, b_q, b1, gam, bet, fcb, b2 = weights
    with phase("m") as (c, sb, ps, sm):
        bmv = sb("bmv", [128, H2, 2])
        bs = sb("bs", [128, H2])
        bb = sb("bb", [128, H2])
        wqt = sb("wqt", [128, CH, C])
        rt = sb("rt", [128, CH, C])
        m1 = sb("m1", [128, CH, C])
        u = sb("u", [128, CH])
        c1 = sb("c1", [128, CH])
        xt = sb("xt", [128, 2, CH * P])
        ht = sb("ht", [128, 2, H2 * P])
        z = sb("z", [128, 2, H2 * P])
        gt = sb("gt", [128, 2, CH * P])
        xn = sb("xn", [P, 2, C])
        zeros = sb("zeros", [128, ZB * C])
        p_a = ps("p_a")
        p_b = ps("p_b")
        p_g = [ps(f"p_g{b}") for b in range(2)]
        p_o = [ps(f"p_o{b}") for b in range(2)]
        (s_dve, s_wqt, s_wqtc, s_rt, s_rtc, s_m1, s_m1c, s_u, s_uc, s_c1, s_c1c, s_bn, s_bns, s_bn2) = (sm(n) for n in
            ("dve", "wqt", "wqtc", "rt", "rtc", "m1", "m1c", "u", "uc", "c1", "c1c", "bn", "bns", "bn2"))
        s_z, s_y, s_gp, s_gt, s_o, s_res, s_zero = (sm(n) for n in ("z", "y", "gp", "gt", "o", "res", "zero"))
        s_out = sm("out", swdge=True)
        s_hl = [sm(f"hl{b}") for b in range(2)]
        s_xl = [sm(f"xl{b}") for b in range(2)]
        block = c.enter_context(nc.Block())

        @block.sync
        def _(sp):
            def step(i, first):
                for b in range(2):
                    t = 2 * i + b
                    if not first:
                        sp.wait_ge(s_z, t - 1)
                    sp.dma_start(ht[:, b], d["ht"][bass.ds(t, 1)].rearrange("o p c -> (o p) c")).then_inc(s_hl[b], 16)
                    if not first:
                        sp.wait_ge(s_o, t - 1)
                    sp.dma_start(xt[:, b], d["xnt"][bass.ds(t, 1)].rearrange("o p c -> (o p) c")).then_inc(s_xl[b], 16)
            loop2(sp, None, NT // 2, 0, step)

        @block.gpsimd
        def _(pool):
            nc.gpsimd.memset(zeros[:, :], 0.0).then_inc(s_zero, 1)
            pool.wait_ge(s_zero, 1)
            for g in range(0, BLOCKS + 1, ZB):
                n = min(ZB, BLOCKS + 1 - g)
                pool.dma_start(d["xg"][g * 128:(g + n) * 128, :].rearrange("(p r) c -> p (r c)", p=128),
                               zeros[:, 0:n * C]).then_inc(s_out, 16)
            for g in range(YG, BLOCKS, ZB):
                n = min(ZB, BLOCKS - g)
                pool.dma_start(d["yg"][g * 128:(g + n) * 128, :].rearrange("(p r) c -> p (r c)", p=128),
                               zeros[:, 0:n * C]).then_inc(s_out, 16)
            for j in range(0, NT, XB):
                pool.wait_ge(s_res, j + XB)
                pool.dma_start(d["x2"].rearrange("(p t) c -> p t c", t=NT)[:, j:j + XB, :],
                               x_sb[:, j:j + XB, :]).then_inc(s_out, 16)
            pool.wait_ge(s_out, 16 * (-(-(BLOCKS + 1) // ZB) - (YG - BLOCKS) // ZB + NT // XB))

        @block.vector
        def _(dve):
            ch = Chain(dve, s_dve)
            v = nc.vector
            for k in range(H2):
                v.bn_aggr(bmv[:, k, :], stats[:, k, :, :].rearrange("p t s -> p (t s)"))
            ch.link(v.tensor_tensor(fcb[:, :], fcb[:, :], b2[:, :], ALU.add))
            v.tensor_scalar_add(bs[:, :], bmv[:, :, 1], EPS).then_inc(s_bn, 1)
            dve.wait_ge(s_bns, 1)
            ch.link(v.reciprocal(bb[:, :], bs[:, :]))
            ch.link(v.tensor_tensor(bs[:, :], bb[:, :], gam[:, :], ALU.mult))
            ch.link(v.tensor_tensor(bb[:, :], bs[:, :], bmv[:, :, 0], ALU.mult))
            v.tensor_tensor(bb[:, :], bet[:, :], bb[:, :], ALU.subtract).then_inc(s_bn2, 1)
            dve.wait_ge(s_wqt, 1)
            v.tensor_copy(wqt[:, 0, :], p_a[:, 0:C])
            v.tensor_copy(wqt[:, 1, :], p_a[:, C:2 * C]).then_inc(s_wqtc, 1)
            dve.wait_ge(s_rt, 1)
            ch.link(v.tensor_copy(rt[:, :, :], p_b[:, :].rearrange("p (k c) -> p k c", k=CH)))
            v.tensor_tensor(rt[:, 0, 0:128], rt[:, 0, 0:128], ident[:, :], ALU.add)
            v.tensor_tensor(rt[:, 1, 128:C], rt[:, 1, 128:C], ident[:, :], ALU.add).then_inc(s_rtc, 1)
            dve.wait_ge(s_m1, 1)
            v.tensor_copy(m1[:, :, :], p_a[:, :].rearrange("p (k c) -> p k c", k=CH)).then_inc(s_m1c, 1)
            dve.wait_ge(s_u, 1)
            v.tensor_copy(u[:, :], p_b[:, 0:CH]).then_inc(s_uc, 1)
            dve.wait_ge(s_c1, 1)
            v.tensor_tensor(c1[:, :], p_b[:, 8:8 + CH], b1[:, :], ALU.add).then_inc(s_c1c, 1)

            def leaky(t, b):
                dve.wait_ge(s_z, t + 1)
                v.scalar_tensor_tensor(z[:, b, :], z[:, b, :], SLOPE, z[:, b, :], ALU.mult, ALU.max).then_inc(s_y, 1)

            leaky(0, 0)

            def step(i, has):
                for b in range(2):
                    t = 2 * i + b
                    if has(b, 1):
                        leaky(t + 1, 1 - b)
                    xrow = x_sb[:, bass.ds(t, 1), :].rearrange("p o c -> p (o c)")
                    ch.link(v.tensor_scalar(xn[:, b, :], xrow, mv[:, bass.ds(t, 1), 0], rstd[:, bass.ds(t, 1)], ALU.subtract, ALU.mult))
                    ch.link(v.tensor_tensor(xn[:, b, :], xn[:, b, :], xrow, ALU.add))
                    ch.link(v.tensor_tensor(xn[:, b, :], xn[:, b, :], fcb[:, :], ALU.add))
                    dve.wait_ge(s_o, t + 1)
                    v.tensor_tensor(xrow, p_o[b][0:P, 0:C], xn[:, b, :], ALU.add).then_inc(s_res, 1)
                    dve.wait_ge(s_res, t + 1)
                    v.bn_stats(xst[:, bass.ds(t, 1), :].rearrange("p o s -> p (o s)"), xrow)
            pipelined(dve, ch, NT // 2, 1, 1, 2 * 3, step)

        @block.scalar
        def _(act):
            act.wait_ge(s_bn, 1)
            nc.scalar.activation(bs[:, :], bs[:, :], ACT.Sqrt).then_inc(s_bns, 1)
            act.wait_ge(s_bn2, 1)
            act.wait_ge(s_c1c, 1)

            def step(i, first):
                for b in range(2):
                    t = 2 * i + b
                    act.wait_ge(s_hl[b], 16 * (i + 1))
                    if not first:
                        act.wait_ge(s_o, t - 1)
                    for k in range(H2):
                        sl = slice(k * P, (k + 1) * P)
                        last = nc.scalar.activation(z[:, b, sl], ht[:, b, sl], ACT.Identity, bias=bb[:, k:k + 1], scale=bs[:, k:k + 1])
                    last.then_inc(s_z, 1)
                    act.wait_ge(s_gp, t + 1)
                    for k in range(CH):
                        sl = slice(k * P, (k + 1) * P)
                        last = nc.scalar.activation(gt[:, b, sl], p_g[b][:, sl], ACT.Gelu, bias=c1[:, k:k + 1])
                    last.then_inc(s_gt, 1)
            loop2(act, None, NT // 2, 0, step)

        @block.tensor
        def _(pe):
            for half in range(CH):
                for k in range(CH):
                    src = wq[:, k, half * 128:(half + 1) * 128]
                    last = nc.tensor.transpose(p_a[:, half * C + k * 128:half * C + (k + 1) * 128], src, ident[:, :])
            last.then_inc(s_wqt, 1)
            pe.wait_ge(s_wqtc, 1)
            for half in range(CH):
                last = nc.tensor.matmul(p_b[:, half * C:(half + 1) * C], kvbd[:, half, :], wqt[:, half, :], start=True, stop=True)
            last.then_inc(s_rt, 1)
            pe.wait_ge(s_rtc, 1)
            for k in range(CH):
                for half in range(CH):
                    last = nc.tensor.matmul(p_a[:, k * C:(k + 1) * C], rt[:, half, k * 128:(k + 1) * 128], w1[:, half, :],
                                            start=half == 0, stop=half == CH - 1)
            last.then_inc(s_m1, 1)
            for half in range(CH):
                last = nc.tensor.matmul(p_b[:, half:half + 1], kvbd[:, half, :], b_q[:, half:half + 1], start=True, stop=True)
            last.then_inc(s_u, 1)
            pe.wait_ge(s_uc, 1)
            for k in range(CH):
                for half in range(CH):
                    last = nc.tensor.matmul(p_b[:, 8 + k:9 + k], w1[:, half, k * 128:(k + 1) * 128], u[:, half:half + 1],
                                            start=half == 0, stop=half == CH - 1)
            last.then_inc(s_c1, 1)
            pe.wait_ge(s_m1c, 1)

            def step(i, first):
                for b in range(2):
                    t = 2 * i + b
                    pe.wait_ge(s_xl[b], 16 * (i + 1))
                    if not first:
                        pe.wait_ge(s_gt, t - 1)
                    for f in range(CH):
                        for k in range(CH):
                            last = nc.tensor.matmul(p_g[b][:, f * P:(f + 1) * P], m1[:, k, f * 128:(f + 1) * 128],
                                                    xt[:, b, k * P:(k + 1) * P], start=k == 0, stop=k == CH - 1)
                    last.then_inc(s_gp, 1)
                    if not first:
                        pe.wait_ge(s_res, t - 1)
                    for k in range(CH):
                        nc.tensor.matmul(p_o[b][0:P, 0:C], xt[:, b, k * P:(k + 1) * P], fcw[:, k, :], start=k == 0, stop=False)
                    pe.wait_ge(s_y, t + 1)
                    for k in range(H2):
                        nc.tensor.matmul(p_o[b][0:P, 0:C], z[:, b, k * P:(k + 1) * P], fcw[:, CH + k, :], start=False, stop=False)
                    pe.wait_ge(s_gt, t + 1)
                    for k in range(CH):
                        last = nc.tensor.matmul(p_o[b][0:P, 0:C], gt[:, b, k * P:(k + 1) * P], w2[:, k, :], start=False, stop=k == CH - 1)
                    last.then_inc(s_o, 1)
            loop2(pe, None, NT // 2, 0, step)


def phase_route(nc, phase, a, d, ident, x_sb, st, pos, gate, blk, pairs, w1, b1, w2_lo):
    X = EXPERTS
    T8 = NT * X
    BUFS = 5
    with phase("r") as (c, sb, ps, sm):
        wr = sb("wr", [128, CH, X])
        br = sb("br", [P, X])
        half = sb("half", [P, NT])
        mv = sb("mv", [P, NT, 2])
        mv2 = sb("mv2", [P, NT, 2])
        r1 = sb("r1", [P, NT])
        r2 = sb("r2", [P, NT])
        xt = sb("xt", [128, 2, CH * P])
        lg = sb("lg", [P, NT, X])
        lane_i = sb("lane_i", [P, X], I32)
        e_id = sb("e_id", [P, X])
        red = sb("red", [P, NT])
        tsum = sb("tsum", [P, NT])
        top1 = sb("top1", [P, NT])
        top2 = sb("top2", [P, NT])
        m1 = sb("m1", [P, NT, X])
        pick = sb("pick", [P, 2, NT, X])
        both = sb("both", [P, X, NT])
        ones = sb("ones", [P, T8])
        run = sb("run", [P, X, NT])
        lane = sb("lane", [P, X])
        lower = sb("lower", [P, P])
        fill = sb("fill", [P, X])
        fill_i = sb("fill_i", [P, X], I32)
        end = sb("end", [P, X])
        off = sb("off", [P, X])
        blk_i = sb("blk_i", [1, BLOCKS], I32)
        blk_f = sb("blk_f", [1, BLOCKS])
        blk_g = sb("blk_g", [1, BLOCKS, X])
        xe = sb("xe", [P, 2, C])
        xs = sb("xs", [P, BUFS, C])
        ln = sb("ln", [2 * X, 2, 128])
        lnt = sb("lnt", [128, 2, 2 * X])
        shift = sb("shift", [128, CH * X, 128])
        pick_row = sb("pick_row", [X, X, 128])
        b1_in = sb("b1_in", [X, HID])
        p_ln = ps("p_ln")
        p_w = [ps(f"p_w{q}") for q in range(2)]
        p_t = [ps(f"p_t{b}") for b in range(2)]
        p_l = [ps(f"p_l{b}") for b in range(2)]
        p_c = ps("p_c")
        (s_c, s_gp, s_dve, s_var, s_std, s_xo, s_tp, s_xt, s_lp, s_lg, s_var2, s_std2, s_ex, s_exd, s_lane,
         s_cnt, s_pos, s_xe, s_keep, s_ln, s_w1, s_w2, s_lt) = (sm(n) for n in
            ("c", "gp", "dve", "var", "std", "xo", "tp", "xt", "lp", "lg", "var2", "std2", "ex", "exd", "lane",
             "cnt", "pos", "xe", "keep", "ln", "w1", "w2", "lt"))
        s_ltc, s_sh, s_wp, s_wc = (sm(n) for n in ("ltc", "sh", "wp", "wc"))
        s_stat = sm("stat")
        s_sc = [sm(f"sc{b}", swdge=True) for b in range(BUFS)]
        block = c.enter_context(nc.Block())

        @block.sync
        def _(sp):
            sp.dma_start(wr[:, :, :], a["L0_ffn_Wr"].rearrange("(k p) n -> p k n", p=128)).then_inc(s_c, 16)
            sp.dma_start(br[:, :], a["L0_ffn_br"].rearrange("(o n) -> o n", o=1).to_broadcast([P, X])).then_inc(s_c, 16)
            for j, n in enumerate(("g", "b")):
                sp.dma_start(ln[:, j, :], a[f"L0_ffn_ln_{n}"].rearrange("e (k p) -> (e k) p", p=128)).then_inc(s_ln, 16)
            sp.dma_start(b1_in[:, :], a["L0_ffn_b1"]).then_inc(s_ln, 16)
            for k in range(CH):
                sp.dma_start(w1[:, k, :].rearrange("p (e h) -> p e h", e=X),
                             a["L0_ffn_W1"][:, k * 128:(k + 1) * 128, :].rearrange("e p h -> p e h")).then_inc(s_w1, 16)
            for k in range(W2_LO):
                sp.wait_ge(s_xe, (k + 1) * X)
                sp.dma_start(w2_lo[:, k, :].rearrange("p (e c) -> p e c", e=X),
                             a["L0_ffn_W2"][:, k * 128:(k + 1) * 128, :].rearrange("e p c -> p e c")).then_inc(s_w2, 16)
            sp.wait_ge(s_w2, 16 * W2_LO)

        @block.gpsimd
        def _(pool):
            g = nc.gpsimd
            g.iota(lane_i[:, :], pattern=[[1, X]], base=0, channel_multiplier=0).then_inc(s_gp, 1)
            g.iota(blk_i[:, :], pattern=[[128, BLOCKS]], base=0, channel_multiplier=0).then_inc(s_gp, 1)
            g.memset(lower[:, :], 1.0).then_inc(s_gp, 1)
            pool.wait_ge(s_gp, 3)
            g.affine_select(out=lower[:, :], in_=lower[:, :], compare_op=ALU.is_gt, fill=0.0, base=0,
                            pattern=[[1, P]], channel_multiplier=-1).then_inc(s_gp, 1)

            def keep_tile(i, first):
                for b in range(2):
                    t = 2 * i + b
                    pool.wait_ge(s_xo, t + 1)
                    g.tensor_copy(x_sb[:, bass.ds(t, 1), :].rearrange("p o c -> p (o c)"), xe[:, b, :]).then_inc(s_keep, 1)
            loop2(pool, None, NT // 2, 0, keep_tile)
            pool.wait_ge(s_pos, 1)

            for t in range(NT):
                pool.wait_ge(s_xe, t + 1)
                for j in range(2):
                    g.indirect_dma_start(out=d["xg"][:, :], out_offset=bass.IndirectOffsetOnAxis(ap=pos[:, j, t:t + 1], axis=0),
                                         in_=xs[:, t % BUFS, :], in_offset=None).then_inc(s_sc[t % BUFS], 16)
            for b in range(BUFS):
                pool.wait_ge(s_sc[b], 32 * (NT // BUFS))

        @block.scalar
        def _(act):
            act.wait_ge(s_var, 1)
            nc.scalar.activation(r1[:, :], r1[:, :], ACT.Sqrt).then_inc(s_std, 1)

            def step(i, first):
                for b in range(2):
                    t = 2 * i + b
                    act.wait_ge(s_tp, t + 1)
                    if not first:
                        act.wait_ge(s_lp, t - 1)
                    nc.scalar.activation(xt[:, b, :], p_t[b][:, 0:CH * P], ACT.Copy).then_inc(s_xt, 1)
            loop2(act, None, NT // 2, 0, step)
            act.wait_ge(s_var2, 1)
            nc.scalar.activation(r2[:, :], r2[:, :], ACT.Sqrt).then_inc(s_std2, 1)
            act.wait_ge(s_ex, 1)
            nc.scalar.activation(lg[:, :, :], lg[:, :, :], ACT.Exp).then_inc(s_exd, 1)
            act.wait_ge(s_lt, 1)
            nc.scalar.activation(lnt[:, :, :], p_ln[:, 0:4 * X].rearrange("p (j r) -> p j r", j=2), ACT.Copy).then_inc(s_ltc, 1)
            act.wait_ge(s_ltc, 1)
            for r in range(CH * X):
                nc.scalar.activation(shift[:, r, :], lnt[:, 1, r:r + 1].to_broadcast([128, 128]), ACT.Copy)
            for e in range(X):
                last = nc.scalar.activation(pick_row[:, e, :], ident[0:X, e:e + 1].to_broadcast([X, 128]), ACT.Copy)
            last.then_inc(s_sh, 1)
            for e in range(X):
                for q in range(2):
                    act.wait_ge(s_wp, 2 * e + q + 1)
                    nc.scalar.activation(b1[:, e * HID + q * 512:e * HID + (q + 1) * 512], p_w[q][:, :], ACT.Copy).then_inc(s_wc, 1)
                for k in range(CH):
                    sl = slice(e * HID, (e + 1) * HID)
                    nc.scalar.activation(w1[:, k, sl], w1[:, k, sl], ACT.Copy, scale=lnt[:, 0, CH * e + k:CH * e + k + 1])

        @block.tensor
        def _(pe):
            pe.wait_ge(s_c, 32)

            def transposes(t, b, first):
                pe.wait_ge(s_xo, t + 1)
                if not first:
                    pe.wait_ge(s_xt, t - 1)
                for k in range(CH):
                    last = nc.tensor.transpose(p_t[b][:, k * P:(k + 1) * P],
                                               xe[:, b, k * 128:(k + 1) * 128], ident[0:P, 0:P])
                last.then_inc(s_tp, 1)

            transposes(0, 0, True)

            def step(i, has):
                for b in range(2):
                    t = 2 * i + b
                    if has(b, 1):
                        transposes(t + 1, 1 - b, not has(b, -1))
                    pe.wait_ge(s_xt, t + 1)
                    if has(b, -2):
                        pe.wait_ge(s_lg, t - 1)
                    for k in range(CH):
                        last = nc.tensor.matmul(p_l[b][0:P, 0:X], xt[:, b, k * P:(k + 1) * P], wr[:, k, :], start=k == 0, stop=k == CH - 1)
                    last.then_inc(s_lp, 1)
            pipelined(pe, None, NT // 2, 1, 1, 0, step)

            def bias_rows(e):
                for q in range(2):
                    if e > 0:
                        pe.wait_ge(s_wc, 2 * (e - 1) + q + 1)
                    cols = slice(q * 512, (q + 1) * 512)
                    for k in range(CH):
                        nc.tensor.matmul(p_w[q][:, :], shift[:, CH * e + k, :], w1[:, k, e * HID + q * 512:e * HID + (q + 1) * 512],
                                         start=k == 0, stop=False)
                    nc.tensor.matmul(p_w[q][:, :], pick_row[:, e, :], b1_in[:, cols], start=False, stop=True).then_inc(s_wp, 1)

            pe.wait_ge(s_ln, 48)
            for j in range(2):
                last = nc.tensor.transpose(p_ln[:, j * 2 * X:(j + 1) * 2 * X], ln[:, j, :], ident[0:2 * X, 0:2 * X])
            last.then_inc(s_lt, 1)
            pe.wait_ge(s_lane, 1)
            pe.wait_ge(s_gp, 4)
            nc.tensor.matmul(p_c[0:P, 0:X], lower[:, :], lane[:, :], start=True, stop=True)
            nc.tensor.matmul(p_c[0:P, 8:8 + X], ones[:, 0:P], lane[:, :], start=True, stop=True).then_inc(s_cnt, 1)
            pe.wait_ge(s_sh, 1)
            pe.wait_ge(s_w1, 16 * CH)
            for e in range(X):
                bias_rows(e)

        @block.vector
        def _(dve):
            ch = Chain(dve, s_dve)
            v = nc.vector
            v.memset(ones[:, :], 1.0)
            halves_to_mean_var(nc, ch, st, mv, half)
            v.tensor_scalar_add(r1[:, :], mv[:, :, 1], EPS).then_inc(s_var, 1)
            dve.wait_ge(s_std, 1)
            ch.link(v.reciprocal(r1[:, :], r1[:, :]))
            dve.wait_ge(s_c, 32)

            def cols(t3, t):
                return t3[:, bass.ds(t, 1), :].rearrange("p o c -> p (o c)")

            def normalise(t, b, first):
                if not first:
                    dve.wait_ge(s_tp, t - 1)
                    dve.wait_ge(s_keep, t - 1)
                v.tensor_scalar(xe[:, b, :], cols(x_sb, t), mv[:, bass.ds(t, 1), 0], r1[:, bass.ds(t, 1)], ALU.subtract, ALU.mult).then_inc(s_xo, 1)
                dve.wait_ge(s_xo, t + 1)
                v.bn_stats(cols(st, t), xe[:, b, :]).then_inc(s_stat, 1)

            normalise(0, 0, True)
            normalise(1, 1, True)

            def step(i, has):
                for b in range(2):
                    t = 2 * i + b
                    if has(b, 2):
                        dve.wait_ge(s_stat, t + 1)
                        normalise(t + 2, b, False)
                    dve.wait_ge(s_lp, t + 1)
                    v.tensor_tensor(cols(lg, t), p_l[b][0:P, 0:X], br[:, :], ALU.add).then_inc(s_lg, 1)
            pipelined(dve, None, NT // 2, 1, 1, 0, step)
            dve.drain()
            halves_to_mean_var(nc, ch, st, mv2, half)
            v.tensor_scalar_add(r2[:, :], mv2[:, :, 1], EPS).then_inc(s_var2, 1)
            dve.wait_ge(s_std2, 1)
            v.reciprocal(r2[:, :], r2[:, :])

            def by_token(t2):
                return t2.unsqueeze(2).to_broadcast([P, NT, X])

            ch.link(v.reduce_max(red[:, :], lg[:, :, :], axis=AX))
            v.tensor_tensor(lg[:, :, :], lg[:, :, :], by_token(red[:, :]), ALU.subtract).then_inc(s_ex, 1)
            dve.wait_ge(s_gp, 4)
            v.tensor_copy(e_id[:, :], lane_i[:, :])
            ch.link(v.tensor_copy(blk_f[:, :], blk_i[:, :]))
            dve.wait_ge(s_exd, 1)
            ch.link(v.reduce_sum(tsum[:, :], lg[:, :, :], axis=AX))
            ch.link(v.reciprocal(tsum[:, :], tsum[:, :]))
            ch.link(v.tensor_tensor(lg[:, :, :], lg[:, :, :], by_token(tsum[:, :]), ALU.mult))
            ids = e_id[:, :].unsqueeze(1).to_broadcast([P, NT, X])
            for k, top in enumerate((top1, top2)):
                ch.link(v.reduce_max(top[:, :], lg[:, :, :], axis=AX))
                ch.link(v.tensor_tensor(m1[:, :, :], lg[:, :, :], by_token(top[:, :]), ALU.not_equal))
                ch.link(v.scalar_tensor_tensor(m1[:, :, :], m1[:, :, :], 2.0 * X, ids, ALU.mult, ALU.add))
                ch.link(v.tensor_reduce(red[:, :], m1[:, :, :], axis=AX, op=ALU.min))
                ch.link(v.tensor_tensor(pick[:, k], ids, by_token(red[:, :]), ALU.is_equal))
                if k == 0:
                    ch.link(v.scalar_tensor_tensor(lg[:, :, :], pick[:, k], -2.0, lg[:, :, :], ALU.mult, ALU.add))
            ch.link(v.tensor_tensor(tsum[:, :], top1[:, :], top2[:, :], ALU.add))
            ch.link(v.reciprocal(tsum[:, :], tsum[:, :]))
            v.tensor_tensor(gate[:, 0, :], top1[:, :], tsum[:, :], ALU.mult)
            v.tensor_tensor(gate[:, 1, :], top2[:, :], tsum[:, :], ALU.mult)
            ch.link(v.tensor_tensor(both[:, :, :].rearrange("p e t -> p t e"), pick[:, 0], pick[:, 1], ALU.add))
            ch.link(v.tensor_tensor_scan(run[:, :, :].rearrange("p e t -> p (e t)"), ones[:, :],
                                         both[:, :, :].rearrange("p e t -> p (e t)"), 0.0, ALU.mult, ALU.add))
            v.tensor_copy(off[:, 0:1], run[:, 0:1, NT - 1])
            ch.link(v.tensor_copy(lane[:, 0:1], run[:, 0:1, NT - 1]))
            v.tensor_tensor(lane[:, 1:X], run[:, 1:X, NT - 1], run[:, 0:X - 1, NT - 1], ALU.subtract).then_inc(s_lane, 1)
            dve.wait_ge(s_cnt, 1)
            ch.link(v.tensor_scalar(fill[:, :], p_c[0:P, 8:8 + X], 127.0, None, ALU.add))
            ch.link(v.tensor_copy(fill_i[:, :], fill[:, :]))
            ch.link(v.tensor_single_scalar(fill_i[:, :], fill_i[:, :], 7, op=ALU.logical_shift_right))
            ch.link(v.tensor_copy(fill[:, :], fill_i[:, :]))
            ch.link(v.tensor_scalar(fill[:, :], fill[:, :], 128.0, None, ALU.mult))
            ch.link(v.tensor_tensor_scan(end[:, :], ones[:, 0:X], fill[:, :], 0.0, ALU.mult, ALU.add))
            ch.link(v.tensor_tensor(off[:, :], end[:, :], fill[:, :], ALU.subtract))
            ch.link(v.tensor_tensor(off[:, :], off[:, :], p_c[0:P, 0:X], ALU.add))
            ch.link(v.tensor_tensor(off[:, 1:X], off[:, 1:X], run[:, 0:X - 1, NT - 1], ALU.subtract))
            ch.link(v.tensor_tensor(run[:, :, :], run[:, :, :], both[:, :, :], ALU.subtract))
            ch.link(v.tensor_tensor(run[:, :, :], run[:, :, :], off[:, :].unsqueeze(2).to_broadcast([P, X, NT]), ALU.add))
            for k in range(2):
                ch.link(v.tensor_tensor(m1[:, :, :], pick[:, k], run[:, :, :].rearrange("p e t -> p t e"), ALU.mult))
                ch.link(v.reduce_sum(red[:, :], m1[:, :, :], axis=AX))
                last = v.tensor_copy(pos[:, k, :], red[:, :])
                ch.link(last)
            v.memset(half[:, 0:1], 0.0).then_inc(s_pos, 1)
            ch.link(v.tensor_tensor(blk_g[:, :, :], blk_f[:, :].unsqueeze(2).to_broadcast([1, BLOCKS, X]),
                                    end[0:1, :].unsqueeze(1).to_broadcast([1, BLOCKS, X]), ALU.is_ge))
            ch.link(v.reduce_sum(blk_f[:, :], blk_g[:, :, :], axis=AX))
            ch.link(v.tensor_scalar(blk_f[:, :], blk_f[:, :], float(X - 1), None, ALU.min))
            ch.link(v.tensor_copy(blk[:, :], blk_f[:, :]))
            ch.link(v.tensor_scalar(fill[0:1, 0:1], end[0:1, X - 1:X], -1.0, None, ALU.add))
            ch.link(v.tensor_copy(pairs[:, :], fill[0:1, 0:1]))
            ch.link(v.tensor_single_scalar(pairs[:, :], pairs[:, :], 8, op=ALU.logical_shift_right))

            dve.wait_ge(s_keep, NT)

            def norm(i, first):
                for b in range(BUFS):
                    t = BUFS * i + b
                    if not first:
                        dve.wait_ge(s_sc[b], 32 * i)
                    v.tensor_scalar(xs[:, b, :], cols(x_sb, t), mv2[:, bass.ds(t, 1), 0], r2[:, bass.ds(t, 1)],
                                    ALU.subtract, ALU.mult).then_inc(s_xe, 1)
            loop2(dve, None, NT // BUFS, 0, norm)


def phase_experts(nc, phase, a, d, ident, blk, pairs, w1, b1, w2_lo):
    X = EXPERTS
    with phase("f") as (c, sb, ps, sm):
        w2_hi = sb("w2_hi", [128, KH - W2_LO, X * C])
        b2 = sb("b2", [128, X * C])
        xin = sb("xin", [128, 2, C])
        xt = sb("xt", [128, 2, C])
        hs = sb("hs", [128, 2, HID])
        ht = sb("ht", [128, HID])
        ys = sb("ys", [128, 2, C])
        p_x = ps("p_x")
        p_y = ps("p_y")
        p_h = [[ps(f"p_h{b}{q}") for q in range(2)] for b in range(2)]
        p_t = [ps(f"p_t{q}") for q in range(2)]
        s_w2, s_b, s_xtp, s_xt, s_h, s_hb, s_ge, s_tp, s_ta, s_tv, s_y, s_ys = (sm(n) for n in
            ("w2", "b", "xtp", "xt", "h", "hb", "ge", "tp", "ta", "tv", "y", "ys"))
        s_x = [sm(f"x{b}") for b in range(2)]
        s_st = [sm(f"st{b}", swdge=True) for b in range(2)]
        block = c.enter_context(nc.Block())
        xg = d["xg"].rearrange("(t p) c -> p t c", p=128)
        yg = d["yg"].rearrange("(t p) c -> p t c", p=128)

        def expert(eng, t):
            return eng.value_load(blk[0:1, bass.ds(t, 1)], min_val=0, max_val=X - 1)

        def last_pair(eng):
            return eng.value_load(pairs[0:1, 0:1], min_val=1, max_val=BLOCKS // 2 - 1)

        @block.sync
        def _(sp):
            m = last_pair(sp)

            def load(t, b):
                sp.dma_start(xin[:, b, :], xg[:, bass.ds(t, 1), :].rearrange("p o c -> p (o c)")).then_inc(s_x[b], 16)

            def step(i, first):
                for b in range(2):
                    t = 2 * i + b
                    if not first:
                        sp.wait_ge(s_xtp, t - 1)
                    load(t, b)
            step(0, True)
            for k in range(W2_LO, KH):
                sp.dma_start(w2_hi[:, k - W2_LO, :].rearrange("p (e c) -> p e c", e=X),
                             a["L0_ffn_W2"][:, k * 128:(k + 1) * 128, :].rearrange("e p c -> p e c")).then_inc(s_w2, 16)
            sp.dma_start(b2[:, :], a["L0_ffn_b2"].rearrange("(o e) h -> o (e h)", o=1).to_broadcast([128, X * C])).then_inc(s_b, 16)
            with sp.Fori(1, m + 1) as i:
                step(i, False)
            sp.wait_ge(s_xtp, 2 * m + 1)
            load(2 * m + 2, 0)

        @block.gpsimd
        def _(pool):
            def step(i, first):
                for b in range(2):
                    t = 2 * i + b
                    pool.wait_ge(s_ys, t + 1)
                    pool.dma_start(yg[:, bass.ds(t, 1), :].rearrange("p o c -> p (o c)"), ys[:, b, :]).then_inc(s_st[b], 16)
            m = last_pair(pool)
            loop2(pool, None, m + 1, 0, step)
            for b in range(2):
                pool.wait_ge(s_st[b], 16 * m + 16)

        @block.tensor
        def _(pe):
            def x_transposed(i, b):
                pe.wait_ge(s_x[b], 16 * (i + 1))
                for k in range(CH):
                    last = nc.tensor.transpose(p_x[:, k * 128:(k + 1) * 128], xin[:, b, k * 128:(k + 1) * 128], ident[:, :])
                last.then_inc(s_xtp, 1)

            def hidden(t, b, e, first):
                if not first:
                    pe.wait_ge(s_hb, t - 1)
                pe.wait_ge(s_xt, t + 1)
                for q in range(2):
                    for k in range(CH):
                        last = nc.tensor.matmul(p_h[b][q][:, :], xt[:, b, k * 128:(k + 1) * 128],
                                                w1[:, k, bass.ds(e * HID + q * 512, 512)], start=k == 0, stop=k == CH - 1)
                    last.then_inc(s_h, 1)

            def h_transposed(t, b, first):
                pe.wait_ge(s_ge, t + 1)
                if not first:
                    pe.wait_ge(s_ta, t)
                    pe.wait_ge(s_tv, t)
                for k in range(KH):
                    last = nc.tensor.transpose(p_t[k // 4][:, (k % 4) * 128:(k % 4 + 1) * 128],
                                               hs[:, b, k * 128:(k + 1) * 128], ident[:, :])
                last.then_inc(s_tp, 1)

            def down(t, b, e, first):
                pe.wait_ge(s_ta, t + 1)
                pe.wait_ge(s_tv, t + 1)
                if not first:
                    pe.wait_ge(s_ys, t)
                for k in range(KH):
                    last = nc.tensor.matmul(p_y[:, 0:C], ht[:, k * 128:(k + 1) * 128],
                                            (w2_lo[:, k] if k < W2_LO else w2_hi[:, k - W2_LO])[:, bass.ds(e * C, C)],
                                            start=k == 0, stop=k == KH - 1)
                last.then_inc(s_y, 1)

            x_transposed(0, 0)

            def step(i, first):
                e = [None if first and k == 0 else expert(pe, 2 * i + (k - 1)) for k in range(3)]
                for b in range(2):
                    t = 2 * i + b
                    if not (first and b == 0):
                        h_transposed(t - 1, 1 - b, first)
                    hidden(t, b, e[b + 1], first)
                    x_transposed(i + b, 1 - b)
                    if not (first and b == 0):
                        down(t - 1, 1 - b, e[b], first)
            pe.wait_ge(s_w2, 16 * (KH - W2_LO))
            m = last_pair(pe)
            loop2(pe, None, m + 1, 0, step)
            h_transposed(2 * m + 1, 1, False)
            down(2 * m + 1, 1, expert(pe, 2 * m + 1), False)

        @block.scalar
        def _(act):
            def x_copy(t, b):
                act.wait_ge(s_xtp, t + 1)
                nc.scalar.activation(xt[:, b, :], p_x[:, 0:C], ACT.Copy).then_inc(s_xt, 1)

            def h_copy(t):
                act.wait_ge(s_tp, t + 1)
                nc.scalar.activation(ht[:, 0:512], p_t[0][:, :], ACT.Copy).then_inc(s_ta, 1)

            x_copy(0, 0)

            def step(i, first):
                for b in range(2):
                    t = 2 * i + b
                    if not (first and b == 0):
                        if not (first and b == 1):
                            act.wait_ge(s_y, t - 1)
                        h_copy(t - 1)
                    x_copy(t + 1, 1 - b)
                    act.wait_ge(s_hb, t + 1)
                    nc.scalar.activation(hs[:, b, :], hs[:, b, :], ACT.Gelu).then_inc(s_ge, 1)
            m = last_pair(act)
            loop2(act, None, m + 1, 0, step)
            act.wait_ge(s_y, 2 * m + 1)
            h_copy(2 * m + 1)

        @block.vector
        def _(dve):
            v = nc.vector
            dve.wait_ge(s_b, 16)

            def h_copy(t, first):
                dve.wait_ge(s_tp, t + 1)
                if not first:
                    dve.wait_ge(s_y, t)
                v.tensor_copy(ht[:, 512:], p_t[1][:, :]).then_inc(s_tv, 1)

            def result(t, b, i, first):
                e = expert(dve, t)
                dve.wait_ge(s_y, t + 1)
                if not first:
                    dve.wait_ge(s_st[b], 16 * i)
                v.tensor_tensor(ys[:, b, :], p_y[:, 0:C], b2[:, bass.ds(e * C, C)], ALU.add).then_inc(s_ys, 1)

            def step(i, first):
                for b in range(2):
                    t = 2 * i + b
                    if not (first and b == 0):
                        h_copy(t - 1, first)
                    e = expert(dve, t)
                    if not first:
                        dve.wait_ge(s_tp, t - 1)
                    for q in range(2):
                        dve.wait_ge(s_h, 2 * t + (q + 1))
                        last = v.tensor_tensor(hs[:, b, q * 512:(q + 1) * 512], p_h[b][q][:, :],
                                               b1[:, bass.ds(e * HID + q * 512, 512)], ALU.add)
                    last.then_inc(s_hb, 1)
                    if not (first and b == 0):
                        result(t - 1, 1 - b, i + b - 1 if not first else 0, first)
            m = last_pair(dve)
            loop2(dve, None, m + 1, 0, step)
            h_copy(2 * m + 1, False)
            result(2 * m + 1, 1, m, False)


def phase_combine(nc, phase, d, out, pos, gate):
    PT = 10
    PIECES = NT // PT
    BUFS = 5
    with phase("o") as (c, sb, ps, sm):
        x2 = sb("x2", [P, NT, C])
        y = sb("y", [P, BUFS, 2, C])
        s_one, s_out, s_done = (sm(n) for n in ("one", "out", "done"))
        s_x = [sm(f"x{j}") for j in range(PIECES)]
        s_y = [sm(f"y{b}", swdge=True) for b in range(BUFS)]
        block = c.enter_context(nc.Block())

        @block.sync
        def _(sp):
            for j in range(PIECES):
                tiles = slice(j * PT, (j + 1) * PT)
                sp.dma_start(x2[:, tiles, :], d["x2"].rearrange("(p t) c -> p t c", t=NT)[:, tiles, :]).then_inc(s_x[j], 16)
            for j in range(PIECES):
                tiles = slice(j * PT, (j + 1) * PT)
                sp.wait_ge(s_out, (j + 1) * PT)
                sp.dma_start(out.rearrange("(p t) c -> p t c", t=NT)[:, tiles, :], x2[:, tiles, :]).then_inc(s_done, 16)
            sp.wait_ge(s_done, 16 * PIECES)

        @block.gpsimd
        def _(pool):
            for t in range(NT):
                if t >= BUFS:
                    pool.wait_ge(s_out, t - BUFS + 1)
                for j in range(2):
                    nc.gpsimd.indirect_dma_start(out=y[:, t % BUFS, j, :], out_offset=None, in_=d["yg"][:, :],
                                                 in_offset=bass.IndirectOffsetOnAxis(ap=pos[:, j, t:t + 1], axis=0)).then_inc(s_y[t % BUFS], 16)

        @block.vector
        def _(dve):
            def step(i):
                for b in range(BUFS):
                    t = BUFS * i + b
                    row = x2[:, bass.ds(t, 1), :].rearrange("p o c -> p (o c)")
                    dve.wait_ge(s_y[b], 32 * (i + 1))
                    nc.vector.scalar_tensor_tensor(row, y[:, b, 0, :], gate[:, 0, bass.ds(t, 1)], row, ALU.mult, ALU.add).then_inc(s_one, 1)
                    dve.wait_ge(s_one, t + 1)
                    nc.vector.scalar_tensor_tensor(row, y[:, b, 1, :], gate[:, 1, bass.ds(t, 1)], row, ALU.mult, ALU.add).then_inc(s_out, 1)
            for j in range(PIECES):
                dve.wait_ge(s_x[j], 16)
                with dve.Fori(j * PT // BUFS, (j + 1) * PT // BUFS) as i:
                    step(i)


_INS = ['x', 'src', 'dst', 'L0_gnn_Wb', 'L0_gnn_Wc', 'L0_gnn_bc', 'L0_gnn_conv_bias', 'L0_gnn_bn_gamma',
        'L0_gnn_bn_beta', 'L0_gnn_fc_W', 'L0_gnn_fc_b', 'L0_mix_w_qkv', 'L0_mix_b_qkv', 'L0_mix_kln_g',
        'L0_mix_kln_b', 'L0_mix_vln_g', 'L0_mix_vln_b', 'L0_mix_w1', 'L0_mix_b1', 'L0_mix_w2', 'L0_mix_b2',
        'L0_ffn_Wr', 'L0_ffn_br', 'L0_ffn_ln_g', 'L0_ffn_ln_b', 'L0_ffn_W1', 'L0_ffn_b1', 'L0_ffn_W2',
        'L0_ffn_b2']


def kernel(**inputs):
    import numpy as _np
    import concourse.bacc as _bacc
    from concourse import mybir as _mybir
    from concourse.bass_utils import run_bass_kernel_spmd as _run

    nc = _bacc.Bacc("TRN2", target_bir_lowering=False, num_devices=1)
    arrays, args = {}, {}
    for name in _INS:
        array = _np.ascontiguousarray(inputs[name])
        arrays[f"in_{name}"] = array
        args[name] = nc.dram_tensor(f"in_{name}", array.shape, _mybir.dt.from_np(array.dtype), kind="ExternalInput").ap()
    out = nc.dram_tensor("out_0", (N, C), _mybir.dt.float32, kind="ExternalOutput").ap()
    build(nc, args, out)
    result = _run(nc, [arrays], core_ids=[0])
    return result.results[0]["out_0"]
```
